# Optimizing a Trainium2 kernel written in Bass

```python
import numpy as np
import jax
import jax.numpy as jnp

def _softmax(x, axis=-1):
    return jax.nn.softmax(x, axis=axis)

def _gelu(x):
    return jax.nn.gelu(x, approximate=True)

def _silu(x):
    return jax.nn.silu(x)

def _sigmoid(x):
    return jax.nn.sigmoid(x)

def _layernorm(x, axis=-1, eps=1e-05):
    m = jnp.mean(x, axis=axis, keepdims=True)
    v = jnp.var(x, axis=axis, keepdims=True)
    return (x - m) / jnp.sqrt(v + eps)

def _scatter_add(tgt, idx, src, axis=0):
    return tgt.at[idx].add(src)

def _segment_sum(src, seg, n):
    return jax.ops.segment_sum(src, seg, n)
kernel_name = 'mk_flamingo_gated_d2_seqx_r4_eaba76'

def setup_inputs(seed: int=0):
    np.random.seed(seed)
    _w = jnp.asarray

    def _rec_inputs():
        import jax
        import jax.numpy as jnp
        _rk = jax.random.key(seed)
        x = -0.000929 + 1 * jax.random.normal(jax.random.fold_in(_rk, 1), (8, 256, 256), jnp.float32)
        _lenS = 256 - jax.random.randint(jax.random.fold_in(_rk, 7), (8,), 0, max(1, 256 // 4) + 1, jnp.int32)
        _lenS2 = 256 - jax.random.randint(jax.random.fold_in(_rk, 8), (8,), 0, max(1, 256 // 4) + 1, jnp.int32)
        _ctx_1024P = jax.random.normal(jax.random.fold_in(_rk, 11), (8, 16, 256), jnp.float32)
        _ctx_1024c = jax.random.dirichlet(jax.random.fold_in(_rk, 511), 0.3 * jnp.ones((16,), jnp.float32), (8, 256))
        _ctx_1024t = jnp.einsum('bsk,bkd->bsd', _ctx_1024c, _ctx_1024P)
        _ctx_1024t = _ctx_1024t * jax.lax.rsqrt(jnp.mean(jnp.square(_ctx_1024t)) + 1e-12) * 0.953939
        ctx_1024 = -1.52775e-05 + 0.999936 * (_ctx_1024t + 0.3 * jax.random.normal(jax.random.fold_in(_rk, 611), (8, 256, 256), jnp.float32))
        _g = jax.random.normal(jax.random.fold_in(_rk, 9001), (2, 2), jnp.float32)
        _g = jnp.sign(_g) * jnp.maximum(jnp.abs(_g), 1.0) + (_g == 0) * 1.0
        g_xattn = _g[0]
        g_ffn = _g[1]
        return (x, ctx_1024, g_xattn, g_ffn)
    x, ctx_1024, g_xattn, g_ffn = _rec_inputs()

    def _L0_xattn_setup():
        import jax, jax.numpy as jnp
        import numpy as np
        DIM = 256
        H = 16
        D = 64
        INNER = H * D
        EPS = 1e-05

        def layernorm(x, w, b):
            mu = jnp.mean(x, axis=-1, keepdims=True)
            var = jnp.var(x, axis=-1, keepdims=True)
            return (x - mu) * jax.lax.rsqrt(var + EPS) * w + b
        key = jax.random.key(seed)
        ks = jax.random.split(key, 8)
        B, N, S = (4, 64, 2048)
        s = 1.0 / np.sqrt(DIM)
        return {'latents': jax.random.normal(ks[0], (B, N, DIM), jnp.float32), 'context': jax.random.normal(ks[1], (B, S, DIM), jnp.float32), 'ln_l_w': jnp.ones((DIM,), jnp.float32), 'ln_l_b': jnp.zeros((DIM,), jnp.float32), 'ln_c_w': jnp.ones((DIM,), jnp.float32), 'ln_c_b': jnp.zeros((DIM,), jnp.float32), 'Wq': jax.random.normal(ks[2], (DIM, INNER), jnp.float32) * s, 'Wkv': jax.random.normal(ks[3], (DIM, 2 * INNER), jnp.float32) * s, 'Wo': jax.random.normal(ks[4], (INNER, DIM), jnp.float32) * (1.0 / np.sqrt(INNER)), 'bo': jnp.zeros((DIM,), jnp.float32)}
    _L0_xattn_all = _L0_xattn_setup()
    _L0_xattn_in = {k: v for k, v in _L0_xattn_all.items() if k in ('ln_l_w', 'ln_l_b', 'ln_c_w', 'ln_c_b', 'Wq', 'Wkv', 'Wo', 'bo')}
    del _L0_xattn_all

    def _L0_ffn_setup():
        import jax, jax.numpy as jnp
        import numpy as np
        DIM = 256
        INTER = 256
        E = 32
        K = 4
        G = 8
        LG = 4
        ROUTE_SCALE = 1.0
        CAP_FACTOR = 1.25
        B, S = (4, 512)

        def _gate(xf, wg):
            logits = xf @ wg.T
            scores = jax.nn.softmax(logits, axis=-1)
            sg = scores.reshape(-1, G, E // G)
            group_scores = sg.max(axis=-1)
            _, gtop = jax.lax.top_k(group_scores, LG)
            keep_g = jnp.sum(jax.nn.one_hot(gtop, G, dtype=jnp.float32), axis=1) > 0
            masked = jnp.where(keep_g[:, :, None], sg, -jnp.inf).reshape(-1, E)
            _, idx = jax.lax.top_k(masked, K)
            w = jnp.take_along_axis(scores, idx, axis=1)
            w = w / (w.sum(-1, keepdims=True) + 1e-09) * ROUTE_SCALE
            return (w.astype(xf.dtype), idx)

        def _forward(x, wg, w1, w2, w3, sw1, sw2, sw3):
            shape = x.shape
            xf = x.reshape(-1, DIM)
            N = xf.shape[0]
            cap = max(1, int(CAP_FACTOR * N * K / E))
            w, idx = _gate(xf, wg)
            fe = idx.reshape(-1)
            oh = jax.nn.one_hot(fe, E, dtype=jnp.int32)
            pos = (jnp.cumsum(oh, axis=0) * oh).sum(-1) - 1
            keep = pos < cap
            dest = jnp.where(keep, fe * cap + pos, E * cap)
            tok = jnp.arange(N * K, dtype=jnp.int32) // K
            buf_tok = jnp.full((E * cap + 1,), N, jnp.int32).at[dest].set(tok)[:-1]
            buf_w = jnp.zeros((E * cap + 1,), x.dtype).at[dest].set(w.reshape(-1))[:-1]
            xp = jnp.concatenate([xf, jnp.zeros((1, DIM), x.dtype)], axis=0)
            xe = xp[buf_tok].reshape(E, cap, DIM)
            h = jax.nn.silu(jnp.einsum('ecd,edh->ech', xe, w1)) * jnp.einsum('ecd,edh->ech', xe, w3)
            out = jnp.einsum('ech,ehd->ecd', h, w2) * buf_w.reshape(E, cap, 1)
            y = jnp.zeros((N + 1, DIM), x.dtype).at[buf_tok].add(out.reshape(E * cap, DIM))[:N]
            z = jax.nn.silu(xf @ sw1) * (xf @ sw3) @ sw2
            return (y + z).reshape(shape)
        key = jax.random.key(seed)
        ks = jax.random.split(key, 9)
        sd = DIM ** (-0.5)
        si = INTER ** (-0.5)
        x = jax.random.normal(ks[0], (B, S, DIM), jnp.float32)
        wg = jax.random.normal(ks[1], (E, DIM), jnp.float32) * sd
        w1 = jax.random.normal(ks[2], (E, DIM, INTER), jnp.float32) * sd
        w3 = jax.random.normal(ks[3], (E, DIM, INTER), jnp.float32) * sd
        w2 = jax.random.normal(ks[4], (E, INTER, DIM), jnp.float32) * si
        sw1 = jax.random.normal(ks[5], (DIM, INTER), jnp.float32) * sd
        sw3 = jax.random.normal(ks[6], (DIM, INTER), jnp.float32) * sd
        sw2 = jax.random.normal(ks[7], (INTER, DIM), jnp.float32) * si
        return dict(x=x, wg=wg, w1=w1, w2=w2, w3=w3, sw1=sw1, sw2=sw2, sw3=sw3)
    _L0_ffn_all = _L0_ffn_setup()
    _L0_ffn_in = {k: v for k, v in _L0_ffn_all.items() if k in ('wg', 'w1', 'w2', 'w3', 'sw1', 'sw2', 'sw3')}
    del _L0_ffn_all

    def _L1_xattn_setup():
        import jax, jax.numpy as jnp
        import numpy as np
        H = 16
        D = 256
        DK = D // H
        WIDTH = 64
        LEFT_TO_RIGHT = True
        B, S = (2, 512)
        SCALE = float(1.0 / np.sqrt(DK))

        def rel_bias(rel, seq_len):
            i = jnp.arange(seq_len)[:, None]
            j = jnp.arange(seq_len)[None, :]
            d = i - j if LEFT_TO_RIGHT else j - i
            valid = (d >= 0) & (d <= WIDTH)
            idx = jnp.where(valid, WIDTH - d if LEFT_TO_RIGHT else d, 0)
            return jnp.where(valid[None], rel[:, idx], 0.0)
        rng = jax.random.key(seed)
        ks = jax.random.split(rng, 12)
        f = lambda k, sh, s=1.0: jax.random.normal(k, sh, dtype=jnp.float32) * s
        return {'query': f(ks[0], (B, S, D)), 'key': f(ks[1], (B, S, D)), 'value': f(ks[2], (B, S, D)), 'Wq': f(ks[3], (D, D), 0.02), 'bq': jnp.zeros((D,), jnp.float32), 'Wk': f(ks[4], (D, D), 0.02), 'bk': jnp.zeros((D,), jnp.float32), 'Wv': f(ks[5], (D, D), 0.02), 'bv': jnp.zeros((D,), jnp.float32), 'Wo': f(ks[6], (D, D), 0.02), 'bo': jnp.zeros((D,), jnp.float32), 'rel': f(ks[7], (H, WIDTH + 1))}
    _L1_xattn_all = _L1_xattn_setup()
    _L1_xattn_in = {k: v for k, v in _L1_xattn_all.items() if k in ('Wq', 'bq', 'Wk', 'bk', 'Wv', 'bv', 'Wo', 'bo', 'rel')}
    del _L1_xattn_all

    def _L1_ffn_setup():
        import jax, jax.numpy as jnp
        import numpy as np
        key = jax.random.key(seed)
        kx, kw = jax.random.split(key)
        x = jax.random.normal(kx, (32, 1024, 256), dtype=jnp.float32)
        weight = jax.random.normal(kw, (256, 256), dtype=jnp.float32) * 0.01
        return {'x': x, 'weight': weight}
    _L1_ffn_all = _L1_ffn_setup()
    _L1_ffn_in = {k: v for k, v in _L1_ffn_all.items() if k in ('weight',)}
    del _L1_ffn_all
    return {'x': x, 'ctx_1024': ctx_1024, 'g_xattn': g_xattn, 'g_ffn': g_ffn, 'L0_xattn_ln_l_w': _L0_xattn_in['ln_l_w'], 'L0_xattn_ln_l_b': _L0_xattn_in['ln_l_b'], 'L0_xattn_ln_c_w': _L0_xattn_in['ln_c_w'], 'L0_xattn_ln_c_b': _L0_xattn_in['ln_c_b'], 'L0_xattn_Wq': _L0_xattn_in['Wq'], 'L0_xattn_Wkv': _L0_xattn_in['Wkv'], 'L0_xattn_Wo': _L0_xattn_in['Wo'], 'L0_xattn_bo': _L0_xattn_in['bo'], 'L0_ffn_wg': _L0_ffn_in['wg'], 'L0_ffn_w1': _L0_ffn_in['w1'], 'L0_ffn_w2': _L0_ffn_in['w2'], 'L0_ffn_w3': _L0_ffn_in['w3'], 'L0_ffn_sw1': _L0_ffn_in['sw1'], 'L0_ffn_sw2': _L0_ffn_in['sw2'], 'L0_ffn_sw3': _L0_ffn_in['sw3'], 'L1_xattn_Wq': _L1_xattn_in['Wq'], 'L1_xattn_bq': _L1_xattn_in['bq'], 'L1_xattn_Wk': _L1_xattn_in['Wk'], 'L1_xattn_bk': _L1_xattn_in['bk'], 'L1_xattn_Wv': _L1_xattn_in['Wv'], 'L1_xattn_bv': _L1_xattn_in['bv'], 'L1_xattn_Wo': _L1_xattn_in['Wo'], 'L1_xattn_bo': _L1_xattn_in['bo'], 'L1_xattn_rel': _L1_xattn_in['rel'], 'L1_ffn_weight': _L1_ffn_in['weight']}

def reference(x, ctx_1024, g_xattn, g_ffn, L0_xattn_ln_l_w, L0_xattn_ln_l_b, L0_xattn_ln_c_w, L0_xattn_ln_c_b, L0_xattn_Wq, L0_xattn_Wkv, L0_xattn_Wo, L0_xattn_bo, L0_ffn_wg, L0_ffn_w1, L0_ffn_w2, L0_ffn_w3, L0_ffn_sw1, L0_ffn_sw2, L0_ffn_sw3, L1_xattn_Wq, L1_xattn_bq, L1_xattn_Wk, L1_xattn_bk, L1_xattn_Wv, L1_xattn_bv, L1_xattn_Wo, L1_xattn_bo, L1_xattn_rel, L1_ffn_weight):
    import jax
    import jax.numpy as jnp

    def _L0_xattn_ref(latents, context, ln_l_w, ln_l_b, ln_c_w, ln_c_b, Wq, Wkv, Wo, bo):
        import jax, jax.numpy as jnp
        import numpy as np
        DIM = 256
        H = 16
        D = 64
        INNER = H * D
        EPS = 1e-05

        def layernorm(x, w, b):
            mu = jnp.mean(x, axis=-1, keepdims=True)
            var = jnp.var(x, axis=-1, keepdims=True)
            return (x - mu) * jax.lax.rsqrt(var + EPS) * w + b
        b, n, _ = latents.shape
        s = context.shape[1]
        lat = layernorm(latents, ln_l_w, ln_l_b)
        ctx = layernorm(context, ln_c_w, ln_c_b)
        q = (lat @ Wq).reshape(b, n, H, D).transpose(0, 2, 1, 3)
        kv = ctx @ Wkv
        k, v = jnp.split(kv, 2, axis=-1)
        k = k.reshape(b, s, H, D).transpose(0, 2, 1, 3)
        v = v.reshape(b, s, H, D).transpose(0, 2, 1, 3)
        scale = D ** (-0.5)
        attn = jnp.einsum('bhnd,bhsd->bhns', q, k) * scale
        attn = jnp.clip(attn, -11.0, 11.0)
        attn = jax.nn.softmax(attn, axis=-1)
        out = jnp.einsum('bhns,bhsd->bhnd', attn, v)
        out = out.transpose(0, 2, 1, 3).reshape(b, n, INNER)
        return out @ Wo + bo

    def _L0_ffn_ref(x, wg, w1, w2, w3, sw1, sw2, sw3):
        import jax, jax.numpy as jnp
        import numpy as np
        DIM = 256
        INTER = 256
        E = 32
        K = 4
        G = 8
        LG = 4
        ROUTE_SCALE = 1.0
        CAP_FACTOR = 1.25
        B, S = (4, 512)

        def _gate(xf, wg):
            logits = xf @ wg.T
            scores = jax.nn.softmax(logits, axis=-1)
            sg = scores.reshape(-1, G, E // G)
            group_scores = sg.max(axis=-1)
            _, gtop = jax.lax.top_k(group_scores, LG)
            keep_g = jnp.sum(jax.nn.one_hot(gtop, G, dtype=jnp.float32), axis=1) > 0
            masked = jnp.where(keep_g[:, :, None], sg, -jnp.inf).reshape(-1, E)
            _, idx = jax.lax.top_k(masked, K)
            w = jnp.take_along_axis(scores, idx, axis=1)
            w = w / (w.sum(-1, keepdims=True) + 1e-09) * ROUTE_SCALE
            return (w.astype(xf.dtype), idx)

        def _forward(x, wg, w1, w2, w3, sw1, sw2, sw3):
            shape = x.shape
            xf = x.reshape(-1, DIM)
            N = xf.shape[0]
            cap = max(1, int(CAP_FACTOR * N * K / E))
            w, idx = _gate(xf, wg)
            fe = idx.reshape(-1)
            oh = jax.nn.one_hot(fe, E, dtype=jnp.int32)
            pos = (jnp.cumsum(oh, axis=0) * oh).sum(-1) - 1
            keep = pos < cap
            dest = jnp.where(keep, fe * cap + pos, E * cap)
            tok = jnp.arange(N * K, dtype=jnp.int32) // K
            buf_tok = jnp.full((E * cap + 1,), N, jnp.int32).at[dest].set(tok)[:-1]
            buf_w = jnp.zeros((E * cap + 1,), x.dtype).at[dest].set(w.reshape(-1))[:-1]
            xp = jnp.concatenate([xf, jnp.zeros((1, DIM), x.dtype)], axis=0)
            xe = xp[buf_tok].reshape(E, cap, DIM)
            h = jax.nn.silu(jnp.einsum('ecd,edh->ech', xe, w1)) * jnp.einsum('ecd,edh->ech', xe, w3)
            out = jnp.einsum('ech,ehd->ecd', h, w2) * buf_w.reshape(E, cap, 1)
            y = jnp.zeros((N + 1, DIM), x.dtype).at[buf_tok].add(out.reshape(E * cap, DIM))[:N]
            z = jax.nn.silu(xf @ sw1) * (xf @ sw3) @ sw2
            return (y + z).reshape(shape)
        return _forward(x, wg, w1, w2, w3, sw1, sw2, sw3)

    def _L1_xattn_ref(query, key, value, Wq, bq, Wk, bk, Wv, bv, Wo, bo, rel):
        import jax, jax.numpy as jnp
        import numpy as np
        H = 16
        D = 256
        DK = D // H
        WIDTH = 64
        LEFT_TO_RIGHT = True
        B, S = (2, 512)
        SCALE = float(1.0 / np.sqrt(DK))

        def rel_bias(rel, seq_len):
            i = jnp.arange(seq_len)[:, None]
            j = jnp.arange(seq_len)[None, :]
            d = i - j if LEFT_TO_RIGHT else j - i
            valid = (d >= 0) & (d <= WIDTH)
            idx = jnp.where(valid, WIDTH - d if LEFT_TO_RIGHT else d, 0)
            return jnp.where(valid[None], rel[:, idx], 0.0)
        b, s, _ = query.shape

        def proj(x, W, bias):
            return (x @ W + bias).reshape(b, s, H, DK).transpose(0, 2, 1, 3)
        q = proj(query, Wq, bq)
        k = proj(key, Wk, bk)
        v = proj(value, Wv, bv)
        scores = jnp.einsum('bhqd,bhkd->bhqk', q, k) * SCALE + rel_bias(rel, s)[None]
        p = jax.nn.softmax(scores, axis=-1)
        x = jnp.einsum('bhqk,bhkd->bhqd', p, v)
        x = x.transpose(0, 2, 1, 3).reshape(b, s, H * DK)
        return x @ Wo + bo

    def _L1_ffn_ref(x, weight):
        import jax, jax.numpy as jnp
        import numpy as np
        b_weight = jnp.sign(weight)
        return jnp.einsum('bsi,oi->bso', x, b_weight)
    x = x + jnp.tanh(g_xattn[0]) * _L0_xattn_ref(_layernorm(x, axis=-1), ctx_1024, L0_xattn_ln_l_w, L0_xattn_ln_l_b, L0_xattn_ln_c_w, L0_xattn_ln_c_b, L0_xattn_Wq, L0_xattn_Wkv, L0_xattn_Wo, L0_xattn_bo)
    x = x + jnp.tanh(g_ffn[0]) * _L0_ffn_ref(_layernorm(x, axis=-1), L0_ffn_wg, L0_ffn_w1, L0_ffn_w2, L0_ffn_w3, L0_ffn_sw1, L0_ffn_sw2, L0_ffn_sw3)
    x = x + jnp.tanh(g_xattn[1]) * _L1_xattn_ref(_layernorm(x, axis=-1), ctx_1024, ctx_1024, L1_xattn_Wq, L1_xattn_bq, L1_xattn_Wk, L1_xattn_bk, L1_xattn_Wv, L1_xattn_bv, L1_xattn_Wo, L1_xattn_bo, L1_xattn_rel)
    x = x + jnp.tanh(g_ffn[1]) * _L1_ffn_ref(_layernorm(x, axis=-1), L1_ffn_weight)
    return x

_drawn_inputs = setup_inputs


def setup_inputs(seed=0):
    import zlib

    import numpy as np

    out = dict(_drawn_inputs(seed))
    spreads = {'g_ffn': (-1.0, 0.2),
     'L0_xattn_ln_l_w': (1.0, 0.2),
     'L0_xattn_ln_l_b': (0.0, 0.333),
     'L0_xattn_ln_c_w': (1.0, 0.2),
     'L0_xattn_ln_c_b': (0.0, 0.1),
     'L0_xattn_bo': (0.0, 0.1),
     'L1_xattn_bq': (0.0, 0.8),
     'L1_xattn_bk': (0.0, 0.8),
     'L1_xattn_bv': (0.0, 0.304),
     'L1_xattn_bo': (0.0, 0.1)}
    factors = {'L1_xattn_Wq': 8.0, 'L1_xattn_Wk': 8.0, 'L1_xattn_rel': 8.0}
    for name, (base, spread) in spreads.items():
        noise = np.random.default_rng([zlib.crc32(name.encode()), seed]).standard_normal(out[name].shape)
        drawn = base * np.exp(spread * noise) if base else spread * noise
        out[name] = jnp.asarray(drawn.astype(out[name].dtype))
    for name, factor in factors.items():
        out[name] = (out[name] * factor).astype(out[name].dtype)
    return out
```

```python
from contextlib import ExitStack

import concourse.bass as bass
from concourse import mybir

P = 128
ALU = mybir.AluOpType
ACT = mybir.ActivationFunctionType
F32 = mybir.dt.float32
U32 = mybir.dt.uint32
AX = mybir.AxisListType

EPS = 1e-5
CLIP = 11.0


def flamingo_kernel(
    nc: bass.Bass,
    x, ctx_in, g_xattn, g_ffn,
    ln_l_w, ln_l_b, ln_c_w, ln_c_b, Wq, Wkv, Wo, bo,
    wg, w1, w2, w3, sw1, sw2, sw3,
    Wq1, bq1, Wk1, bk1, Wv1, bv1, Wo1, bo1, rel, sign_w,
    out,
):
    B, S, D = x.shape
    INNER = Wq.shape[1]
    H0, D0 = 16, INNER // 16
    PAIRS = H0 // 2
    E, F = wg.shape[0], w1.shape[2]
    K, G, LG = 4, 8, 4
    N = B * S
    NT = N // P
    T = S // P
    C = D // P
    CAP = int(1.25 * N * K / E)
    H1 = rel.shape[0]
    DK = D // H1
    WIDTH = rel.shape[1] - 1
    GR = H1 // 4
    SCALE1 = DK ** -0.5
    assert (T, C, NT, CAP) == (2, 2, 16, 320)

    stack = ExitStack()
    scratch_rel = nc.dram_tensor("scratch_rel", [H1, P, 4 * P - 1], F32, kind="Internal").ap()
    scratch_xe = nc.dram_tensor("scratch_xe", [E * CAP, D], F32, kind="Internal").ap()
    scratch_oe = nc.dram_tensor("scratch_oe", [E * CAP, D], F32, kind="Internal").ap()

    with stack as keep:
        def alloc(where):
            def sb(name, shape, dt=F32):
                return where.enter_context(nc.sbuf_tensor(name, shape, dt))
            return sb

        sb = alloc(keep)
        ident = sb("ident", [P, P])
        x_all = sb("x_all", [P, NT, D])
        gates = sb("gates", [P, 4])
        tgates = sb("tgates", [P, 4])
        neg_half = sb("neg_half", [P, NT])
        eps = sb("eps", [P, NT])
        row_index = sb("row_index", [P, NT, K], U32)
        row_weight = sb("row_weight", [P, NT, K])
        z_all = sb("z_all", [P, NT, D])
        rel_bias = sb("rel_bias", [P, H1, 3 * P])

        xattn0(nc, keep, locals())
        moe(nc, keep, locals())
        xattn1(nc, keep, locals())


def make_tools(nc, phase, name):
    def sb(n, shape, dt=F32):
        return phase.enter_context(nc.sbuf_tensor(f"{name}_{n}", shape, dt))

    def ps(n, shape, dt=F32):
        return phase.enter_context(nc.psum_tensor(f"{name}_{n}", shape, dt))

    def sem(n):
        return phase.enter_context(nc.semaphore(f"{name}_{n}"))

    return sb, ps, sem


class Ordered:

    def __init__(self, engine, sem, per_round):
        self.engine, self.sem, self.per_round = engine, sem, per_round
        self.base, self.count = 0, 0

    def start(self, rnd):
        assert self.count in (0, self.per_round)
        self.base, self.count = rnd * self.per_round, 0

    def done(self, instruction):
        self.count += 1
        instruction.then_inc(self.sem, 1)

    def wait(self):
        self.engine.wait_ge(self.sem, self.base + self.count)


def xattn0(nc, keep, env):
    x, ctx_in, g_xattn, g_ffn = env["x"], env["ctx_in"], env["g_xattn"], env["g_ffn"]
    ln_l_w, ln_l_b, ln_c_w, ln_c_b = env["ln_l_w"], env["ln_l_b"], env["ln_c_w"], env["ln_c_b"]
    Wq, Wkv, Wo, bo, rel = env["Wq"], env["Wkv"], env["Wo"], env["bo"], env["rel"]
    ident, x_all, gates, tgates, neg_half = env["ident"], env["x_all"], env["gates"], env["tgates"], env["neg_half"]
    eps = env["eps"]
    rel_bias, scratch_rel, scratch_xe = env["rel_bias"], env["scratch_rel"], env["scratch_xe"]
    B, D, INNER, T, C, PAIRS, D0, H0 = (env[k] for k in ("B", "D", "INNER", "T", "C", "PAIRS", "D0", "H0"))
    H1, WIDTH, E, CAP = (env[k] for k in ("H1", "WIDTH", "E", "CAP"))
    S = T * P
    SC = D0 ** -0.5

    with ExitStack() as phase:
        sb, ps, sem = make_tools(nc, phase, "a")
        ps_scores = ps("scores", [P, 2, 2, T, S])
        ps_pv = ps("pv", [P, 2, 512])
        ps_work = ps("work", [P, 2, 512])

        wq = sb("wq", [P, C, INNER])
        wkv = sb("wkv", [P, C, 2 * INNER])
        wo = sb("wo", [P, PAIRS, D])
        affine = sb("affine", [P, 4, C])
        bo_row = sb("bo_row", [P, D])
        bo_g = sb("bo_g", [P, D])
        xin = [sb(f"xin{i}", [P, T, D]) for i in range(2)]
        cin = [sb(f"cin{i}", [P, T, D]) for i in range(2)]
        stats = sb("stats", [P, 3 * T, 6])
        moments = sb("moments", [P, 3 * T, 2])
        var_eps = sb("var_eps", [P, 3 * T])
        rstd = sb("rstd", [P, 3 * T])
        xn = sb("xn", [P, T, D])
        lat = sb("lat", [P, T, D])
        cn = sb("cn", [P, T, D])
        latT = sb("latT", [P, C, S])
        ctxT = sb("ctxT", [P, C, S])
        qT = [sb(f"qT{i}", [P, PAIRS, S]) for i in range(2)]
        kT = [sb(f"kT{i}", [P, PAIRS, S]) for i in range(2)]
        v_aug = [sb(f"v{i}", [P, T, H0, D0 + 1]) for i in range(2)]
        clipped = sb("clipped", [P, 2, 2, T, S])
        probs = sb("probs", [P, 2, 2, T, S])
        rsum = sb("rsum", [P, 2, 2, 2])
        o_rows = sb("o_rows", [P, T, INNER])
        oT = sb("oT", [P, PAIRS, S])
        relpad = sb("relpad", [H1, 4 * P - 1])
        rel_in = sb("rel_in", [H1, WIDTH + 1])
        xb = [sb(f"xb{i}", [P, T, D]) for i in range(2)]
        ZR = 8
        ZERO_DMAS = E * CAP // (P * ZR)
        zeros = sb("zeros", [P, ZR * D])

        weights_loaded = sem("weights_loaded")
        params_loaded = sem("params_loaded")
        inputs_loaded = [sem(f"inputs_loaded{i}") for i in range(2)]
        rel_loaded = sem("rel_loaded")
        rel_stored = sem("rel_stored")
        bias_loaded = sem("bias_loaded")
        zeroed = sem("zeroed")
        ident_ready = sem("ident_ready")
        ones_ready = sem("ones_ready")
        consts_ready = sem("consts_ready")
        relpad_zero = sem("relpad_zero")
        relpad_ready = sem("relpad_ready")
        xb_ready = sem("xb_ready")
        gates_ready = sem("gates_ready")
        bo_ready = sem("bo_ready")
        dve_steps = sem("dve_steps")
        moments_ready = sem("moments_ready")
        pool_steps = sem("pool_steps")
        rstd_ready = sem("rstd_ready")
        lat_ready = sem("lat_ready")
        front_ready = sem("front_ready")
        front_out = sem("front_out")
        scores_ready = sem("scores_ready")
        clip_ready = sem("clip_ready")
        probs_ready = sem("probs_ready")
        pv_ready = sem("pv_ready")
        rsum_ready = sem("rsum_ready")
        o_ready = sem("o_ready")
        oT_ready = sem("oT_ready")
        oT_out = sem("oT_out")
        y_ready = sem("y_ready")
        x_updated = sem("x_updated")

        FRONT = 14
        x_rows = x.rearrange("b (t p) d -> b p t d", p=P)
        c_rows = ctx_in.rearrange("b (t p) d -> b p t d", p=P)

        def batches(eng, front, attend):
            front(0, 0)
            with eng.Fori(0, B // 2 - 1) as i:
                attend(2 * i, 0, True)
                attend(2 * i + 1, 1, True)
            attend(B - 2, 0, True)
            attend(B - 1, 1, False)

        block = phase.enter_context(nc.Block())

        @block.sync
        def _(sp):
            def load(b, p):
                sp.dma_start(xin[p][:], x_rows[bass.ds(b, 1)].rearrange("b p t d -> p (b t) d")).then_inc(inputs_loaded[p], 16)
                sp.dma_start(cin[p][:], c_rows[bass.ds(b, 1)].rearrange("b p t d -> p (b t) d")).then_inc(inputs_loaded[p], 16)

            load(0, 0)
            for i, v in enumerate((ln_l_w, ln_l_b, ln_c_w, ln_c_b)):
                sp.dma_start(affine[:, i, :], v.rearrange("(c p) -> p c", p=P), allow_slow_non_contiguous=True).then_inc(params_loaded, 16)
            sp.dma_start(bo_row[:], bo.partition_broadcast(P)).then_inc(params_loaded, 16)
            for i, v in enumerate((g_xattn, g_ffn)):
                sp.dma_start(gates[:, 2 * i:2 * i + 2], v.partition_broadcast(P)).then_inc(params_loaded, 16)
            sp.dma_start(wq[:], Wq.rearrange("(c p) n -> p c n", p=P)).then_inc(weights_loaded, 16)
            sp.dma_start(wkv[:], Wkv.rearrange("(c p) n -> p c n", p=P)).then_inc(weights_loaded, 16)
            load(1, 1)
            sp.dma_start(wo[:], Wo.rearrange("(j p) n -> p j n", p=P)).then_inc(weights_loaded, 16)
            sp.dma_start(rel_in[:], rel).then_inc(rel_loaded, 16)
            sp.wait_ge(relpad_ready, 1)
            sp.dma_start(scratch_rel, relpad[:].unsqueeze(1).to_broadcast([H1, P, 4 * P - 1])).then_inc(rel_stored, 16)
            sp.wait_ge(rel_stored, 16)
            sp.dma_start(rel_bias[:], bass.AP(scratch_rel.tensor, P - 1, [[4 * P - 2, P], [P * (4 * P - 1), H1], [1, 3 * P]])).then_inc(bias_loaded, 16)
            sp.wait_ge(consts_ready, 3)
            for j in range(ZERO_DMAS):
                rows = scratch_xe[j * P * ZR:(j + 1) * P * ZR, :]
                sp.dma_start(rows.rearrange("(p r) d -> p (r d)", p=P), zeros[:]).then_inc(zeroed, 16)
            with sp.Fori(1, B // 2) as i:
                for p in range(2):
                    sp.wait_ge(x_updated, (2 * i - 1 + p) * T)
                    load(2 * i + p, p)
            sp.wait_ge(bias_loaded, 16)
            sp.wait_ge(zeroed, 16 * ZERO_DMAS)

        @block.gpsimd
        def _(pool):
            nc.gpsimd.memset(ident[:], 0.0).then_inc(consts_ready, 1)
            nc.gpsimd.memset(neg_half[:], -0.5).then_inc(consts_ready, 1)
            nc.gpsimd.memset(zeros[:], 0.0).then_inc(consts_ready, 1)
            nc.gpsimd.memset(eps[:], EPS).then_inc(consts_ready, 1)
            pool.wait_ge(consts_ready, 4)
            nc.gpsimd.affine_select(out=ident[:], in_=ident[:], compare_op=ALU.not_equal, fill=1.0, base=0,
                                    pattern=[[-1, P]], channel_multiplier=1).then_inc(ident_ready, 1)
            for i in range(2):
                nc.gpsimd.memset(v_aug[i][:, :, :, D0:D0 + 1], 1.0).then_inc(ones_ready, 1)
            own = Ordered(pool, pool_steps, 2)

            with pool.Fori(0, B) as b:
                own.start(b)
                for lo, hi in ((0, 2 * T), (2 * T, 3 * T)):
                    pool.wait_ge(moments_ready, 3 * T * b + hi)
                    own.done(nc.gpsimd.tensor_tensor(var_eps[:, lo:hi], moments[:, lo:hi, 1], eps[:, lo:hi], ALU.add))
                    own.wait()
                    nc.gpsimd.tensor_tensor(rstd[:, lo:hi], var_eps[:, lo:hi], neg_half[:, lo:hi], ALU.pow).then_inc(rstd_ready, 1)

        @block.vector
        def _(dve):
            own = Ordered(dve, dve_steps, 4 * T)

            def front(b, p, step=None):
                if step in (None, 0):
                    own.start(b)
                    dve.wait_ge(inputs_loaded[p], 16 * (b - p) + 32)
                    for n in range(2 * T):
                        own.done(nc.vector.bn_stats(stats[:, n, :], (xin[p], cin[p])[n // T][:, n % T, :]))
                    own.wait()
                    nc.vector.tensor_tensor(xb[p][:], xin[p][:], bo_g[:].unsqueeze(1).to_broadcast([P, T, D]), ALU.add).then_inc(xb_ready, 1)
                    for n in range(2 * T):
                        nc.vector.bn_aggr(moments[:, n, :], stats[:, n, :]).then_inc(moments_ready, 1)
                if step in (None, 1):
                    dve.wait_ge(rstd_ready, 2 * b + 1)
                    if step is not None:
                        dve.wait_ge(front_ready, FRONT * (b - 1) + 2)
                    for t in range(T):
                        own.done(nc.vector.tensor_scalar(xn[:, t, :], xin[p][:, t, :], moments[:, t, 0:1], rstd[:, t:t + 1],
                                                         ALU.subtract, ALU.mult))
                if step in (None, 2):
                    own.wait()
                    for t in range(T):
                        own.done(nc.vector.bn_stats(stats[:, 2 * T + t, :], xn[:, t, :]))
                    own.wait()
                    for t in range(T):
                        nc.vector.tensor_scalar(cn[:, t, :], cin[p][:, t, :], moments[:, T + t, 0:1], rstd[:, T + t:T + t + 1],
                                                ALU.subtract, ALU.mult).then_inc(lat_ready, 1)
                    for t in range(T):
                        nc.vector.bn_aggr(moments[:, 2 * T + t, :], stats[:, 2 * T + t, :]).then_inc(moments_ready, 1)
                if step in (None, 3):
                    dve.wait_ge(rstd_ready, 2 * b + 2)
                    for t in range(T):
                        m = 2 * T + t
                        nc.vector.tensor_scalar(lat[:, t, :], xn[:, t, :], moments[:, m, 0:1], rstd[:, m:m + 1],
                                                ALU.subtract, ALU.mult).then_inc(lat_ready, 1)

            def clip(b, j):
                dve.wait_ge(scores_ready, PAIRS * b + j + 1)
                dve.wait_ge(probs_ready, PAIRS * b + max(j - 1, 0))
                nc.vector.tensor_scalar(clipped[:, j % 2], ps_scores[:, j % 2], CLIP / SC, -CLIP / SC,
                                        ALU.min, ALU.max).then_inc(clip_ready, 1)

            def normalise(b, j):
                dve.wait_ge(pv_ready, PAIRS * b + j + 1)
                if j == 0:
                    dve.wait_ge(oT_ready, 4 * b)
                pv = ps_pv[:, j % 2, 0:T * 2 * (D0 + 1)].rearrange("p (t h d) -> p t h d", t=T, h=2)
                nc.vector.reciprocal(rsum[:, j % 2], pv[:, :, :, D0]).then_inc(rsum_ready, 1)
                dve.wait_ge(rsum_ready, PAIRS * b + j + 1)
                nc.vector.tensor_tensor(o_rows[:, :, 2 * D0 * j:2 * D0 * (j + 1)].rearrange("p t (h d) -> p t h d", h=2),
                                        pv[:, :, :, 0:D0], rsum[:, j % 2].unsqueeze(3).to_broadcast([P, T, 2, D0]),
                                        ALU.mult).then_inc(o_ready, 1)

            def attend(b, p, more):
                for j in range(PAIRS):
                    clip(b, j)
                    if j >= 2:
                        normalise(b, j - 2)
                    if more and j >= 4:
                        front(b + 1, 1 - p, j - 4)
                for j in range(PAIRS - 2, PAIRS):
                    normalise(b, j)
                for t in range(T):
                    dve.wait_ge(y_ready, T * b + t + 1)
                    dve.wait_ge(xb_ready, b + 1)
                    nc.vector.scalar_tensor_tensor(x_all[:, bass.ds(T * b + t, 1), :].rearrange("p t d -> p (t d)"),
                                                   ps_work[:, t, 0:D], tgates[:, 0:1], xb[p][:, t, :],
                                                   ALU.mult, ALU.add).then_inc(x_updated, 1)

            dve.wait_ge(rel_loaded, 16)
            nc.vector.memset(relpad[:], 0.0).then_inc(relpad_zero, 1)
            dve.wait_ge(relpad_zero, 1)
            lead = P + P // 2 - 1
            nc.vector.tensor_scalar(relpad[:, lead:lead + WIDTH + 1], rel_in[:], -1.0, None, ALU.mult).then_inc(relpad_ready, 1)
            dve.wait_ge(gates_ready, 1)
            nc.vector.tensor_scalar(bo_g[:], bo_row[:], tgates[:, 0:1], None, ALU.mult).then_inc(bo_ready, 1)
            dve.wait_ge(bo_ready, 1)
            batches(dve, front, attend)

        @block.scalar
        def _(act):
            def front(b, p):
                for n in range(FRONT):
                    act.wait_ge(front_ready, FRONT * b + n + 1)
                    bank = ps_work[:, n % 2, :]
                    if n < 2:
                        for c in range(C):
                            ins = nc.scalar.activation((ctxT, latT)[n][:, c, :], bank[:, c * S:(c + 1) * S], ACT.Identity,
                                                       bias=affine[:, 3 - 2 * n, c:c + 1], scale=affine[:, 2 - 2 * n, c:c + 1])
                    elif n < 10:
                        dst = (qT, kT)[(n - 2) // 4][p]
                        m = 2 * ((n - 2) % 4)
                        ins = nc.scalar.copy(dst[:, m:m + 2, :].rearrange("p m s -> p (m s)"), bank[:])
                    else:
                        t, half = divmod(n - 10, 2)
                        hs = H0 // 2
                        ins = nc.scalar.copy(v_aug[p][:, t, half * hs:(half + 1) * hs, 0:D0],
                                             bank.rearrange("p (h d) -> p h d", d=D0))
                    ins.then_inc(front_out, 1)

            def attend(b, p, more):
                for j in range(PAIRS):
                    act.wait_ge(clip_ready, PAIRS * b + j + 1)
                    act.wait_ge(pv_ready, PAIRS * b + max(j - 1, 0))
                    nc.scalar.activation(probs[:, j % 2], clipped[:, j % 2], ACT.Exp, scale=SC).then_inc(probs_ready, 1)
                if more:
                    front(b + 1, 1 - p)
                for n in range(4):
                    act.wait_ge(oT_ready, 4 * b + n + 1)
                    nc.scalar.copy(oT[:, 2 * n:2 * n + 2, :].rearrange("p m s -> p (m s)"), ps_work[:, n % 2, :]).then_inc(oT_out, 1)

            act.wait_ge(params_loaded, 16 * 7)
            nc.scalar.activation(tgates[:], gates[:], ACT.Tanh).then_inc(gates_ready, 1)
            batches(act, front, attend)

        @block.tensor
        def _(pe):
            def front(b, p):
                for n in range(FRONT):
                    bank = ps_work[:, n % 2, :]
                    if n < 2:
                        if isinstance(b, int) and b == 0:
                            pe.wait_ge(ident_ready, 1)
                        else:
                            pe.wait_ge(front_out, FRONT * b)
                            pe.wait_ge(x_updated, T * (b - 1))
                        pe.wait_ge(lat_ready, 2 * T * b + (T, 2 * T)[n])
                        rows = (cn, lat)[n]
                        for c in range(C):
                            for t in range(T):
                                ins = nc.tensor.transpose(bank[:, c * S + t * P:c * S + (t + 1) * P],
                                                          rows[:, t, c * P:(c + 1) * P], ident[:])
                    elif n < 10:
                        pe.wait_ge(front_out, FRONT * b + max(n - 1, 2))
                        for k in range(2):
                            m = 2 * ((n - 2) % 4) + k
                            for c in range(C):
                                w = (wq, wkv)[(n - 2) // 4][:, c, m * P:(m + 1) * P]
                                ins = nc.tensor.matmul(bank[:, k * S:(k + 1) * S], w, (latT, ctxT)[(n - 2) // 4][:, c, :],
                                                       start=(c == 0), stop=(c == C - 1))
                    else:
                        pe.wait_ge(front_out, FRONT * b + n - 1)
                        t, half = divmod(n - 10, 2)
                        for c in range(C):
                            ins = nc.tensor.matmul(bank, ctxT[:, c, t * P:(t + 1) * P],
                                                   wkv[:, c, INNER + half * 512:INNER + (half + 1) * 512],
                                                   start=(c == 0), stop=(c == C - 1))
                    ins.then_inc(front_ready, 1)

            def scores(b, p, j):
                pe.wait_ge(clip_ready, PAIRS * b + max(j - 1, 0))
                for h in range(2):
                    rows = slice(h * D0, (h + 1) * D0)
                    for t in range(T):
                        ins = nc.tensor.matmul(ps_scores[:, j % 2, h, t, :], kT[p][rows, j, t * P:(t + 1) * P], qT[p][rows, j, :],
                                               start=True, stop=True)
                ins.then_inc(scores_ready, 1)

            def values(b, p, j):
                pe.wait_ge(probs_ready, PAIRS * b + j + 1)
                pe.wait_ge(o_ready, PAIRS * b + max(j - 1, 0))
                for tq in range(T):
                    for h in range(2):
                        at = (2 * tq + h) * (D0 + 1)
                        for t in range(T):
                            ins = nc.tensor.matmul(ps_pv[:, j % 2, at:at + D0 + 1], probs[:, j % 2, h, t, tq * P:(tq + 1) * P],
                                                   v_aug[p][:, t, 2 * j + h, :], start=(t == 0), stop=(t == T - 1))
                ins.then_inc(pv_ready, 1)

            def attend(b, p, more):
                pe.wait_ge(front_out, FRONT * b + FRONT)
                scores(b, p, 0)
                scores(b, p, 1)
                for j in range(PAIRS):
                    if j + 2 < PAIRS:
                        scores(b, p, j + 2)
                    values(b, p, j)
                if more:
                    front(b + 1, 1 - p)
                    pe.wait_ge(front_out, FRONT * b + 2 * FRONT)
                else:
                    pe.wait_ge(x_updated, T * b)
                pe.wait_ge(o_ready, PAIRS * b + PAIRS)
                for n in range(4):
                    if n >= 2:
                        pe.wait_ge(oT_out, 4 * b + n - 1)
                    for k in range(2):
                        m = 2 * n + k
                        for t in range(T):
                            ins = nc.tensor.transpose(ps_work[:, n % 2, k * S + t * P:k * S + (t + 1) * P],
                                                      o_rows[:, t, m * P:(m + 1) * P], ident[:])
                    ins.then_inc(oT_ready, 1)
                pe.wait_ge(oT_out, 4 * b + 4)
                for t in range(T):
                    for m in range(PAIRS):
                        ins = nc.tensor.matmul(ps_work[:, t, 0:D], oT[:, m, t * P:(t + 1) * P], wo[:, m, :],
                                               start=(m == 0), stop=(m == PAIRS - 1))
                    ins.then_inc(y_ready, 1)

            pe.wait_ge(weights_loaded, 48)
            pe.wait_ge(ones_ready, 2)
            batches(pe, front, attend)


def moe(nc, keep, env):
    wg, w1, w2, w3, sw1, sw2, sw3 = (env[k] for k in ("wg", "w1", "w2", "w3", "sw1", "sw2", "sw3"))
    x_all, ident, neg_half, eps, z_all = (env[k] for k in ("x_all", "ident", "neg_half", "eps", "z_all"))
    row_index, row_weight, scratch_xe, scratch_oe = (env[k] for k in ("row_index", "row_weight", "scratch_xe", "scratch_oe"))
    E, K, G, LG, CAP, NT, D, F, C = (env[k] for k in ("E", "K", "G", "LG", "CAP", "NT", "D", "F", "C"))
    EG = E // G
    TG = 4
    NG = NT // TG
    GS = TG * P
    FC = F // P
    FAR = float(1 << 20)
    tails = ((0, 2, P), (2, 3, CAP - 2 * P))

    with ExitStack() as phase:
        sb, ps, sem = make_tools(nc, phase, "m")
        ps_turn = ps("turn", [P, C, 512])
        ps_h = ps("h", [P, 2, FC, 512])
        ps_out = ps("out", [P, 2, 512])

        xf = sb("xf", [P, NT, D])
        xfT = sb("xfT", [P, C, NT * P])
        wg_rows = sb("wg_rows", [E, D])
        wgT = sb("wgT", [P, C, E])
        s1 = sb("s1", [P, C, F])
        s3 = sb("s3", [P, C, F])
        s2 = sb("s2", [P, FC, D])
        stats = sb("stats", [P, NT, 6])
        moments = sb("moments", [P, NT, 2])
        var_eps = sb("var_eps", [P, NT])
        rstd = sb("rstd", [P, NT])
        count_e = sb("count_e", [P, E])
        before = sb("before", [P, P])
        ones = sb("ones", [P, P])
        neg_max = sb("neg_max", [P, NT])
        logits = sb("logits", [P, NT, E])
        exps = sb("exps", [P, NT, E])
        total = sb("total", [P, NT])
        rtotal = sb("rtotal", [P, NT])
        score = sb("score", [P, NT, E])
        gmax = sb("gmax", [P, NT, G])
        gtop = sb("gtop", [P, NT, 8])
        gidx = sb("gidx", [P, NT, 8], U32)
        gidx_f = sb("gidx_f", [P, NT, LG])
        ghot = sb("ghot", [P, NT, LG, G])
        gkeep = sb("gkeep", [P, NT, G])
        gpen = sb("gpen", [P, NT, G])
        masked = sb("masked", [P, NT, E])
        etop = sb("etop", [P, NT, 8])
        eidx = sb("eidx", [P, NT, 8], U32)
        eidx_f = sb("eidx_f", [P, NT, K])
        wsum = sb("wsum", [P, NT])
        rwsum = sb("rwsum", [P, NT])
        ehot = sb("ehot", [P, NT, K, E])
        epos = sb("epos", [P, NT, K, E])
        chosen = sb("chosen", [P, NT, E])
        earlier = sb("earlier", [P, NT, E])
        pos = sb("pos", [P, NT, K])
        fits = sb("fits", [P, NT, K])
        dest = sb("dest", [P, NT, K])
        kept = sb("kept", [P, NT, K])
        away = sb("away", [P, NT, K])
        send_index = sb("send_index", [P, NT, K], U32)
        act_t = sb("act_t", [P, FC, GS])
        act_a = sb("act_a", [P, FC, GS])
        gated = sb("gated", [P, FC, GS])
        w1s = [sb(f"w1_{i}", [P, C, F]) for i in range(2)]
        w3s = [sb(f"w3_{i}", [P, C, F]) for i in range(2)]
        w2s = [sb(f"w2_{i}", [P, FC, D]) for i in range(2)]
        xe = [sb(f"xe{i}", [P, 3, D]) for i in range(2)]
        xeT = [sb(f"xeT{i}", [P, C, CAP]) for i in range(2)]
        e_tanh = sb("e_tanh", [P, FC, CAP])
        e_a = sb("e_a", [P, FC, CAP])
        e_gated = [sb(f"e_gated{i}", [P, FC, CAP]) for i in range(2)]
        oe = [sb(f"oe{i}", [P, 3, D]) for i in range(2)]

        shared_loaded = sem("shared_loaded")
        w13_loaded = [sem(f"w13_loaded{i}") for i in range(2)]
        w2_loaded = [sem(f"w2_loaded{i}") for i in range(2)]
        xe_loaded = [sem(f"xe_loaded{i}") for i in range(2)]
        stored = [sem(f"stored{i}") for i in range(2)]
        scattered = sem("scattered")
        tables_ready = sem("tables_ready")
        own_pool = sem("own_pool")
        own_dve = sem("own_dve")
        moments_ready = sem("moments_ready")
        rstd_ready = sem("rstd_ready")
        xf_ready = sem("xf_ready")
        turned = sem("turned")
        xfT_ready = sem("xfT_ready")
        wg_turned = sem("wg_turned")
        wgT_ready = sem("wgT_ready")
        logits_ready = sem("logits_ready")
        shifted_ready = sem("shifted_ready")
        exps_ready = sem("exps_ready")
        chosen_ready = sem("chosen_ready")
        pos_ready = sem("pos_ready")
        index_ready = sem("index_ready")
        sh_ready = sem("sh_ready")
        sh_tanh = sem("sh_tanh")
        sh_a = sem("sh_a")
        sh_gated = sem("sh_gated")
        z_ready = sem("z_ready")
        z_out = sem("z_out")
        e_turned = sem("e_turned")
        xeT_ready = sem("xeT_ready")
        h_ready = sem("h_ready")
        tanh_ready = sem("tanh_ready")
        a_ready = sem("a_ready")
        gated_ready = sem("gated_ready")
        o_ready = sem("o_ready")
        oe_ready = sem("oe_ready")

        block = phase.enter_context(nc.Block())

        @block.sync
        def _(sp):
            def load_w13(e, p):
                for w, s in ((w1, w1s), (w3, w3s)):
                    sp.dma_start(s[p][:], w[bass.ds(e, 1)].rearrange("e (c p) n -> p (e c) n", p=P)).then_inc(w13_loaded[p], 16)

            def load_w2(e, p):
                sp.dma_start(w2s[p][:], w2[bass.ds(e, 1)].rearrange("e (c p) n -> p (e c) n", p=P)).then_inc(w2_loaded[p], 16)

            def load_xe(e, p):
                for lo, hi, rows in tails:
                    src = scratch_xe[bass.ds(e * CAP + lo * P, (hi - lo) * rows)].rearrange("(c p) d -> p c d", p=rows)
                    sp.dma_start(xe[p][0:rows, lo:hi, :], src).then_inc(xe_loaded[p], 16)

            sp.dma_start(wg_rows[:], wg).then_inc(shared_loaded, 16)
            for w, s in ((sw1, s1), (sw3, s3), (sw2, s2)):
                sp.dma_start(s[:], w.rearrange("(c p) n -> p c n", p=P)).then_inc(shared_loaded, 16)
            load_w13(0, 0)
            load_w13(1, 1)
            load_w2(0, 0)
            sp.wait_ge(scattered, 16 * NT * K)
            load_xe(0, 0)
            load_xe(1, 1)
            with sp.Fori(1, E // 2) as i:
                for p in range(2):
                    e = 2 * i + p
                    sp.wait_ge(e_turned, e - 1)
                    load_xe(e, p)
                    sp.wait_ge(h_ready, e - 1)
                    load_w13(e, p)
                    sp.wait_ge(o_ready, 2 * (e - 2))
                    load_w2(e - 1, 1 - p)
            sp.wait_ge(o_ready, 2 * (E - 2))
            load_w2(E - 1, 1)

        @block.gpsimd
        def _(pool):
            nc.gpsimd.iota(count_e[:], [[1, E]], base=0, channel_multiplier=0,
                           allow_small_or_imprecise_dtypes=True).then_inc(tables_ready, 1)
            nc.gpsimd.memset(ones[:], 1.0).then_inc(tables_ready, 1)
            pool.wait_ge(tables_ready, 2)
            nc.gpsimd.affine_select(out=before[:], in_=ones[:], compare_op=ALU.is_gt, fill=0.0, base=0,
                                    pattern=[[1, P]], channel_multiplier=-1).then_inc(tables_ready, 1)
            for g in range(NG):
                at = slice(g * TG, (g + 1) * TG)
                pool.wait_ge(moments_ready, TG * (g + 1))
                nc.gpsimd.tensor_tensor(var_eps[:, at], moments[:, at, 1], eps[:, at], ALU.add).then_inc(own_pool, 1)
                pool.wait_ge(own_pool, g + 1)
                nc.gpsimd.tensor_tensor(rstd[:, at], var_eps[:, at], neg_half[:, at], ALU.pow).then_inc(rstd_ready, 1)
            pool.wait_ge(index_ready, 1)
            for t in range(NT):
                for k in range(K):
                    nc.gpsimd.indirect_dma_start(
                        out=scratch_xe, out_offset=bass.IndirectOffsetOnAxis(ap=send_index[:, t, k:k + 1], axis=0),
                        in_=xf[:, t, :], in_offset=None, bounds_check=E * CAP - 1, oob_is_err=False).then_inc(scattered, 16)
            pool.wait_ge(scattered, 16 * NT * K)

        @block.vector
        def _(dve):
            own = Ordered(dve, own_dve, 0)

            def step(instruction):
                own.done(instruction)
                own.wait()

            def moments_of(g):
                for t in range(g * TG, (g + 1) * TG):
                    own.done(nc.vector.bn_stats(stats[:, t, :], x_all[:, t, :]))
                own.wait()
                for t in range(g * TG, (g + 1) * TG):
                    nc.vector.bn_aggr(moments[:, t, :], stats[:, t, :]).then_inc(moments_ready, 1)

            moments_of(0)
            for g in range(NG):
                if g + 1 < NG:
                    moments_of(g + 1)
                dve.wait_ge(rstd_ready, g + 1)
                for t in range(g * TG, (g + 1) * TG):
                    nc.vector.tensor_scalar(xf[:, t, :], x_all[:, t, :], moments[:, t, 0:1], rstd[:, t:t + 1],
                                            ALU.subtract, ALU.mult).then_inc(xf_ready, 1)

            raw = ps_turn[:, 0, :].rearrange("p (t e) -> p t e", e=E)
            dve.wait_ge(logits_ready, NG)
            step(nc.vector.tensor_reduce(neg_max[:], raw, AX.X, ALU.max, negate=True))
            nc.vector.tensor_tensor(logits[:], raw, neg_max[:].unsqueeze(2).to_broadcast([P, NT, E]), ALU.add).then_inc(shifted_ready, 1)
            dve.wait_ge(exps_ready, 1)
            step(nc.vector.tensor_reduce(total[:], exps[:], AX.X, ALU.add))
            step(nc.vector.reciprocal(rtotal[:], total[:]))
            step(nc.vector.tensor_tensor(score[:], exps[:], rtotal[:].unsqueeze(2).to_broadcast([P, NT, E]), ALU.mult))
            step(nc.vector.tensor_reduce(gmax[:], score[:].rearrange("p t (g e) -> p t g e", g=G), AX.X, ALU.max))
            for t in range(NT):
                own.done(nc.vector.max(gtop[:, t, :], gmax[:, t, :]))
            own.wait()
            for t in range(NT):
                own.done(nc.vector.max_index(gidx[:, t, :], gtop[:, t, :], gmax[:, t, :]))
            own.wait()
            step(nc.vector.tensor_copy(gidx_f[:], gidx[:, :, 0:LG]))
            dve.wait_ge(tables_ready, 3)
            step(nc.vector.tensor_tensor(ghot[:], count_e[:, 0:G].unsqueeze(1).unsqueeze(1).to_broadcast([P, NT, LG, G]),
                                         gidx_f[:].unsqueeze(3).to_broadcast([P, NT, LG, G]), ALU.is_equal))
            step(nc.vector.tensor_reduce(gkeep[:], ghot[:].rearrange("p t k g -> p t g k"), AX.X, ALU.add))
            own.done(nc.vector.tensor_scalar(gpen[:], gkeep[:], -1.0, None, ALU.add))
            step(nc.vector.tensor_tensor(masked[:].rearrange("p t (g e) -> p t g e", g=G), score[:].rearrange("p t (g e) -> p t g e", g=G),
                                         gkeep[:].unsqueeze(3).to_broadcast([P, NT, G, EG]), ALU.mult))
            step(nc.vector.tensor_tensor(masked[:].rearrange("p t (g e) -> p t g e", g=G), masked[:].rearrange("p t (g e) -> p t g e", g=G),
                                         gpen[:].unsqueeze(3).to_broadcast([P, NT, G, EG]), ALU.add))
            for t in range(NT):
                own.done(nc.vector.max(etop[:, t, :], masked[:, t, :]))
            own.wait()
            for t in range(NT):
                own.done(nc.vector.max_index(eidx[:, t, :], etop[:, t, :], masked[:, t, :]))
            own.wait()
            own.done(nc.vector.tensor_copy(eidx_f[:], eidx[:, :, 0:K]))
            step(nc.vector.tensor_reduce(wsum[:], etop[:, :, 0:K], AX.X, ALU.add))
            step(nc.vector.tensor_tensor(ehot[:], count_e[:].unsqueeze(1).unsqueeze(1).to_broadcast([P, NT, K, E]),
                                         eidx_f[:].unsqueeze(3).to_broadcast([P, NT, K, E]), ALU.is_equal))
            step(nc.vector.tensor_reduce(chosen[:], ehot[:].rearrange("p t k e -> p t e k"), AX.X, ALU.add))
            step(nc.vector.memset(earlier[:, 0, :], 0.0))
            for t in range(1, NT):
                step(nc.vector.tensor_tensor(earlier[:, t, :], earlier[:, t - 1, :], chosen[:, t - 1, :], ALU.add))
            nc.vector.engine_nop().then_inc(chosen_ready, 1)
            step(nc.vector.tensor_scalar(wsum[:], wsum[:], 1e-9, None, ALU.add))
            step(nc.vector.reciprocal(rwsum[:], wsum[:]))
            step(nc.vector.tensor_tensor(row_weight[:], etop[:, :, 0:K], rwsum[:].unsqueeze(2).to_broadcast([P, NT, K]), ALU.mult))
            dve.wait_ge(pos_ready, 1)
            places = ps_turn[:, 1, :].rearrange("p (t e) -> p t e", e=E)
            step(nc.vector.tensor_tensor(epos[:], ehot[:], places.unsqueeze(2).to_broadcast([P, NT, K, E]), ALU.mult))
            step(nc.vector.tensor_reduce(pos[:], epos[:], AX.X, ALU.add))
            own.done(nc.vector.tensor_scalar(fits[:], pos[:], float(CAP), None, ALU.is_lt))
            step(nc.vector.scalar_tensor_tensor(out=dest[:], in0=eidx_f[:], scalar=float(CAP), in1=pos[:], op0=ALU.mult, op1=ALU.add))
            own.done(nc.vector.tensor_tensor(kept[:], dest[:], fits[:], ALU.mult))
            own.done(nc.vector.tensor_scalar(away[:], fits[:], -FAR, FAR, ALU.mult, ALU.add))
            step(nc.vector.tensor_tensor(row_weight[:], row_weight[:], fits[:], ALU.mult))
            nc.vector.tensor_tensor(send_index[:], kept[:], away[:], ALU.add).then_inc(index_ready, 1)
            step(nc.vector.tensor_copy(row_index[:], kept[:]))

            for g in range(NG):
                dve.wait_ge(sh_tanh, g + 1)
                if g:
                    dve.wait_ge(sh_gated, FC * g)
                for m in range(FC):
                    nc.vector.scalar_tensor_tensor(out=act_a[:, m, :], in0=act_t[:, m, :], scalar=1.0, in1=ps_h[:, 0, m, :],
                                                   op0=ALU.add, op1=ALU.mult).then_inc(sh_a, 1)
                dve.wait_ge(sh_a, FC * (g + 1))
                dve.wait_ge(z_ready, 2 * g)
                for m in range(FC):
                    nc.vector.scalar_tensor_tensor(out=gated[:, m, :], in0=act_a[:, m, :], scalar=0.5, in1=ps_h[:, 1, m, :],
                                                   op0=ALU.mult, op1=ALU.mult).then_inc(sh_gated, 1)

            def gate(e, p):
                dve.wait_ge(tanh_ready, e + 1)
                for m in range(FC):
                    nc.vector.scalar_tensor_tensor(out=e_a[:, m, :], in0=e_tanh[:, m, :], scalar=1.0, in1=ps_h[:, 0, m, 0:CAP],
                                                   op0=ALU.add, op1=ALU.mult).then_inc(a_ready, 1)
                dve.wait_ge(a_ready, FC * (e + 1))
                for m in range(FC):
                    nc.vector.scalar_tensor_tensor(out=e_gated[p][:, m, :], in0=e_a[:, m, :], scalar=0.5, in1=ps_h[:, 1, m, 0:CAP],
                                                   op0=ALU.mult, op1=ALU.mult).then_inc(gated_ready, 1)

            with dve.Fori(0, E // 2) as i:
                for p in range(2):
                    gate(2 * i + p, p)

        @block.scalar
        def _(act):
            act.wait_ge(wg_turned, 1)
            nc.scalar.copy(wgT[:], ps_h[:, 0, 0, 0:C * E].rearrange("p (c e) -> p c e", c=C)).then_inc(wgT_ready, 1)
            for g in range(NG):
                for c in range(C):
                    act.wait_ge(turned, C * g + c + 1)
                    nc.scalar.copy(xfT[:, c, g * GS:(g + 1) * GS], ps_out[:, c, :]).then_inc(xfT_ready, 1)
            act.wait_ge(shifted_ready, 1)
            nc.scalar.activation(exps[:], logits[:], ACT.Exp).then_inc(exps_ready, 1)
            for g in range(NG):
                act.wait_ge(sh_ready, g + 1)
                if g:
                    act.wait_ge(sh_a, FC * g)
                nc.scalar.activation(act_t[:], ps_h[:, 0], ACT.Tanh, scale=0.5).then_inc(sh_tanh, 1)
                for half in range(2):
                    act.wait_ge(z_ready, 2 * g + half + 1)
                    t = g * TG + 2 * half
                    nc.scalar.copy(z_all[:, t:t + 2, :], ps_out[:, half, :].rearrange("p (t d) -> p t d", t=2)).then_inc(z_out, 1)

            def take_inputs(e, p):
                act.wait_ge(e_turned, e + 1)
                nc.scalar.copy(xeT[p][:], ps_turn[:, :, 0:CAP]).then_inc(xeT_ready, 1)

            def tanh(e):
                act.wait_ge(h_ready, e + 1)
                nc.scalar.activation(e_tanh[:], ps_h[:, 0, :, 0:CAP], ACT.Tanh, scale=0.5).then_inc(tanh_ready, 1)

            def put_outputs(e, p):
                for n, (lo, hi, rows) in enumerate(tails):
                    act.wait_ge(o_ready, 2 * e + n + 1)
                    if n == 0:
                        act.wait_ge(stored[p], 16 * (e - p))
                    nc.scalar.copy(oe[p][0:rows, lo:hi, :], ps_out[0:rows, n, 0:(hi - lo) * D].rearrange("p (c d) -> p c d", d=D)).then_inc(oe_ready, 1)
                for n, (lo, hi, rows) in enumerate(tails):
                    act.wait_ge(oe_ready, 2 * e + n + 1)
                    dst = scratch_oe[bass.ds(e * CAP + lo * P, (hi - lo) * rows)].rearrange("(c p) d -> p c d", p=rows)
                    act.dma_start(dst, oe[p][0:rows, lo:hi, :]).then_inc(stored[p], 16)

            take_inputs(0, 0)
            tanh(0)
            take_inputs(1, 1)
            with act.Fori(0, E // 2 - 1) as i:
                for p in (1, 0):
                    e = 2 * i + 2 - p
                    tanh(e)
                    take_inputs(e + 1, 1 - p)
                    put_outputs(e - 1, 1 - p)
            tanh(E - 1)
            put_outputs(E - 2, 0)
            put_outputs(E - 1, 1)
            for p in range(2):
                act.wait_ge(stored[p], 16 * E)

        @block.tensor
        def _(pe):
            pe.wait_ge(shared_loaded, 64)
            for c in range(C):
                ins = nc.tensor.transpose(ps_h[:, 0, 0, c * E:(c + 1) * E], wg_rows[:, c * P:(c + 1) * P], ident[0:E, 0:E])
            ins.then_inc(wg_turned, 1)
            pe.wait_ge(wgT_ready, 1)

            def route(g):
                pe.wait_ge(xfT_ready, C * (g + 1))
                for t in range(g * TG, (g + 1) * TG):
                    for c in range(C):
                        ins = nc.tensor.matmul(ps_turn[:, 0, t * E:(t + 1) * E], xfT[:, c, t * P:(t + 1) * P], wgT[:, c, :],
                                               start=(c == 0), stop=(c == C - 1))
                ins.then_inc(logits_ready, 1)

            for g in range(NG):
                pe.wait_ge(xf_ready, TG * (g + 1))
                for c in range(C):
                    if g:
                        pe.wait_ge(xfT_ready, C * (g - 1) + c + 1)
                    for t in range(TG):
                        ins = nc.tensor.transpose(ps_out[:, c, t * P:(t + 1) * P], xf[:, g * TG + t, c * P:(c + 1) * P], ident[:])
                    ins.then_inc(turned, 1)
                if g:
                    route(g - 1)
            route(NG - 1)

            def shared_h(g):
                pe.wait_ge(sh_gated, FC * g)
                for w, s in enumerate((s1, s3)):
                    for m in range(FC):
                        for c in range(C):
                            ins = nc.tensor.matmul(ps_h[:, w, m, :], s[:, c, m * P:(m + 1) * P], xfT[:, c, g * GS:(g + 1) * GS],
                                                   start=(c == 0), stop=(c == C - 1))
                ins.then_inc(sh_ready, 1)

            shared_h(0)
            pe.wait_ge(chosen_ready, 1)
            pe.wait_ge(tables_ready, 3)
            nc.tensor.matmul(ps_turn[:, 1, :], before[:], chosen[:].rearrange("p t e -> p (t e)"), start=True, stop=False)
            nc.tensor.matmul(ps_turn[:, 1, :], ones[:], earlier[:].rearrange("p t e -> p (t e)"), start=False, stop=True).then_inc(pos_ready, 1)
            for g in range(NG):
                if g:
                    shared_h(g)
                pe.wait_ge(sh_gated, FC * (g + 1))
                for half in range(2):
                    pe.wait_ge(z_out, max(2 * (g - 1) + half + 1, 0))
                    for k in range(2):
                        t = 2 * half + k
                        for m in range(FC):
                            ins = nc.tensor.matmul(ps_out[:, half, k * D:(k + 1) * D], gated[:, m, t * P:(t + 1) * P], s2[:, m, :],
                                                   start=(m == 0), stop=(m == FC - 1))
                    ins.then_inc(z_ready, 1)

            def turn(e, p):
                pe.wait_ge(xe_loaded[p], 16 * (e - p) + 32)
                pe.wait_ge(xeT_ready, e)
                for c in range(C):
                    for chunk in range(3):
                        rows = min(P, CAP - chunk * P)
                        ins = nc.tensor.transpose(ps_turn[:, c, chunk * P:chunk * P + rows],
                                                  xe[p][0:rows, chunk, c * P:(c + 1) * P], ident[0:rows, 0:rows])
                ins.then_inc(e_turned, 1)

            def hidden(e, p):
                pe.wait_ge(w13_loaded[p], 16 * (e - p) + 32)
                pe.wait_ge(xeT_ready, e + 1)
                pe.wait_ge(gated_ready, FC * e)
                for w, s in enumerate((w1s, w3s)):
                    for m in range(FC):
                        for c in range(C):
                            ins = nc.tensor.matmul(ps_h[:, w, m, 0:CAP], s[p][:, c, m * P:(m + 1) * P], xeT[p][:, c, :],
                                                   start=(c == 0), stop=(c == C - 1))
                ins.then_inc(h_ready, 1)

            def output(e, p):
                pe.wait_ge(w2_loaded[p], 8 * (e - p) + 16)
                pe.wait_ge(gated_ready, FC * (e + 1))
                for n, (lo, hi, rows) in enumerate(tails):
                    pe.wait_ge(oe_ready, 2 * e)
                    for chunk in range(lo, hi):
                        for m in range(FC):
                            ins = nc.tensor.matmul(ps_out[0:rows, n, (chunk - lo) * D:(chunk - lo + 1) * D],
                                                   e_gated[p][:, m, chunk * P:chunk * P + rows], w2s[p][:, m, :],
                                                   start=(m == 0), stop=(m == FC - 1))
                    ins.then_inc(o_ready, 1)

            pe.wait_ge(z_out, 2 * NG)
            pe.wait_ge(index_ready, 1)
            turn(0, 0)
            hidden(0, 0)
            turn(1, 1)
            with pe.Fori(0, E // 2 - 1) as i:
                for p in (1, 0):
                    e = 2 * i + 2 - p
                    hidden(e, p)
                    turn(e + 1, 1 - p)
                    output(e - 1, 1 - p)
            hidden(E - 1, 1)
            output(E - 2, 0)
            output(E - 1, 1)


def xattn1(nc, keep, env):
    ctx_in, out, sign_w, bo1, bv1 = (env[k] for k in ("ctx_in", "out", "sign_w", "bo1", "bv1"))
    Wq1, bq1, Wk1, bk1, Wv1, Wo1 = (env[k] for k in ("Wq1", "bq1", "Wk1", "bk1", "Wv1", "Wo1"))
    x_all, z_all, ident, neg_half, eps, tgates, rel_bias = (env[k] for k in ("x_all", "z_all", "ident", "neg_half", "eps", "tgates", "rel_bias"))
    row_index, row_weight, scratch_oe = env["row_index"], env["row_weight"], env["scratch_oe"]
    B, T, C, D, K, GR, DK, SCALE1 = (env[k] for k in ("B", "T", "C", "D", "K", "GR", "DK", "SCALE1"))
    H = env["H1"]
    S = T * P
    HG = H // GR
    FR = 6

    with ExitStack() as phase:
        sb, ps, sem = make_tools(nc, phase, "c")
        ps_scores = ps("scores", [P, 2, T, S])
        ps_turn = ps("turn", [P, 2, T, S])
        ps_o = ps("o", [P, T, H, DK])
        ps_work = ps("work", [P, 2, 512])

        wq_rows = sb("wq_rows", [P, C, D])
        wk_rows = sb("wk_rows", [P, C, D])
        wq = sb("wq", [P, C, GR * HG, 32])
        wk = sb("wk", [P, C, GR * HG, 32])
        wv = sb("wv", [P, C, D])
        wo = sb("wo", [P, C, D])
        sw_rows = sb("sw_rows", [P, C, D])
        sw_pos = sb("sw_pos", [P, C, D])
        sw_neg = sb("sw_neg", [P, C, D])
        sw_sign = sb("sw_sign", [P, C, D])
        swT = sb("swT", [P, C, D])
        bqk = sb("bqk", [P, 2, GR])
        bq_neg = sb("bq_neg", [P, GR])
        bv_row = sb("bv_row", [P, D])
        bo_row = sb("bo_row", [P, D])
        bo_g = sb("bo_g", [P, D])
        cin = [sb(f"cin{i}", [P, T, D]) for i in range(2)]
        index_now = [sb(f"index_now{i}", [P, T, K], U32) for i in range(2)]
        rows = [sb(f"rows{i}", [P, T, K, D]) for i in range(2)]
        acc = sb("acc", [P, T, D])
        x2 = sb("x2", [P, T, D])
        xb = [sb(f"xb{i}", [P, T, D]) for i in range(2)]
        weight_now = sb("weight_now", [P, T, K])
        stats = sb("stats", [P, 2, T, 6])
        moments = sb("moments", [P, 2, T, 2])
        var_eps = sb("var_eps", [P, 2, T])
        rstd = sb("rstd", [P, 2, T])
        xn = sb("xn", [P, T, D])
        xnT = sb("xnT", [P, C, S])
        ctxT = sb("ctxT", [P, C, S])
        qT = [sb(f"qT{i}", [P, GR, S]) for i in range(2)]
        kT = [sb(f"kT{i}", [P, GR, S]) for i in range(2)]
        v = [sb(f"v{i}", [P, T, D]) for i in range(2)]
        s_neg = sb("s_neg", [P, 2, T, S])
        max_neg = sb("max_neg", [P, 2, T])
        probs = sb("probs", [P, 2, T, S])
        rsum = sb("rsum", [P, H, T])
        rinv = sb("rinv", [P, H, T])
        pT = sb("pT", [P, 2, T, S])
        o_rows = sb("o_rows", [P, T, D])
        oT = sb("oT", [P, C, S])
        x3 = [sb(f"x3_{i}", [P, T, D]) for i in range(2)]
        x3n = sb("x3n", [P, T, D])
        x3T = sb("x3T", [P, C, S])
        fin = [sb(f"fin{i}", [P, T, D]) for i in range(2)]

        names = ("w_loaded", "b_zero", "b_loaded", "w_zero", "w_ready", "sign_parts", "sign_ready", "sign_turned", "swT_ready", "bq_ready", "bo_ready",
                 "own_front", "own_late", "own_pool", "own_pool_late", "scores_seen", "stats_seen", "index_seen", "f_moments", "f_rstd", "l_moments", "l_rstd", "index_copied", "weight_copied", "x2_ready", "xb_ready",
                 "xn_ready", "front_ready", "front_out", "v_ready", "v_out", "scores_ready", "biased", "probs_ready", "turned",
                 "pT_ready", "pv_ready", "rinv_ready", "o_ready", "oT_turned", "oT_out", "y_ready", "x3_ready", "x3n_ready", "x3_turned",
                 "x3T_out", "f_ready", "fin_ready")
        (w_loaded, b_zero, b_loaded, w_zero, w_ready, sign_parts, sign_ready, sign_turned, swT_ready, bq_ready, bo_ready,
         own_front, own_late, own_pool, own_pool_late, scores_seen, stats_seen, index_seen, f_moments, f_rstd, l_moments, l_rstd, index_copied, weight_copied, x2_ready, xb_ready,
         xn_ready, front_ready, front_out, v_ready, v_out, scores_ready, biased, probs_ready, turned,
         pT_ready, pv_ready, rinv_ready, o_ready, oT_turned, oT_out, y_ready, x3_ready, x3n_ready, x3_turned,
         x3T_out, f_ready, fin_ready) = [sem(n) for n in names]
        ctx_loaded = [sem(f"ctx_loaded{i}") for i in range(2)]
        gathered = [sem(f"gathered{i}") for i in range(2)]
        stored = [sem(f"stored{i}") for i in range(2)]

        c_rows = ctx_in.rearrange("b (t p) d -> b p t d", p=P)
        out_rows = out.rearrange("b (t p) d -> b p t d", p=P)

        def slots(eng, slot):
            slot(0, 0, True, False)
            with eng.Fori(0, B // 2 - 1) as i:
                slot(2 * i + 1, 1, True, True)
                slot(2 * i + 2, 0, True, True)
            slot(B - 1, 1, False, True)

        LATE_AT = (0, 2, 4, 12)
        LATE_TURN = 7
        FRONT_AT = (5, 7, 9, 11, 13)

        block = phase.enter_context(nc.Block())

        @block.sync
        def _(sp):
            def load(b, p):
                sp.dma_start(cin[p][:], c_rows[bass.ds(b, 1)].rearrange("b p t d -> p (b t) d")).then_inc(ctx_loaded[p], 16)

            load(0, 0)
            load(1, 1)
            for w, s in ((Wq1, wq_rows), (Wk1, wk_rows), (Wv1, wv), (Wo1, wo), (sign_w, sw_rows)):
                sp.dma_start(s[:], w.rearrange("(c p) n -> p c n", p=P)).then_inc(w_loaded, 16)
            for r, s in ((bv1, bv_row), (bo1, bo_row)):
                sp.dma_start(s[:], r.partition_broadcast(P)).then_inc(w_loaded, 16)
            sp.wait_ge(b_zero, 1)
            for n, r in enumerate((bq1, bk1)):
                for j in range(HG):
                    sp.dma_start(bqk[32 * j:32 * j + DK, n, :], r.rearrange("(g j i) -> j i g", j=HG, i=DK)[j],
                                 allow_slow_non_contiguous=True).then_inc(b_loaded, 16)
            with sp.Fori(1, B // 2) as i:
                for p in range(2):
                    b = 2 * i + p
                    sp.wait_ge(front_ready, FR * (b - 2) + 1)
                    load(b, p)
                    sp.wait_ge(fin_ready, T * (b - 1))
                    sp.dma_start(out_rows[bass.ds(b - 2, 1)].rearrange("b p t d -> p (b t) d"), fin[p][:]).then_inc(stored[p], 16)
            for b in (B - 2, B - 1):
                sp.wait_ge(fin_ready, T * (b + 1))
                sp.dma_start(out_rows[b], fin[b % 2][:]).then_inc(stored[b % 2], 16)
            for p in range(2):
                sp.wait_ge(stored[p], 16 * B // 2)

        @block.gpsimd
        def _(pool):
            def gather(b, p):
                pool.wait_ge(gathered[p], 16 * T * K // 2 * (b - p))
                pool.wait_ge(x2_ready, T * (max(b - 1, 0) if isinstance(b, int) else b - 1))
                nc.gpsimd.tensor_copy(index_now[p][:], row_index[:, bass.ds(T * b, T), :]).then_inc(index_copied, 1)
                pool.wait_ge(index_copied, b + 1)
                pool.sem_inc(index_seen, 1)
                for t in range(T):
                    for k in range(K):
                        nc.gpsimd.indirect_dma_start(
                            out=rows[p][:, t, k, :], out_offset=None, in_=scratch_oe,
                            in_offset=bass.IndirectOffsetOnAxis(ap=index_now[p][:, t, k:k + 1], axis=0)).then_inc(gathered[p], 16)

            def rstds(b, late):
                pool.wait_ge((f_moments, l_moments)[late], T * (b + 1))
                nc.gpsimd.tensor_tensor(var_eps[:, late, :], moments[:, late, :, 1], eps[:, 0:T], ALU.add).then_inc((own_pool, own_pool_late)[late], 1)
                pool.wait_ge((own_pool, own_pool_late)[late], b + 1)
                nc.gpsimd.tensor_tensor(rstd[:, late, :], var_eps[:, late, :], neg_half[:, 0:T], ALU.pow).then_inc((f_rstd, l_rstd)[late], 1)

            gather(0, 0)
            gather(1, 1)
            rstds(0, 0)
            rstds(1, 0)
            gather(2, 0)
            with pool.Fori(0, B // 2 - 2) as i:
                for p in (1, 0):
                    b = 2 * i + 2 - p
                    rstds(b - 1, 1)
                    rstds(b + 1, 0)
                    gather(b + 2, p)
            rstds(B - 4, 1)
            rstds(B - 2, 0)
            gather(B - 1, 1)
            rstds(B - 3, 1)
            rstds(B - 1, 0)
            rstds(B - 2, 1)
            rstds(B - 1, 1)

        @block.vector
        def _(dve):
            of = Ordered(dve, own_front, K * T + T)
            ol = Ordered(dve, own_late, T)

            def front(b, p, step=None):
                if step in (None, 0):
                    of.start(b)
                    nc.vector.tensor_copy(weight_now[:], row_weight[:, bass.ds(T * b, T), :]).then_inc(weight_copied, 1)
                    dve.wait_ge(gathered[p], 16 * T * K // 2 * (b - p) + 16 * T * K)
                    dve.wait_ge(weight_copied, b + 1)
                for k in range(K):
                    if step in (None, k // 2):
                        if k:
                            of.wait()
                        for t in range(T):
                            other = acc[:, t, :] if k else z_all[:, bass.ds(T * b + t, 1), :].rearrange("p t d -> p (t d)")
                            of.done(nc.vector.scalar_tensor_tensor(out=acc[:, t, :], in0=rows[p][:, t, k, :], scalar=weight_now[:, t, k:k + 1],
                                                                   in1=other, op0=ALU.mult, op1=ALU.add))
                if step in (None, 2):
                    of.wait()
                    for t in range(T):
                        nc.vector.scalar_tensor_tensor(out=x2[:, t, :], in0=acc[:, t, :], scalar=tgates[:, 2:3],
                                                       in1=x_all[:, bass.ds(T * b + t, 1), :].rearrange("p t d -> p (t d)"),
                                                       op0=ALU.mult, op1=ALU.add).then_inc(x2_ready, 1)
                    dve.wait_ge(x2_ready, T * (b + 1))
                    nc.vector.tensor_tensor(xb[p][:], x2[:], bo_g[:].unsqueeze(1).to_broadcast([P, T, D]), ALU.add).then_inc(xb_ready, 1)
                    for t in range(T):
                        of.done(nc.vector.bn_stats(stats[:, 0, t, :], x2[:, t, :]))
                if step in (None, 3):
                    of.wait()
                    dve.sem_inc(stats_seen, 1)
                    for t in range(T):
                        nc.vector.bn_aggr(moments[:, 0, t, :], stats[:, 0, t, :]).then_inc(f_moments, 1)
                if step in (None, 4):
                    dve.wait_ge(f_rstd, b + 1)
                    if step is not None:
                        dve.wait_ge(front_ready, FR * (b - 1) + 2)
                    for t in range(T):
                        nc.vector.tensor_scalar(xn[:, t, :], x2[:, t, :], moments[:, 0, t, 0:1], rstd[:, 0, t:t + 1],
                                                ALU.subtract, ALU.mult).then_inc(xn_ready, 1)

            def late(b, p, step=None):
                if step in (None, 0):
                    ol.start(b)
                    dve.wait_ge(x3_ready, T * (b + 1))
                    for t in range(T):
                        ol.done(nc.vector.bn_stats(stats[:, 1, t, :], x3[p][:, t, :]))
                if step in (None, 1):
                    ol.wait()
                    dve.sem_inc(stats_seen, 1)
                    for t in range(T):
                        nc.vector.bn_aggr(moments[:, 1, t, :], stats[:, 1, t, :]).then_inc(l_moments, 1)
                if step in (None, 2):
                    dve.wait_ge(l_rstd, b + 1)
                    dve.wait_ge(x3_turned, b)
                    for t in range(T):
                        nc.vector.tensor_scalar(x3n[:, t, :], x3[p][:, t, :], moments[:, 1, t, 0:1], rstd[:, 1, t:t + 1],
                                                ALU.subtract, ALU.mult).then_inc(x3n_ready, 1)
                if step in (None, 3):
                    dve.wait_ge(f_ready, b + 1)
                    dve.wait_ge(stored[p], 8 * (b - p))
                    for t in range(T):
                        nc.vector.scalar_tensor_tensor(out=fin[p][:, t, :], in0=ps_work[:, 1, t * D:(t + 1) * D], scalar=tgates[:, 3:4],
                                                       in1=x3[p][:, t, :], op0=ALU.mult, op1=ALU.add).then_inc(fin_ready, 1)

            def take_values(b, p):
                dve.wait_ge(v_ready, b + 1)
                nc.vector.tensor_tensor(v[p][:], ps_work[:, 0, :].rearrange("p (t d) -> p t d", t=T),
                                        bv_row[:].unsqueeze(1).to_broadcast([P, T, D]), ALU.add).then_inc(v_out, 1)

            def bias(b, h):
                dve.wait_ge(probs_ready, T * (H * b + max(h - 1, 0)))
                dve.wait_ge(scores_ready, H * b + h + 1)
                dve.sem_inc(scores_seen, 1)
                for t in range(T):
                    nc.vector.tensor_tensor_reduce(s_neg[:, h % 2, t, :], ps_scores[:, h % 2, t, :], rel_bias[:, h, (1 - t) * P:(1 - t) * P + S],
                                                   1.0, 3.0e38, ALU.add, ALU.min, max_neg[:, h % 2, t:t + 1]).then_inc(biased, 1)

            def take_turned(b, h):
                dve.wait_ge(turned, H * b + h + 1)
                dve.wait_ge(pv_ready, H * b + max(h - 1, 0))
                nc.vector.tensor_copy(pT[:, h % 2], ps_turn[:, h % 2]).then_inc(pT_ready, 1)

            def slot(b, p, more, behind):
                for h in range(H):
                    bias(b, h)
                    if h >= 1:
                        take_turned(b, h - 1)
                    if behind and h in LATE_AT:
                        late(b - 1, 1 - p, LATE_AT.index(h))
                    if more and h in FRONT_AT:
                        front(b + 1, 1 - p, FRONT_AT.index(h))
                take_turned(b, H - 1)
                dve.wait_ge(probs_ready, T * H * (b + 1))
                nc.vector.reciprocal(rinv[:], rsum[:]).then_inc(rinv_ready, 1)
                dve.wait_ge(rinv_ready, b + 1)
                dve.wait_ge(pv_ready, H * (b + 1))
                nc.vector.tensor_tensor(o_rows[:].rearrange("p t (h d) -> p t h d", d=DK), ps_o[:],
                                        rinv[:].rearrange("p h t -> p t h").unsqueeze(3).to_broadcast([P, T, H, DK]),
                                        ALU.mult).then_inc(o_ready, 1)
                if more:
                    take_values(b + 1, 1 - p)
                dve.wait_ge(y_ready, b + 1)
                dve.wait_ge(xb_ready, b + 1)
                for t in range(T):
                    nc.vector.scalar_tensor_tensor(out=x3[p][:, t, :], in0=ps_work[:, 0, t * D:(t + 1) * D], scalar=tgates[:, 1:2],
                                                   in1=xb[p][:, t, :], op0=ALU.mult, op1=ALU.add).then_inc(x3_ready, 1)

            nc.vector.memset(bqk[:], 0.0).then_inc(b_zero, 1)
            nc.vector.memset(wq[:], 0.0).then_inc(w_zero, 1)
            nc.vector.memset(wk[:], 0.0).then_inc(w_zero, 1)
            dve.wait_ge(w_zero, 2)
            dve.wait_ge(w_loaded, 16 * 7)
            for s, d in ((wq_rows, wq), (wk_rows, wk)):
                for c in range(C):
                    nc.vector.tensor_copy(d[:, c, :, 0:DK], s[:, c, :].rearrange("p (h i) -> p h i", i=DK)).then_inc(w_ready, 1)
            nc.vector.tensor_scalar(sw_pos[:], sw_rows[:], 0.0, None, ALU.is_gt).then_inc(sign_parts, 1)
            nc.vector.tensor_scalar(sw_neg[:], sw_rows[:], 0.0, None, ALU.is_lt).then_inc(sign_parts, 1)
            nc.vector.tensor_scalar(bo_g[:], bo_row[:], tgates[:, 1:2], None, ALU.mult).then_inc(bo_ready, 1)
            dve.wait_ge(sign_parts, 2)
            nc.vector.tensor_tensor(sw_sign[:], sw_pos[:], sw_neg[:], ALU.subtract).then_inc(sign_ready, 1)
            dve.wait_ge(bo_ready, 1)
            front(0, 0)
            take_values(0, 0)
            slots(dve, slot)
            late(B - 1, 1)

        @block.scalar
        def _(act):
            def front(b, p):
                for n in range(FR):
                    act.wait_ge(front_ready, FR * b + n + 1)
                    bank = ps_work[:, n % 2, :]
                    if n < 2:
                        ins = nc.scalar.copy((ctxT, xnT)[n][:].rearrange("p c s -> p (c s)"), bank)
                    else:
                        for k in range(2):
                            g = 2 * (n % 2) + k
                            src = bank[:, k * S:(k + 1) * S]
                            if n < 4:
                                ins = nc.scalar.activation(qT[p][:, g, :], src, ACT.Identity, bias=bq_neg[:, g:g + 1], scale=-SCALE1)
                            else:
                                ins = nc.scalar.activation(kT[p][:, g, :], src, ACT.Identity, bias=bqk[:, 1, g:g + 1], scale=1.0)
                    ins.then_inc(front_out, 1)

            def slot(b, p, more, behind):
                for h in range(H):
                    if h == 0:
                        act.wait_ge(rinv_ready, b)
                    act.wait_ge(biased, T * (H * b + h + 1))
                    act.wait_ge(turned, H * b + max(h - 1, 0))
                    for t in range(T):
                        nc.scalar.activation(probs[:, h % 2, t, :], s_neg[:, h % 2, t, :], ACT.Exp, bias=max_neg[:, h % 2, t:t + 1],
                                             scale=-1.0, accum_out=rsum[:, h, t:t + 1]).then_inc(probs_ready, 1)
                    if behind and h == LATE_TURN:
                        take_x3(b - 1)
                if more:
                    front(b + 1, 1 - p)
                act.wait_ge(oT_turned, b + 1)
                nc.scalar.copy(oT[:].rearrange("p c s -> p (c s)"), ps_work[:, 1, :]).then_inc(oT_out, 1)

            def take_x3(b):
                act.wait_ge(x3_turned, b + 1)
                nc.scalar.copy(x3T[:].rearrange("p c s -> p (c s)"), ps_work[:, 0, :]).then_inc(x3T_out, 1)

            act.wait_ge(sign_turned, 1)
            nc.scalar.copy(swT[:].rearrange("p c s -> p (c s)"), ps_work[:, 0, :]).then_inc(swT_ready, 1)
            act.wait_ge(b_loaded, 16 * 2 * HG)
            nc.scalar.activation(bq_neg[:], bqk[:, 0, :], ACT.Copy, scale=-SCALE1).then_inc(bq_ready, 1)
            act.wait_ge(bq_ready, 1)
            front(0, 0)
            slots(act, slot)
            take_x3(B - 1)

        @block.tensor
        def _(pe):
            def turn(bank, src):
                for c in range(C):
                    for t in range(T):
                        ins = nc.tensor.transpose(ps_work[:, bank, c * S + t * P:c * S + (t + 1) * P], src[:, t, c * P:(c + 1) * P], ident[:])
                return ins

            def project(bank, srcT, w):
                for t in range(T):
                    for c in range(C):
                        ins = nc.tensor.matmul(ps_work[:, bank, t * D:(t + 1) * D], srcT[:, c, t * P:(t + 1) * P], w[:, c, :],
                                               start=(c == 0), stop=(c == C - 1))
                return ins

            def front(b, p):
                first = isinstance(b, int) and b == 0
                if first:
                    pe.wait_ge(swT_ready, 1)
                else:
                    pe.wait_ge(x3T_out, b - 1)
                    pe.wait_ge(v_out, b)
                pe.wait_ge(ctx_loaded[p], 8 * (b - p) + 16)
                turn(0, cin[p]).then_inc(front_ready, 1)
                if not first:
                    pe.wait_ge(fin_ready, T * (b - 1))
                    pe.wait_ge(front_out, FR * b)
                pe.wait_ge(xn_ready, T * (b + 1))
                turn(1, xn).then_inc(front_ready, 1)
                for n in range(2, FR):
                    pe.wait_ge(front_out, FR * b + max(n - 1, 2))
                    w, src = ((wq, xnT), (wk, ctxT))[n // 4]
                    for k in range(2):
                        g = 2 * (n % 2) + k
                        for c in range(C):
                            ins = nc.tensor.matmul(ps_work[:, n % 2, k * S:(k + 1) * S], w[:, c, g * HG:(g + 1) * HG, :].rearrange("p h i -> p (h i)"),
                                                   src[:, c, :], start=(c == 0), stop=(c == C - 1))
                    ins.then_inc(front_ready, 1)
                pe.wait_ge(front_out, FR * b + FR - 1)
                project(0, ctxT, wv).then_inc(v_ready, 1)

            def scores(b, p, h):
                g, j = divmod(h, HG)
                pe.wait_ge(biased, T * (H * b + max(h - 1, 0)))
                for t in range(T):
                    ins = nc.tensor.matmul(ps_scores[:, h % 2, t, :], qT[p][32 * j:32 * j + DK, g, t * P:(t + 1) * P],
                                           kT[p][32 * j:32 * j + DK, g, :], start=True, stop=True)
                ins.then_inc(scores_ready, 1)

            def turn_probs(b, h):
                pe.wait_ge(probs_ready, T * (H * b + h + 1))
                pe.wait_ge(pT_ready, H * b + max(h - 1, 0))
                for tk in range(T):
                    for tq in range(T):
                        ins = nc.tensor.transpose(ps_turn[:, h % 2, tk, tq * P:(tq + 1) * P], probs[:, h % 2, tq, tk * P:(tk + 1) * P], ident[:])
                ins.then_inc(turned, 1)

            def values(b, p, h):
                pe.wait_ge(pT_ready, H * b + h + 1)
                if h == 0:
                    pe.wait_ge(o_ready, b)
                for tq in range(T):
                    for tk in range(T):
                        ins = nc.tensor.matmul(ps_o[:, tq, h, :], pT[:, h % 2, tk, tq * P:(tq + 1) * P], v[p][:, tk, h * DK:(h + 1) * DK],
                                               start=(tk == 0), stop=(tk == T - 1))
                ins.then_inc(pv_ready, 1)

            def turn_x3(b):
                pe.wait_ge(x3n_ready, T * (b + 1))
                pe.wait_ge(x3_ready, T * (b + 1))
                turn(0, x3n).then_inc(x3_turned, 1)

            def feed_forward(b):
                pe.wait_ge(x3T_out, b + 1)
                pe.wait_ge(oT_out, b + 1)
                project(1, x3T, swT).then_inc(f_ready, 1)

            def slot(b, p, more, behind):
                pe.wait_ge(front_out, FR * (b + 1))
                pe.wait_ge(v_out, b + 1)
                scores(b, p, 0)
                scores(b, p, 1)
                for h in range(H):
                    turn_probs(b, h)
                    if h + 2 < H:
                        scores(b, p, h + 2)
                    if h:
                        values(b, p, h - 1)
                    if behind and h == LATE_TURN:
                        turn_x3(b - 1)
                    if behind and h == LATE_TURN + 2:
                        feed_forward(b - 1)
                values(b, p, H - 1)
                if more:
                    front(b + 1, 1 - p)
                pe.wait_ge(front_out, FR * (b + 2) if more else FR * (b + 1))
                pe.wait_ge(o_ready, b + 1)
                if not more:
                    pe.wait_ge(fin_ready, T * b)
                turn(1, o_rows).then_inc(oT_turned, 1)
                pe.wait_ge(oT_out, b + 1)
                if more:
                    pe.wait_ge(v_out, b + 2)
                else:
                    pe.wait_ge(x3T_out, b)
                project(0, oT, wo).then_inc(y_ready, 1)

            pe.wait_ge(sign_ready, 1)
            turn(0, sw_sign).then_inc(sign_turned, 1)
            pe.wait_ge(w_ready, 2 * C)
            front(0, 0)
            slots(pe, slot)
            turn_x3(B - 1)
            feed_forward(B - 1)


_INS = ["x", "ctx_1024", "g_xattn", "g_ffn", "L0_xattn_ln_l_w", "L0_xattn_ln_l_b", "L0_xattn_ln_c_w", "L0_xattn_ln_c_b",
        "L0_xattn_Wq", "L0_xattn_Wkv", "L0_xattn_Wo", "L0_xattn_bo", "L0_ffn_wg", "L0_ffn_w1", "L0_ffn_w2", "L0_ffn_w3",
        "L0_ffn_sw1", "L0_ffn_sw2", "L0_ffn_sw3", "L1_xattn_Wq", "L1_xattn_bq", "L1_xattn_Wk", "L1_xattn_bk",
        "L1_xattn_Wv", "L1_xattn_bv", "L1_xattn_Wo", "L1_xattn_bo", "L1_xattn_rel", "L1_ffn_weight"]


def kernel(**inputs):
    import numpy as np
    import concourse.bacc as bacc
    from concourse.bass_utils import run_bass_kernel_spmd

    nc = bacc.Bacc("TRN2", target_bir_lowering=False, num_devices=1)
    arrays, args = {}, []
    for name in _INS:
        a = np.ascontiguousarray(inputs[name])
        arrays[f"in_{name}"] = a
        args.append(nc.dram_tensor(f"in_{name}", a.shape, mybir.dt.from_np(a.dtype), kind="ExternalInput").ap())
    shape = inputs["x"].shape
    args.append(nc.dram_tensor("out", shape, F32, kind="ExternalOutput").ap())
    flamingo_kernel(nc, *args)
    r = run_bass_kernel_spmd(nc, [arrays], core_ids=[0])
    return r.results[0]["out"]
```

```python
from contextlib import ExitStack

import concourse.bass as bass
from concourse import mybir

P = 128
ALU = mybir.AluOpType
ACT = mybir.ActivationFunctionType
F32 = mybir.dt.float32
F32R = mybir.dt.float32r
U32 = mybir.dt.uint32
AX = mybir.AxisListType

EPS = 1e-5
CLIP = 11.0


def flamingo_kernel(
    nc: bass.Bass,
    x, ctx_in, g_xattn, g_ffn,
    ln_l_w, ln_l_b, ln_c_w, ln_c_b, Wq, Wkv, Wo, bo,
    wg, w1, w2, w3, sw1, sw2, sw3,
    Wq1, bq1, Wk1, bk1, Wv1, bv1, Wo1, bo1, rel, sign_w,
    out,
):
    B, S, D = x.shape
    INNER = Wq.shape[1]
    H0, D0 = 16, INNER // 16
    PAIRS = H0 // 2
    E, F = wg.shape[0], w1.shape[2]
    K, G, LG = 4, 8, 4
    N = B * S
    NT = N // P
    T = S // P
    C = D // P
    CAP = int(1.25 * N * K / E)
    H1 = rel.shape[0]
    DK = D // H1
    WIDTH = rel.shape[1] - 1
    GR = H1 // 4
    SCALE1 = DK ** -0.5
    assert (T, C, NT, CAP) == (2, 2, 16, 320)

    stack = ExitStack()
    scratch_rel = nc.dram_tensor("scratch_rel", [H1, P, 4 * P - 1], F32, kind="Internal").ap()
    scratch_xe = nc.dram_tensor("scratch_xe", [E * CAP, D], F32, kind="Internal").ap()
    scratch_oe = nc.dram_tensor("scratch_oe", [E * CAP, D], F32, kind="Internal").ap()

    with stack as keep:
        def alloc(where):
            def sb(name, shape, dt=F32):
                return where.enter_context(nc.sbuf_tensor(name, shape, dt))
            return sb

        sb = alloc(keep)
        ident = sb("ident", [P, P])
        x_all = sb("x_all", [P, NT, D])
        gates = sb("gates", [P, 4])
        tgates = sb("tgates", [P, 4])
        neg_half = sb("neg_half", [P, NT])
        eps = sb("eps", [P, NT])
        row_index = sb("row_index", [P, NT, K], U32)
        row_weight = sb("row_weight", [P, NT, K])

        xattn0(nc, keep, locals())
        w2l1 = {n: [sb(f"l1_{n}_{part}", [P, C, D], F32R) for part in ("hi", "lo")] for n in ("wq", "wk", "wv", "wo")}
        swT = sb("swT", [P, C, D], F32R)
        sel = {n: [sb(f"sel{n}_{part}", [P, 4, 2, 4, DK], F32R) for part in ("hi", "lo")] for n in ("q", "k")}
        join = sb("join", [P, P // 32, DK])
        b_cols = sb("b_cols", [P, 2, C])
        b_neg = sb("b_neg", [P, C])
        bv_row = sb("bv_row", [P, D])
        bo1_g = sb("bo1_g", [P, D])
        rel_bias = sb("rel_bias", [P, H1, 3 * P])
        moe(nc, keep, locals())
        xattn1(nc, keep, locals())


def make_tools(nc, phase, name):
    def sb(n, shape, dt=F32):
        return phase.enter_context(nc.sbuf_tensor(f"{name}_{n}", shape, dt))

    def ps(n, shape, dt=F32):
        return phase.enter_context(nc.psum_tensor(f"{name}_{n}", shape, dt))

    def sem(n):
        return phase.enter_context(nc.semaphore(f"{name}_{n}"))

    return sb, ps, sem


class Ordered:

    def __init__(self, engine, sem, per_round):
        self.engine, self.sem, self.per_round = engine, sem, per_round
        self.base, self.count = 0, 0

    def start(self, rnd):
        assert self.count in (0, self.per_round)
        self.base, self.count = rnd * self.per_round, 0

    def done(self, instruction):
        self.count += 1
        instruction.then_inc(self.sem, 1)

    def wait(self):
        self.engine.wait_ge(self.sem, self.base + self.count)


def xattn0(nc, keep, env):
    x, ctx_in, g_xattn, g_ffn = env["x"], env["ctx_in"], env["g_xattn"], env["g_ffn"]
    ln_l_w, ln_l_b, ln_c_w, ln_c_b = env["ln_l_w"], env["ln_l_b"], env["ln_c_w"], env["ln_c_b"]
    Wq, Wkv, Wo, bo, rel = env["Wq"], env["Wkv"], env["Wo"], env["bo"], env["rel"]
    ident, x_all, gates, tgates, neg_half = env["ident"], env["x_all"], env["gates"], env["tgates"], env["neg_half"]
    eps = env["eps"]
    scratch_rel, scratch_xe = env["scratch_rel"], env["scratch_xe"]
    B, D, INNER, T, C, PAIRS, D0, H0 = (env[k] for k in ("B", "D", "INNER", "T", "C", "PAIRS", "D0", "H0"))
    H1, WIDTH, E, CAP = (env[k] for k in ("H1", "WIDTH", "E", "CAP"))
    S = T * P
    SC = D0 ** -0.5

    with ExitStack() as phase:
        sb, ps, sem = make_tools(nc, phase, "a")
        ps_scores = ps("scores", [P, 2, 2, T, S])
        ps_pv = ps("pv", [P, 2, 512])
        ps_work = ps("work", [P, 2, 512])

        wq = sb("wq", [P, C, INNER])
        wkv = sb("wkv", [P, C, 2 * INNER])
        wo = sb("wo", [P, PAIRS, D])
        affine = sb("affine", [P, 4, C])
        bo_row = sb("bo_row", [P, D])
        bo_g = sb("bo_g", [P, D])
        xin = [sb(f"xin{i}", [P, T, D]) for i in range(2)]
        cin = [sb(f"cin{i}", [P, T, D]) for i in range(2)]
        stats = sb("stats", [P, 3 * T, 6])
        moments = sb("moments", [P, 3 * T, 2])
        var_eps = sb("var_eps", [P, 3 * T])
        rstd = sb("rstd", [P, 3 * T])
        xn = sb("xn", [P, T, D])
        lat = sb("lat", [P, T, D])
        cn = sb("cn", [P, T, D])
        latT = sb("latT", [P, C, S])
        ctxT = sb("ctxT", [P, C, S])
        qT = [sb(f"qT{i}", [P, PAIRS, S]) for i in range(2)]
        kT = [sb(f"kT{i}", [P, PAIRS, S]) for i in range(2)]
        v_aug = [sb(f"v{i}", [P, T, H0, D0 + 1]) for i in range(2)]
        clipped = sb("clipped", [P, 2, 2, T, S])
        probs = sb("probs", [P, 2, 2, T, S])
        rsum = sb("rsum", [P, 2, 2, 2])
        o_rows = sb("o_rows", [P, T, INNER])
        oT = sb("oT", [P, PAIRS, S])
        relpad = sb("relpad", [H1, 4 * P - 1])
        rel_in = sb("rel_in", [H1, WIDTH + 1])
        xb = [sb(f"xb{i}", [P, T, D]) for i in range(2)]
        ZR = 8
        ZERO_DMAS = E * CAP // (P * ZR)
        zeros = sb("zeros", [P, ZR * D])

        weights_loaded = sem("weights_loaded")
        params_loaded = sem("params_loaded")
        inputs_loaded = [sem(f"inputs_loaded{i}") for i in range(2)]
        rel_loaded = sem("rel_loaded")
        rel_stored = sem("rel_stored")
        zeroed = sem("zeroed")
        ident_ready = sem("ident_ready")
        ones_ready = sem("ones_ready")
        consts_ready = sem("consts_ready")
        relpad_zero = sem("relpad_zero")
        relpad_ready = sem("relpad_ready")
        xb_ready = sem("xb_ready")
        gates_ready = sem("gates_ready")
        bo_ready = sem("bo_ready")
        dve_steps = sem("dve_steps")
        moments_ready = sem("moments_ready")
        pool_steps = sem("pool_steps")
        rstd_ready = sem("rstd_ready")
        lat_ready = sem("lat_ready")
        front_ready = sem("front_ready")
        front_out = sem("front_out")
        scores_ready = sem("scores_ready")
        clip_ready = sem("clip_ready")
        probs_ready = sem("probs_ready")
        pv_ready = sem("pv_ready")
        rsum_ready = sem("rsum_ready")
        o_ready = sem("o_ready")
        oT_ready = sem("oT_ready")
        oT_out = sem("oT_out")
        y_ready = sem("y_ready")
        x_updated = sem("x_updated")

        FRONT = 14
        x_rows = x.rearrange("b (t p) d -> b p t d", p=P)
        c_rows = ctx_in.rearrange("b (t p) d -> b p t d", p=P)

        def batches(eng, front, attend):
            front(0, 0)
            with eng.Fori(0, B // 2 - 1) as i:
                attend(2 * i, 0, True)
                attend(2 * i + 1, 1, True)
            attend(B - 2, 0, True)
            attend(B - 1, 1, False)

        block = phase.enter_context(nc.Block())

        @block.sync
        def _(sp):
            def load(b, p):
                sp.dma_start(xin[p][:], x_rows[bass.ds(b, 1)].rearrange("b p t d -> p (b t) d")).then_inc(inputs_loaded[p], 16)
                sp.dma_start(cin[p][:], c_rows[bass.ds(b, 1)].rearrange("b p t d -> p (b t) d")).then_inc(inputs_loaded[p], 16)

            load(0, 0)
            for i, v in enumerate((ln_l_w, ln_l_b, ln_c_w, ln_c_b)):
                sp.dma_start(affine[:, i, :], v.rearrange("(c p) -> p c", p=P), allow_slow_non_contiguous=True).then_inc(params_loaded, 16)
            sp.dma_start(bo_row[:], bo.partition_broadcast(P)).then_inc(params_loaded, 16)
            for i, v in enumerate((g_xattn, g_ffn)):
                sp.dma_start(gates[:, 2 * i:2 * i + 2], v.partition_broadcast(P)).then_inc(params_loaded, 16)
            sp.dma_start(wq[:], Wq.rearrange("(c p) n -> p c n", p=P)).then_inc(weights_loaded, 16)
            sp.dma_start(wkv[:], Wkv.rearrange("(c p) n -> p c n", p=P)).then_inc(weights_loaded, 16)
            load(1, 1)
            sp.dma_start(wo[:], Wo.rearrange("(j p) n -> p j n", p=P)).then_inc(weights_loaded, 16)
            sp.dma_start(rel_in[:], rel).then_inc(rel_loaded, 16)
            sp.wait_ge(relpad_ready, 1)
            sp.dma_start(scratch_rel, relpad[:].unsqueeze(1).to_broadcast([H1, P, 4 * P - 1])).then_inc(rel_stored, 16)
            sp.wait_ge(rel_stored, 16)
            sp.wait_ge(consts_ready, 3)
            for j in range(ZERO_DMAS):
                rows = scratch_xe[j * P * ZR:(j + 1) * P * ZR, :]
                sp.dma_start(rows.rearrange("(p r) d -> p (r d)", p=P), zeros[:]).then_inc(zeroed, 16)
            with sp.Fori(1, B // 2) as i:
                for p in range(2):
                    sp.wait_ge(x_updated, (2 * i - 1 + p) * T)
                    load(2 * i + p, p)
            sp.wait_ge(zeroed, 16 * ZERO_DMAS)

        @block.gpsimd
        def _(pool):
            nc.gpsimd.memset(ident[:], 0.0).then_inc(consts_ready, 1)
            nc.gpsimd.memset(neg_half[:], -0.5).then_inc(consts_ready, 1)
            nc.gpsimd.memset(zeros[:], 0.0).then_inc(consts_ready, 1)
            nc.gpsimd.memset(eps[:], EPS).then_inc(consts_ready, 1)
            pool.wait_ge(consts_ready, 4)
            nc.gpsimd.affine_select(out=ident[:], in_=ident[:], compare_op=ALU.not_equal, fill=1.0, base=0,
                                    pattern=[[-1, P]], channel_multiplier=1).then_inc(ident_ready, 1)
            for i in range(2):
                nc.gpsimd.memset(v_aug[i][:, :, :, D0:D0 + 1], 1.0).then_inc(ones_ready, 1)
            own = Ordered(pool, pool_steps, 2)

            with pool.Fori(0, B) as b:
                own.start(b)
                for lo, hi in ((0, 2 * T), (2 * T, 3 * T)):
                    pool.wait_ge(moments_ready, 3 * T * b + hi)
                    own.done(nc.gpsimd.tensor_tensor(var_eps[:, lo:hi], moments[:, lo:hi, 1], eps[:, lo:hi], ALU.add))
                    own.wait()
                    nc.gpsimd.tensor_tensor(rstd[:, lo:hi], var_eps[:, lo:hi], neg_half[:, lo:hi], ALU.pow).then_inc(rstd_ready, 1)

        @block.vector
        def _(dve):
            own = Ordered(dve, dve_steps, 4 * T)

            def front(b, p, step=None):
                if step in (None, 0):
                    own.start(b)
                    dve.wait_ge(inputs_loaded[p], 16 * (b - p) + 32)
                    for n in range(2 * T):
                        own.done(nc.vector.bn_stats(stats[:, n, :], (xin[p], cin[p])[n // T][:, n % T, :]))
                    own.wait()
                    nc.vector.tensor_tensor(xb[p][:], xin[p][:], bo_g[:].unsqueeze(1).to_broadcast([P, T, D]), ALU.add).then_inc(xb_ready, 1)
                    for n in range(2 * T):
                        nc.vector.bn_aggr(moments[:, n, :], stats[:, n, :]).then_inc(moments_ready, 1)
                if step in (None, 1):
                    dve.wait_ge(rstd_ready, 2 * b + 1)
                    if step is not None:
                        dve.wait_ge(front_ready, FRONT * (b - 1) + 2)
                    for t in range(T):
                        own.done(nc.vector.tensor_scalar(xn[:, t, :], xin[p][:, t, :], moments[:, t, 0:1], rstd[:, t:t + 1],
                                                         ALU.subtract, ALU.mult))
                if step in (None, 2):
                    own.wait()
                    for t in range(T):
                        own.done(nc.vector.bn_stats(stats[:, 2 * T + t, :], xn[:, t, :]))
                    own.wait()
                    for t in range(T):
                        nc.vector.tensor_scalar(cn[:, t, :], cin[p][:, t, :], moments[:, T + t, 0:1], rstd[:, T + t:T + t + 1],
                                                ALU.subtract, ALU.mult).then_inc(lat_ready, 1)
                    for t in range(T):
                        nc.vector.bn_aggr(moments[:, 2 * T + t, :], stats[:, 2 * T + t, :]).then_inc(moments_ready, 1)
                if step in (None, 3):
                    dve.wait_ge(rstd_ready, 2 * b + 2)
                    for t in range(T):
                        m = 2 * T + t
                        nc.vector.tensor_scalar(lat[:, t, :], xn[:, t, :], moments[:, m, 0:1], rstd[:, m:m + 1],
                                                ALU.subtract, ALU.mult).then_inc(lat_ready, 1)

            def clip(b, j):
                dve.wait_ge(scores_ready, PAIRS * b + j + 1)
                dve.wait_ge(probs_ready, PAIRS * b + max(j - 1, 0))
                nc.vector.tensor_scalar(clipped[:, j % 2], ps_scores[:, j % 2], CLIP / SC, -CLIP / SC,
                                        ALU.min, ALU.max).then_inc(clip_ready, 1)

            def normalise(b, j):
                dve.wait_ge(pv_ready, PAIRS * b + j + 1)
                if j == 0:
                    dve.wait_ge(oT_ready, 4 * b)
                pv = ps_pv[:, j % 2, 0:T * 2 * (D0 + 1)].rearrange("p (t h d) -> p t h d", t=T, h=2)
                nc.vector.reciprocal(rsum[:, j % 2], pv[:, :, :, D0]).then_inc(rsum_ready, 1)
                dve.wait_ge(rsum_ready, PAIRS * b + j + 1)
                nc.vector.tensor_tensor(o_rows[:, :, 2 * D0 * j:2 * D0 * (j + 1)].rearrange("p t (h d) -> p t h d", h=2),
                                        pv[:, :, :, 0:D0], rsum[:, j % 2].unsqueeze(3).to_broadcast([P, T, 2, D0]),
                                        ALU.mult).then_inc(o_ready, 1)

            def attend(b, p, more):
                for j in range(PAIRS):
                    clip(b, j)
                    if j >= 2:
                        normalise(b, j - 2)
                    if more and j >= 4:
                        front(b + 1, 1 - p, j - 4)
                for j in range(PAIRS - 2, PAIRS):
                    normalise(b, j)
                for t in range(T):
                    dve.wait_ge(y_ready, T * b + t + 1)
                    dve.wait_ge(xb_ready, b + 1)
                    nc.vector.scalar_tensor_tensor(x_all[:, bass.ds(T * b + t, 1), :].rearrange("p t d -> p (t d)"),
                                                   ps_work[:, t, 0:D], tgates[:, 0:1], xb[p][:, t, :],
                                                   ALU.mult, ALU.add).then_inc(x_updated, 1)

            dve.wait_ge(rel_loaded, 16)
            nc.vector.memset(relpad[:], 0.0).then_inc(relpad_zero, 1)
            dve.wait_ge(relpad_zero, 1)
            lead = P + P // 2 - 1
            nc.vector.tensor_scalar(relpad[:, lead:lead + WIDTH + 1], rel_in[:], -1.0, None, ALU.mult).then_inc(relpad_ready, 1)
            dve.wait_ge(gates_ready, 1)
            nc.vector.tensor_scalar(bo_g[:], bo_row[:], tgates[:, 0:1], None, ALU.mult).then_inc(bo_ready, 1)
            dve.wait_ge(bo_ready, 1)
            batches(dve, front, attend)

        @block.scalar
        def _(act):
            def front(b, p):
                for n in range(FRONT):
                    act.wait_ge(front_ready, FRONT * b + n + 1)
                    bank = ps_work[:, n % 2, :]
                    if n < 2:
                        for c in range(C):
                            ins = nc.scalar.activation((ctxT, latT)[n][:, c, :], bank[:, c * S:(c + 1) * S], ACT.Identity,
                                                       bias=affine[:, 3 - 2 * n, c:c + 1], scale=affine[:, 2 - 2 * n, c:c + 1])
                    elif n < 10:
                        dst = (qT, kT)[(n - 2) // 4][p]
                        m = 2 * ((n - 2) % 4)
                        ins = nc.scalar.copy(dst[:, m:m + 2, :].rearrange("p m s -> p (m s)"), bank[:])
                    else:
                        t, half = divmod(n - 10, 2)
                        hs = H0 // 2
                        ins = nc.scalar.copy(v_aug[p][:, t, half * hs:(half + 1) * hs, 0:D0],
                                             bank.rearrange("p (h d) -> p h d", d=D0))
                    ins.then_inc(front_out, 1)

            def attend(b, p, more):
                for j in range(PAIRS):
                    act.wait_ge(clip_ready, PAIRS * b + j + 1)
                    act.wait_ge(pv_ready, PAIRS * b + max(j - 1, 0))
                    nc.scalar.activation(probs[:, j % 2], clipped[:, j % 2], ACT.Exp, scale=SC).then_inc(probs_ready, 1)
                if more:
                    front(b + 1, 1 - p)
                for n in range(4):
                    act.wait_ge(oT_ready, 4 * b + n + 1)
                    nc.scalar.copy(oT[:, 2 * n:2 * n + 2, :].rearrange("p m s -> p (m s)"), ps_work[:, n % 2, :]).then_inc(oT_out, 1)

            act.wait_ge(params_loaded, 16 * 7)
            nc.scalar.activation(tgates[:], gates[:], ACT.Tanh).then_inc(gates_ready, 1)
            batches(act, front, attend)

        @block.tensor
        def _(pe):
            def front(b, p):
                for n in range(FRONT):
                    bank = ps_work[:, n % 2, :]
                    if n < 2:
                        if isinstance(b, int) and b == 0:
                            pe.wait_ge(ident_ready, 1)
                        else:
                            pe.wait_ge(front_out, FRONT * b)
                            pe.wait_ge(x_updated, T * (b - 1))
                        pe.wait_ge(lat_ready, 2 * T * b + (T, 2 * T)[n])
                        rows = (cn, lat)[n]
                        for c in range(C):
                            for t in range(T):
                                ins = nc.tensor.transpose(bank[:, c * S + t * P:c * S + (t + 1) * P],
                                                          rows[:, t, c * P:(c + 1) * P], ident[:])
                    elif n < 10:
                        pe.wait_ge(front_out, FRONT * b + max(n - 1, 2))
                        for k in range(2):
                            m = 2 * ((n - 2) % 4) + k
                            for c in range(C):
                                w = (wq, wkv)[(n - 2) // 4][:, c, m * P:(m + 1) * P]
                                ins = nc.tensor.matmul(bank[:, k * S:(k + 1) * S], w, (latT, ctxT)[(n - 2) // 4][:, c, :],
                                                       start=(c == 0), stop=(c == C - 1))
                    else:
                        pe.wait_ge(front_out, FRONT * b + n - 1)
                        t, half = divmod(n - 10, 2)
                        for c in range(C):
                            ins = nc.tensor.matmul(bank, ctxT[:, c, t * P:(t + 1) * P],
                                                   wkv[:, c, INNER + half * 512:INNER + (half + 1) * 512],
                                                   start=(c == 0), stop=(c == C - 1))
                    ins.then_inc(front_ready, 1)

            def scores(b, p, j):
                pe.wait_ge(clip_ready, PAIRS * b + max(j - 1, 0))
                for h in range(2):
                    rows = slice(h * D0, (h + 1) * D0)
                    for t in range(T):
                        ins = nc.tensor.matmul(ps_scores[:, j % 2, h, t, :], kT[p][rows, j, t * P:(t + 1) * P], qT[p][rows, j, :],
                                               start=True, stop=True)
                ins.then_inc(scores_ready, 1)

            def values(b, p, j):
                pe.wait_ge(probs_ready, PAIRS * b + j + 1)
                pe.wait_ge(o_ready, PAIRS * b + max(j - 1, 0))
                for tq in range(T):
                    for h in range(2):
                        at = (2 * tq + h) * (D0 + 1)
                        for t in range(T):
                            ins = nc.tensor.matmul(ps_pv[:, j % 2, at:at + D0 + 1], probs[:, j % 2, h, t, tq * P:(tq + 1) * P],
                                                   v_aug[p][:, t, 2 * j + h, :], start=(t == 0), stop=(t == T - 1))
                ins.then_inc(pv_ready, 1)

            def attend(b, p, more):
                pe.wait_ge(front_out, FRONT * b + FRONT)
                scores(b, p, 0)
                scores(b, p, 1)
                for j in range(PAIRS):
                    if j + 2 < PAIRS:
                        scores(b, p, j + 2)
                    values(b, p, j)
                if more:
                    front(b + 1, 1 - p)
                    pe.wait_ge(front_out, FRONT * b + 2 * FRONT)
                else:
                    pe.wait_ge(x_updated, T * b)
                pe.wait_ge(o_ready, PAIRS * b + PAIRS)
                for n in range(4):
                    if n >= 2:
                        pe.wait_ge(oT_out, 4 * b + n - 1)
                    for k in range(2):
                        m = 2 * n + k
                        for t in range(T):
                            ins = nc.tensor.transpose(ps_work[:, n % 2, k * S + t * P:k * S + (t + 1) * P],
                                                      o_rows[:, t, m * P:(m + 1) * P], ident[:])
                    ins.then_inc(oT_ready, 1)
                pe.wait_ge(oT_out, 4 * b + 4)
                for t in range(T):
                    for m in range(PAIRS):
                        ins = nc.tensor.matmul(ps_work[:, t, 0:D], oT[:, m, t * P:(t + 1) * P], wo[:, m, :],
                                               start=(m == 0), stop=(m == PAIRS - 1))
                    ins.then_inc(y_ready, 1)

            pe.wait_ge(weights_loaded, 48)
            pe.wait_ge(ones_ready, 2)
            batches(pe, front, attend)


def moe(nc, keep, env):
    wg, w1, w2, w3, sw1, sw2, sw3 = (env[k] for k in ("wg", "w1", "w2", "w3", "sw1", "sw2", "sw3"))
    x_all, ident, neg_half, eps, tgates = (env[k] for k in ("x_all", "ident", "neg_half", "eps", "tgates"))
    row_index, row_weight, scratch_xe, scratch_oe = (env[k] for k in ("row_index", "row_weight", "scratch_xe", "scratch_oe"))
    E, K, G, LG, CAP, NT, D, F, C = (env[k] for k in ("E", "K", "G", "LG", "CAP", "NT", "D", "F", "C"))
    Wq1, bq1, Wk1, bk1, Wv1, bv1, Wo1, bo1, sign_w = (env[k] for k in ("Wq1", "bq1", "Wk1", "bk1", "Wv1", "bv1", "Wo1", "bo1", "sign_w"))
    l1_w2, swT, sel, join, b_cols, b_neg, bv_row, bo1_g = (env[k] for k in ("w2l1", "swT", "sel", "join", "b_cols", "b_neg", "bv_row", "bo1_g"))
    DK, SCALE1, H1, rel_bias, scratch_rel = (env[k] for k in ("DK", "SCALE1", "H1", "rel_bias", "scratch_rel"))
    EG = E // G
    TG = 4
    NG = NT // TG
    GS = TG * P
    FC = F // P
    FAR = float(1 << 20)
    tails = ((0, 2, P), (2, 3, CAP - 2 * P))

    with ExitStack() as phase:
        sb, ps, sem = make_tools(nc, phase, "m")
        ps_turn = ps("turn", [P, C, 512])
        ps_h = ps("h", [P, 2, FC, 512])
        ps_out = ps("out", [P, 2, 512])

        xf = sb("xf", [P, NT, D])
        xfT = sb("xfT", [P, C, NT * P])
        wg_rows = sb("wg_rows", [E, D])
        wgT = sb("wgT", [P, C, E])
        s1 = sb("s1", [P, C, F])
        s3 = sb("s3", [P, C, F])
        s2 = sb("s2", [P, FC, D])
        stats = sb("stats", [P, NT, 6])
        moments = sb("moments", [P, NT, 2])
        var_eps = sb("var_eps", [P, NT])
        rstd = sb("rstd", [P, NT])
        count_e = sb("count_e", [P, E])
        before = sb("before", [P, P])
        ones = sb("ones", [P, P])
        neg_max = sb("neg_max", [P, NT])
        logits = sb("logits", [P, NT, E])
        exps = sb("exps", [P, NT, E])
        total = sb("total", [P, NT])
        rtotal = sb("rtotal", [P, NT])
        score = sb("score", [P, NT, E])
        gmax = sb("gmax", [P, NT, G])
        gtop = sb("gtop", [P, NT, 8])
        gidx = sb("gidx", [P, NT, 8], U32)
        gidx_f = sb("gidx_f", [P, NT, LG])
        ghot = sb("ghot", [P, NT, LG, G])
        gkeep = sb("gkeep", [P, NT, G])
        gpen = sb("gpen", [P, NT, G])
        masked = sb("masked", [P, NT, E])
        etop = sb("etop", [P, NT, 8])
        eidx = sb("eidx", [P, NT, 8], U32)
        eidx_f = sb("eidx_f", [P, NT, K])
        wsum = sb("wsum", [P, NT])
        rwsum = sb("rwsum", [P, NT])
        ehot = sb("ehot", [P, NT, K, E])
        epos = sb("epos", [P, NT, K, E])
        chosen = sb("chosen", [P, NT, E])
        earlier = sb("earlier", [P, NT, E])
        pos = sb("pos", [P, NT, K])
        fits = sb("fits", [P, NT, K])
        dest = sb("dest", [P, NT, K])
        kept = sb("kept", [P, NT, K])
        away = sb("away", [P, NT, K])
        send_index = sb("send_index", [P, NT, K], U32)
        act_t = sb("act_t", [P, FC, GS])
        act_a = sb("act_a", [P, FC, GS])
        gated = sb("gated", [P, FC, GS])
        w1s = [sb(f"w1_{i}", [P, C, F]) for i in range(2)]
        w3s = [sb(f"w3_{i}", [P, C, F]) for i in range(2)]
        w2s = [sb(f"l1_w2{i}", [P, FC, D]) for i in range(2)]
        xe = [sb(f"xe{i}", [P, 3, D]) for i in range(2)]
        xeT = [sb(f"xeT{i}", [P, C, CAP]) for i in range(2)]
        e_tanh = sb("e_tanh", [P, FC, CAP])
        e_a = sb("e_a", [P, FC, CAP])
        e_gated = [sb(f"e_gated{i}", [P, FC, CAP]) for i in range(2)]
        oe = [sb(f"oe{i}", [P, 3, D]) for i in range(2)]

        l1_rows = {n: sb(f"{n}_rows", [P, C, D]) for n in ("wq", "wk", "wv", "wo")}
        l1_rows["sw"] = e_a[:].rearrange("p c n -> p (c n)")[:, 0:C * D].rearrange("p (c d) -> p c d", d=D)
        sw_pos, sw_neg, sw_sign = (epos[:, 4 * n:4 * n + 4].rearrange("p t k e -> p (t k e)").rearrange("p (c d) -> p c d", d=D) for n in range(3))

        bo1_row = e_tanh[:].rearrange("p c n -> p (c n)")[:, 0:D]

        shared_loaded = sem("shared_loaded")
        l1_loaded = sem("l1_loaded")
        sel_zero = sem("sel_zero")
        bias_loaded = sem("bias_loaded")
        sel_ready = sem("sel_ready")
        wq_scaled = sem("wq_scaled")
        hi_ready = sem("hi_ready")
        lo_ready = sem("lo_ready")
        sign_parts = sem("sign_parts")
        sign_ready = sem("sign_ready")
        sign_turned = sem("sign_turned")
        swT_ready = sem("swT_ready")
        w13_loaded = [sem(f"w13_loaded{i}") for i in range(2)]
        l1_w2loaded = [sem(f"l1_w2loaded{i}") for i in range(2)]
        xe_loaded = [sem(f"xe_loaded{i}") for i in range(2)]
        stored = [sem(f"stored{i}") for i in range(2)]
        scattered = sem("scattered")
        tables_ready = sem("tables_ready")
        own_pool = sem("own_pool")
        own_dve = sem("own_dve")
        moments_ready = sem("moments_ready")
        rstd_ready = sem("rstd_ready")
        xf_ready = sem("xf_ready")
        turned = sem("turned")
        xfT_ready = sem("xfT_ready")
        wg_turned = sem("wg_turned")
        wgT_ready = sem("wgT_ready")
        logits_ready = sem("logits_ready")
        shifted_ready = sem("shifted_ready")
        exps_ready = sem("exps_ready")
        chosen_ready = sem("chosen_ready")
        pos_ready = sem("pos_ready")
        index_ready = sem("index_ready")
        sh_ready = sem("sh_ready")
        sh_tanh = sem("sh_tanh")
        sh_a = sem("sh_a")
        sh_gated = sem("sh_gated")
        z_ready = sem("z_ready")
        z_out = sem("z_out")
        e_turned = sem("e_turned")
        xeT_ready = sem("xeT_ready")
        h_ready = sem("h_ready")
        tanh_ready = sem("tanh_ready")
        a_ready = sem("a_ready")
        gated_ready = sem("gated_ready")
        o_ready = sem("o_ready")
        oe_ready = sem("oe_ready")

        block = phase.enter_context(nc.Block())

        @block.sync
        def _(sp):
            def load_w13(e, p):
                for w, s in ((w1, w1s), (w3, w3s)):
                    sp.dma_start(s[p][:], w[bass.ds(e, 1)].rearrange("e (c p) n -> p (e c) n", p=P)).then_inc(w13_loaded[p], 16)

            def load_w2(e, p):
                sp.dma_start(w2s[p][:], w2[bass.ds(e, 1)].rearrange("e (c p) n -> p (e c) n", p=P)).then_inc(l1_w2loaded[p], 16)

            def load_xe(e, p):
                for lo, hi, rows in tails:
                    src = scratch_xe[bass.ds(e * CAP + lo * P, (hi - lo) * rows)].rearrange("(c p) d -> p c d", p=rows)
                    sp.dma_start(xe[p][0:rows, lo:hi, :], src).then_inc(xe_loaded[p], 16)

            sp.dma_start(wg_rows[:], wg).then_inc(shared_loaded, 16)
            for w, s in ((sw1, s1), (sw3, s3), (sw2, s2)):
                sp.dma_start(s[:], w.rearrange("(c p) n -> p c n", p=P)).then_inc(shared_loaded, 16)
            load_w13(0, 0)
            load_w13(1, 1)
            load_w2(0, 0)
            for w, n in ((Wq1, "wq"), (Wk1, "wk"), (Wv1, "wv"), (Wo1, "wo"), (sign_w, "sw")):
                sp.dma_start(l1_rows[n][:], w.rearrange("(c p) n -> p c n", p=P)).then_inc(l1_loaded, 16)
            for r, d in ((bv1, bv_row[:]), (bo1, bo1_row)):
                sp.dma_start(d, r.partition_broadcast(P)).then_inc(l1_loaded, 16)
            for n, r in enumerate((bq1, bk1)):
                sp.dma_start(b_cols[:, n, :], r.rearrange("(c p) -> p c", p=P), allow_slow_non_contiguous=True).then_inc(l1_loaded, 16)
            sp.dma_start(rel_bias[:], bass.AP(scratch_rel.tensor, P - 1, [[4 * P - 2, P], [P * (4 * P - 1), H1], [1, 3 * P]])).then_inc(bias_loaded, 16)
            sp.wait_ge(bias_loaded, 16)
            sp.wait_ge(scattered, 16 * NT * K)
            load_xe(0, 0)
            load_xe(1, 1)
            with sp.Fori(1, E // 2) as i:
                for p in range(2):
                    e = 2 * i + p
                    sp.wait_ge(e_turned, e - 1)
                    load_xe(e, p)
                    sp.wait_ge(h_ready, e - 1)
                    load_w13(e, p)
                    sp.wait_ge(o_ready, 2 * (e - 2))
                    load_w2(e - 1, 1 - p)
            sp.wait_ge(o_ready, 2 * (E - 2))
            load_w2(E - 1, 1)

        @block.gpsimd
        def _(pool):
            nc.gpsimd.iota(count_e[:], [[1, E]], base=0, channel_multiplier=0,
                           allow_small_or_imprecise_dtypes=True).then_inc(tables_ready, 1)
            nc.gpsimd.memset(ones[:], 1.0).then_inc(tables_ready, 1)
            pool.wait_ge(tables_ready, 2)
            nc.gpsimd.affine_select(out=before[:], in_=ones[:], compare_op=ALU.is_gt, fill=0.0, base=0,
                                    pattern=[[1, P]], channel_multiplier=-1).then_inc(tables_ready, 1)
            for g in range(NG):
                at = slice(g * TG, (g + 1) * TG)
                pool.wait_ge(moments_ready, TG * (g + 1))
                nc.gpsimd.tensor_tensor(var_eps[:, at], moments[:, at, 1], eps[:, at], ALU.add).then_inc(own_pool, 1)
                pool.wait_ge(own_pool, g + 1)
                nc.gpsimd.tensor_tensor(rstd[:, at], var_eps[:, at], neg_half[:, at], ALU.pow).then_inc(rstd_ready, 1)
            pool.wait_ge(index_ready, 1)
            for t in range(NT):
                for k in range(K):
                    nc.gpsimd.indirect_dma_start(
                        out=scratch_xe, out_offset=bass.IndirectOffsetOnAxis(ap=send_index[:, t, k:k + 1], axis=0),
                        in_=xf[:, t, :], in_offset=None, bounds_check=E * CAP - 1, oob_is_err=False).then_inc(scattered, 16)
            pool.wait_ge(scattered, 16 * NT * K)

        @block.vector
        def _(dve):
            own = Ordered(dve, own_dve, 0)

            def step(instruction):
                own.done(instruction)
                own.wait()

            def moments_of(g):
                for t in range(g * TG, (g + 1) * TG):
                    own.done(nc.vector.bn_stats(stats[:, t, :], x_all[:, t, :]))
                own.wait()
                for t in range(g * TG, (g + 1) * TG):
                    nc.vector.bn_aggr(moments[:, t, :], stats[:, t, :]).then_inc(moments_ready, 1)

            moments_of(0)
            for g in range(NG):
                if g + 1 < NG:
                    moments_of(g + 1)
                dve.wait_ge(rstd_ready, g + 1)
                for t in range(g * TG, (g + 1) * TG):
                    nc.vector.tensor_scalar(xf[:, t, :], x_all[:, t, :], moments[:, t, 0:1], rstd[:, t:t + 1],
                                            ALU.subtract, ALU.mult).then_inc(xf_ready, 1)

            raw = ps_turn[:, 0, :].rearrange("p (t e) -> p t e", e=E)
            dve.wait_ge(logits_ready, NG)
            step(nc.vector.tensor_reduce(neg_max[:], raw, AX.X, ALU.max, negate=True))
            nc.vector.tensor_tensor(logits[:], raw, neg_max[:].unsqueeze(2).to_broadcast([P, NT, E]), ALU.add).then_inc(shifted_ready, 1)
            dve.wait_ge(exps_ready, 1)
            step(nc.vector.tensor_reduce(total[:], exps[:], AX.X, ALU.add))
            step(nc.vector.reciprocal(rtotal[:], total[:]))
            step(nc.vector.tensor_tensor(score[:], exps[:], rtotal[:].unsqueeze(2).to_broadcast([P, NT, E]), ALU.mult))
            step(nc.vector.tensor_reduce(gmax[:], score[:].rearrange("p t (g e) -> p t g e", g=G), AX.X, ALU.max))
            for t in range(NT):
                own.done(nc.vector.max(gtop[:, t, :], gmax[:, t, :]))
            own.wait()
            for t in range(NT):
                own.done(nc.vector.max_index(gidx[:, t, :], gtop[:, t, :], gmax[:, t, :]))
            own.wait()
            step(nc.vector.tensor_copy(gidx_f[:], gidx[:, :, 0:LG]))
            dve.wait_ge(tables_ready, 3)
            step(nc.vector.tensor_tensor(ghot[:], count_e[:, 0:G].unsqueeze(1).unsqueeze(1).to_broadcast([P, NT, LG, G]),
                                         gidx_f[:].unsqueeze(3).to_broadcast([P, NT, LG, G]), ALU.is_equal))
            step(nc.vector.tensor_reduce(gkeep[:], ghot[:].rearrange("p t k g -> p t g k"), AX.X, ALU.add))
            own.done(nc.vector.tensor_scalar(gpen[:], gkeep[:], -1.0, None, ALU.add))
            step(nc.vector.tensor_tensor(masked[:].rearrange("p t (g e) -> p t g e", g=G), score[:].rearrange("p t (g e) -> p t g e", g=G),
                                         gkeep[:].unsqueeze(3).to_broadcast([P, NT, G, EG]), ALU.mult))
            step(nc.vector.tensor_tensor(masked[:].rearrange("p t (g e) -> p t g e", g=G), masked[:].rearrange("p t (g e) -> p t g e", g=G),
                                         gpen[:].unsqueeze(3).to_broadcast([P, NT, G, EG]), ALU.add))
            for t in range(NT):
                own.done(nc.vector.max(etop[:, t, :], masked[:, t, :]))
            own.wait()
            for t in range(NT):
                own.done(nc.vector.max_index(eidx[:, t, :], etop[:, t, :], masked[:, t, :]))
            own.wait()
            own.done(nc.vector.tensor_copy(eidx_f[:], eidx[:, :, 0:K]))
            step(nc.vector.tensor_reduce(wsum[:], etop[:, :, 0:K], AX.X, ALU.add))
            step(nc.vector.tensor_tensor(ehot[:], count_e[:].unsqueeze(1).unsqueeze(1).to_broadcast([P, NT, K, E]),
                                         eidx_f[:].unsqueeze(3).to_broadcast([P, NT, K, E]), ALU.is_equal))
            step(nc.vector.tensor_reduce(chosen[:], ehot[:].rearrange("p t k e -> p t e k"), AX.X, ALU.add))
            step(nc.vector.memset(earlier[:, 0, :], 0.0))
            for t in range(1, NT):
                step(nc.vector.tensor_tensor(earlier[:, t, :], earlier[:, t - 1, :], chosen[:, t - 1, :], ALU.add))
            nc.vector.engine_nop().then_inc(chosen_ready, 1)
            step(nc.vector.tensor_scalar(wsum[:], wsum[:], 1e-9, None, ALU.add))
            step(nc.vector.reciprocal(rwsum[:], wsum[:]))
            step(nc.vector.tensor_tensor(row_weight[:], etop[:, :, 0:K], rwsum[:].unsqueeze(2).to_broadcast([P, NT, K]), ALU.mult))
            dve.wait_ge(pos_ready, 1)
            places = ps_turn[:, 1, :].rearrange("p (t e) -> p t e", e=E)
            step(nc.vector.tensor_tensor(epos[:], ehot[:], places.unsqueeze(2).to_broadcast([P, NT, K, E]), ALU.mult))
            step(nc.vector.tensor_reduce(pos[:], epos[:], AX.X, ALU.add))
            own.done(nc.vector.tensor_scalar(fits[:], pos[:], float(CAP), None, ALU.is_lt))
            step(nc.vector.scalar_tensor_tensor(out=dest[:], in0=eidx_f[:], scalar=float(CAP), in1=pos[:], op0=ALU.mult, op1=ALU.add))
            own.done(nc.vector.tensor_tensor(kept[:], dest[:], fits[:], ALU.mult))
            own.done(nc.vector.tensor_scalar(away[:], fits[:], -FAR, FAR, ALU.mult, ALU.add))
            step(nc.vector.tensor_tensor(row_weight[:], row_weight[:], fits[:], ALU.mult))
            nc.vector.tensor_tensor(send_index[:], kept[:], away[:], ALU.add).then_inc(index_ready, 1)
            step(nc.vector.tensor_copy(row_index[:], kept[:]))

            for g in range(NG):
                dve.wait_ge(sh_tanh, g + 1)
                if g:
                    dve.wait_ge(sh_gated, FC * g)
                for m in range(FC):
                    nc.vector.scalar_tensor_tensor(out=act_a[:, m, :], in0=act_t[:, m, :], scalar=1.0, in1=ps_h[:, 0, m, :],
                                                   op0=ALU.add, op1=ALU.mult).then_inc(sh_a, 1)
                dve.wait_ge(sh_a, FC * (g + 1))
                dve.wait_ge(z_ready, 2 * g)
                for m in range(FC):
                    nc.vector.scalar_tensor_tensor(out=gated[:, m, :], in0=act_a[:, m, :], scalar=0.5, in1=ps_h[:, 1, m, :],
                                                   op0=ALU.mult, op1=ALU.mult).then_inc(sh_gated, 1)
                for half in range(2):
                    dve.wait_ge(z_ready, 2 * g + half + 1)
                    t = g * TG + 2 * half
                    at = x_all[:, t:t + 2, :].rearrange("p t d -> p (t d)")
                    nc.vector.scalar_tensor_tensor(out=at, in0=ps_out[:, half, :], scalar=tgates[:, 2:3], in1=at,
                                                   op0=ALU.mult, op1=ALU.add).then_inc(z_out, 1)

            def prepare_layer1():
                blocks = {("q", 0): (0, 1), ("q", 1): (2, 3), ("k", 0): (0, 2), ("k", 1): (1, 3)}
                for n in ("q", "k"):
                    for part in range(2):
                        nc.vector.memset(sel[n][part][:].bitcast(F32), 0.0).then_inc(sel_zero, 1)
                dve.wait_ge(sel_zero, 4)
                for (n, part), at in blocks.items():
                    for k in at:
                        nc.vector.tensor_copy(sel[n][part][:, :, :, k, :], ident[:].rearrange("p (m h i) -> p m h i", m=4, h=2)).then_inc(sel_ready, 1)
                parts = ident[:].rearrange("p (j a d) -> p j a d", a=2, d=DK)
                nc.vector.tensor_tensor(join[:], parts[:, :, 0, :], parts[:, :, 1, :], ALU.add).then_inc(sel_ready, 1)
                dve.wait_ge(l1_loaded, 16 * 9)
                nc.vector.tensor_scalar(l1_rows["wq"][:], l1_rows["wq"][:], -SCALE1, None, ALU.mult).then_inc(wq_scaled, 1)
                nc.vector.tensor_scalar(b_neg[:], b_cols[:, 0, :], -SCALE1, None, ALU.mult).then_inc(lo_ready, 1)
                nc.vector.tensor_scalar(bo1_g[:], bo1_row, tgates[:, 1:2], None, ALU.mult).then_inc(lo_ready, 1)
                nc.vector.tensor_scalar(sw_pos, l1_rows["sw"][:], 0.0, None, ALU.is_gt).then_inc(sign_parts, 1)
                nc.vector.tensor_scalar(sw_neg, l1_rows["sw"][:], 0.0, None, ALU.is_lt).then_inc(sign_parts, 1)
                dve.wait_ge(sign_parts, 2)
                nc.vector.tensor_tensor(sw_sign, sw_pos, sw_neg, ALU.subtract).then_inc(sign_ready, 1)
                dve.wait_ge(wq_scaled, 1)
                for n in l1_w2:
                    nc.vector.tensor_copy(l1_w2[n][0][:], l1_rows[n][:]).then_inc(hi_ready, 1)
                for i, n in enumerate(l1_w2):
                    dve.wait_ge(hi_ready, i + 1)
                    nc.vector.tensor_tensor(l1_w2[n][1][:], l1_rows[n][:], l1_w2[n][0][:].bitcast(F32), ALU.subtract).then_inc(lo_ready, 1)

            prepare_layer1()

            def gate(e, p):
                dve.wait_ge(tanh_ready, e + 1)
                for m in range(FC):
                    nc.vector.scalar_tensor_tensor(out=e_a[:, m, :], in0=e_tanh[:, m, :], scalar=1.0, in1=ps_h[:, 0, m, 0:CAP],
                                                   op0=ALU.add, op1=ALU.mult).then_inc(a_ready, 1)
                dve.wait_ge(a_ready, FC * (e + 1))
                for m in range(FC):
                    nc.vector.scalar_tensor_tensor(out=e_gated[p][:, m, :], in0=e_a[:, m, :], scalar=0.5, in1=ps_h[:, 1, m, 0:CAP],
                                                   op0=ALU.mult, op1=ALU.mult).then_inc(gated_ready, 1)

            with dve.Fori(0, E // 2) as i:
                for p in range(2):
                    gate(2 * i + p, p)

        @block.scalar
        def _(act):
            act.wait_ge(wg_turned, 1)
            nc.scalar.copy(wgT[:], ps_h[:, 0, 0, 0:C * E].rearrange("p (c e) -> p c e", c=C)).then_inc(wgT_ready, 1)
            for g in range(NG):
                for c in range(C):
                    act.wait_ge(turned, C * g + c + 1)
                    nc.scalar.copy(xfT[:, c, g * GS:(g + 1) * GS], ps_out[:, c, :]).then_inc(xfT_ready, 1)
            act.wait_ge(shifted_ready, 1)
            nc.scalar.activation(exps[:], logits[:], ACT.Exp).then_inc(exps_ready, 1)
            for g in range(NG):
                act.wait_ge(sh_ready, g + 1)
                if g:
                    act.wait_ge(sh_a, FC * g)
                nc.scalar.activation(act_t[:], ps_h[:, 0], ACT.Tanh, scale=0.5).then_inc(sh_tanh, 1)

            act.wait_ge(sign_turned, 1)
            nc.scalar.copy(swT[:].rearrange("p c s -> p (c s)"), ps_out[:, 0, :]).then_inc(swT_ready, 1)

            def take_inputs(e, p):
                act.wait_ge(e_turned, e + 1)
                nc.scalar.copy(xeT[p][:], ps_turn[:, :, 0:CAP]).then_inc(xeT_ready, 1)

            def tanh(e):
                act.wait_ge(h_ready, e + 1)
                nc.scalar.activation(e_tanh[:], ps_h[:, 0, :, 0:CAP], ACT.Tanh, scale=0.5).then_inc(tanh_ready, 1)

            def put_outputs(e, p):
                for n, (lo, hi, rows) in enumerate(tails):
                    act.wait_ge(o_ready, 2 * e + n + 1)
                    if n == 0:
                        act.wait_ge(stored[p], 16 * (e - p))
                    nc.scalar.copy(oe[p][0:rows, lo:hi, :], ps_out[0:rows, n, 0:(hi - lo) * D].rearrange("p (c d) -> p c d", d=D)).then_inc(oe_ready, 1)
                for n, (lo, hi, rows) in enumerate(tails):
                    act.wait_ge(oe_ready, 2 * e + n + 1)
                    dst = scratch_oe[bass.ds(e * CAP + lo * P, (hi - lo) * rows)].rearrange("(c p) d -> p c d", p=rows)
                    act.dma_start(dst, oe[p][0:rows, lo:hi, :]).then_inc(stored[p], 16)

            take_inputs(0, 0)
            tanh(0)
            take_inputs(1, 1)
            with act.Fori(0, E // 2 - 1) as i:
                for p in (1, 0):
                    e = 2 * i + 2 - p
                    tanh(e)
                    take_inputs(e + 1, 1 - p)
                    put_outputs(e - 1, 1 - p)
            tanh(E - 1)
            put_outputs(E - 2, 0)
            put_outputs(E - 1, 1)
            for p in range(2):
                act.wait_ge(stored[p], 16 * E)

        @block.tensor
        def _(pe):
            pe.wait_ge(shared_loaded, 64)
            for c in range(C):
                ins = nc.tensor.transpose(ps_h[:, 0, 0, c * E:(c + 1) * E], wg_rows[:, c * P:(c + 1) * P], ident[0:E, 0:E])
            ins.then_inc(wg_turned, 1)
            pe.wait_ge(wgT_ready, 1)

            def route(g):
                pe.wait_ge(xfT_ready, C * (g + 1))
                for t in range(g * TG, (g + 1) * TG):
                    for c in range(C):
                        ins = nc.tensor.matmul(ps_turn[:, 0, t * E:(t + 1) * E], xfT[:, c, t * P:(t + 1) * P], wgT[:, c, :],
                                               start=(c == 0), stop=(c == C - 1))
                ins.then_inc(logits_ready, 1)

            for g in range(NG):
                pe.wait_ge(xf_ready, TG * (g + 1))
                for c in range(C):
                    if g:
                        pe.wait_ge(xfT_ready, C * (g - 1) + c + 1)
                    for t in range(TG):
                        ins = nc.tensor.transpose(ps_out[:, c, t * P:(t + 1) * P], xf[:, g * TG + t, c * P:(c + 1) * P], ident[:])
                    ins.then_inc(turned, 1)
                if g:
                    route(g - 1)
            route(NG - 1)

            def shared_h(g):
                pe.wait_ge(sh_gated, FC * g)
                for w, s in enumerate((s1, s3)):
                    for m in range(FC):
                        for c in range(C):
                            ins = nc.tensor.matmul(ps_h[:, w, m, :], s[:, c, m * P:(m + 1) * P], xfT[:, c, g * GS:(g + 1) * GS],
                                                   start=(c == 0), stop=(c == C - 1))
                ins.then_inc(sh_ready, 1)

            shared_h(0)
            pe.wait_ge(chosen_ready, 1)
            pe.wait_ge(tables_ready, 3)
            nc.tensor.matmul(ps_turn[:, 1, :], before[:], chosen[:].rearrange("p t e -> p (t e)"), start=True, stop=False)
            nc.tensor.matmul(ps_turn[:, 1, :], ones[:], earlier[:].rearrange("p t e -> p (t e)"), start=False, stop=True).then_inc(pos_ready, 1)
            for g in range(NG):
                if g:
                    shared_h(g)
                pe.wait_ge(sh_gated, FC * (g + 1))
                for half in range(2):
                    pe.wait_ge(z_out, max(2 * (g - 1) + half + 1, 0))
                    for k in range(2):
                        t = 2 * half + k
                        for m in range(FC):
                            ins = nc.tensor.matmul(ps_out[:, half, k * D:(k + 1) * D], gated[:, m, t * P:(t + 1) * P], s2[:, m, :],
                                                   start=(m == 0), stop=(m == FC - 1))
                    ins.then_inc(z_ready, 1)

            def turn(e, p):
                pe.wait_ge(xe_loaded[p], 16 * (e - p) + 32)
                pe.wait_ge(xeT_ready, e)
                for c in range(C):
                    for chunk in range(3):
                        rows = min(P, CAP - chunk * P)
                        ins = nc.tensor.transpose(ps_turn[:, c, chunk * P:chunk * P + rows],
                                                  xe[p][0:rows, chunk, c * P:(c + 1) * P], ident[0:rows, 0:rows])
                ins.then_inc(e_turned, 1)

            def hidden(e, p):
                pe.wait_ge(w13_loaded[p], 16 * (e - p) + 32)
                pe.wait_ge(xeT_ready, e + 1)
                pe.wait_ge(gated_ready, FC * e)
                for w, s in enumerate((w1s, w3s)):
                    for m in range(FC):
                        for c in range(C):
                            ins = nc.tensor.matmul(ps_h[:, w, m, 0:CAP], s[p][:, c, m * P:(m + 1) * P], xeT[p][:, c, :],
                                                   start=(c == 0), stop=(c == C - 1))
                ins.then_inc(h_ready, 1)

            def output(e, p):
                pe.wait_ge(l1_w2loaded[p], 8 * (e - p) + 16)
                pe.wait_ge(gated_ready, FC * (e + 1))
                for n, (lo, hi, rows) in enumerate(tails):
                    pe.wait_ge(oe_ready, 2 * e)
                    for chunk in range(lo, hi):
                        for m in range(FC):
                            ins = nc.tensor.matmul(ps_out[0:rows, n, (chunk - lo) * D:(chunk - lo + 1) * D],
                                                   e_gated[p][:, m, chunk * P:chunk * P + rows], w2s[p][:, m, :],
                                                   start=(m == 0), stop=(m == FC - 1))
                    ins.then_inc(o_ready, 1)

            pe.wait_ge(z_out, 2 * NG)
            pe.wait_ge(sign_ready, 1)
            for c in range(C):
                for t in range(C):
                    ins = nc.tensor.transpose(ps_out[:, 0, c * D + t * P:c * D + (t + 1) * P], sw_sign[:, t, c * P:(c + 1) * P], ident[:])
            ins.then_inc(sign_turned, 1)
            pe.wait_ge(index_ready, 1)
            pe.wait_ge(swT_ready, 1)
            turn(0, 0)
            hidden(0, 0)
            turn(1, 1)
            with pe.Fori(0, E // 2 - 1) as i:
                for p in (1, 0):
                    e = 2 * i + 2 - p
                    hidden(e, p)
                    turn(e + 1, 1 - p)
                    output(e - 1, 1 - p)
            hidden(E - 1, 1)
            output(E - 2, 0)
            output(E - 1, 1)


def xattn1(nc, keep, env):
    ctx_in, out = env["ctx_in"], env["out"]
    w2, swT, sel, join, b_cols, b_neg, bv_row, bo_g = (env[k] for k in ("w2l1", "swT", "sel", "join", "b_cols", "b_neg", "bv_row", "bo1_g"))
    x_all, ident, neg_half, eps, tgates, rel_bias = (env[k] for k in ("x_all", "ident", "neg_half", "eps", "tgates", "rel_bias"))
    row_index, row_weight, scratch_oe = env["row_index"], env["row_weight"], env["scratch_oe"]
    B, T, C, D, K, DK, SCALE1 = (env[k] for k in ("B", "T", "C", "D", "K", "DK", "SCALE1"))
    H = env["H1"]
    S = T * P
    GR = P // 32
    M = H // 2
    PAD = P - 32

    with ExitStack() as phase:
        sb, ps, sem = make_tools(nc, phase, "c")
        ps_scores = ps("scores", [P, 2, T, S])
        ps_turn = ps("turn", [P, 2, T, S])
        ps_o = ps("o", [P, H // GR, S])
        ps_work = ps("work", [P, 2, 512])

        cin = sb("cin", [P, T, D])
        index_now = sb("index_now", [P, T, K], U32)
        rows = sb("rows", [P, T, K, D])
        weight_now = sb("weight_now", [P, T, K])
        x2 = [sb(f"x2_{i}", [P, T, D]) for i in range(2)]
        xb = [sb(f"xb{i}", [P, T, D]) for i in range(2)]
        stats = sb("stats", [P, 2, T, 6])
        moments = sb("moments", [P, 2, T, 2])
        var_eps = sb("var_eps", [P, 2, T])
        rstd = sb("rstd", [P, 2, T])
        xn = sb("xn", [P, T, D])
        x3 = [sb(f"x3_{i}", [P, T, D]) for i in range(2)]
        x3n = sb("x3n", [P, T, D])
        o_rows = x3n
        turned2 = {n: [sb(f"{n}T_{part}", [P, C, S], F32R) for part in ("hi", "lo")] for n in ("ctx", "x", "x3", "o")}
        qk2 = {n: [sb(f"{n}_{part}", [P, C, S], F32R) for part in ("hi", "lo")] for n in ("q", "k")}
        stacked = {n: [sb(f"{n}S{i}", [P, M, S], F32R) for i in range(2)] for n in ("q", "k")}
        v_sum = sb("v_sum", [P, T, D])
        v_pad = [sb(f"v_pad{i}", [P, T, PAD + H * P], F32R) for i in range(2)]
        s_neg = sb("s_neg", [P, 2, T, S])
        max_neg = sb("max_neg", [P, 2, T])
        probs = sb("probs", [P, 2, T, S])
        rsum = [sb(f"rsum{i}", [P, H, T]) for i in range(2)]
        rinv = sb("rinv", [P, H, T])
        pT2 = [sb(f"pT_{part}", [P, 2, T, S], F32R) for part in ("hi", "lo")]
        o_parts = sb("o_parts", [P, H // GR, S])

        USES = (("ctx", True, 0), ("o_join", False, 1), ("k", True, 2), ("o", False, 3), ("x", True, 4), ("y", False, 5),
                ("q", True, 6), ("k0", True, 6), ("q0", True, 8), ("q1", True, 8), ("k1", True, 10), ("v", True, 10),
                ("x3", False, 11), ("k2", True, 12), ("ff", False, 13), ("k3", True, 14), ("q2", True, 15), ("q3", True, 15))
        BANK = {u[0]: n % 2 for n, u in enumerate(USES)}

        names = ("v_zero",
                 "own_front", "own_late", "own_pool", "own_combine", "f_moments", "f_rstd", "l_moments", "l_rstd",
                 "scores_seen", "stats_seen", "index_seen", "rstd_seen", "index_copied", "weight_copied", "summed", "x2_ready", "xb_ready",
                 "xn_ready", "scores_ready", "biased", "probs_ready", "turned", "pT_hi", "pT_lo", "pv_ready", "o_parts_out",
                 "rinv_ready", "o_ready", "v_summed", "v_hi", "v_lo", "own_front_rstd", "own_late_rstd", "x3_ready", "x3n_ready", "fin_ready")
        (v_zero,
         own_front, own_late, own_pool, own_combine, f_moments, f_rstd, l_moments, l_rstd,
         scores_seen, stats_seen, index_seen, rstd_seen, index_copied, weight_copied, summed, x2_ready, xb_ready,
         xn_ready, scores_ready, biased, probs_ready, turned, pT_hi, pT_lo, pv_ready, o_parts_out,
         rinv_ready, o_ready, v_summed, v_hi, v_lo, own_front_rstd, own_late_rstd, x3_ready, x3n_ready, fin_ready) = [sem(n) for n in names]
        ready = {u[0]: sem(f"{u[0]}_in_bank") for u in USES}
        hi_out = {n: sem(f"{n}_hi_out") for n in ("ctx", "k", "o", "x3", "x", "q")}
        bank_free = [sem(f"bank_free{i}") for i in range(2)]
        ctx_loaded = sem("ctx_loaded")
        gathered = sem("gathered")
        stored = [sem(f"stored{i}") for i in range(2)]

        c_rows = ctx_in.rearrange("b (t p) d -> b p t d", p=P)
        out_rows = out.rearrange("b (t p) d -> b p t d", p=P)

        def slots(eng, slot):
            slot(0, 0, True, False)
            with eng.Fori(0, B // 2 - 1) as i:
                slot(2 * i + 1, 1, True, True)
                slot(2 * i + 2, 0, True, True)
            slot(B - 1, 1, False, True)

        def uses_at(h, more, behind):
            return [(n, ahead) for n, ahead, at in USES if at == h and (more if ahead else behind)]

        def empty_banks(take, b, p, h, more, behind):
            if h >= 2:
                for name, ahead in uses_at(h - 2, more, behind):
                    take(name, b + 1 if ahead else b - 1, 1 - p)
            elif behind:
                for name, _ in uses_at(H + h - 2, True, False):
                    take(name, b, p)

        FRONT_AT = (0, 1, 1, 3)
        LATE_AT = (7, 8, 10)

        def heads(b, h):
            n = H * b + h + 1
            return max(n, 0) if isinstance(n, int) else n

        block = phase.enter_context(nc.Block())

        @block.sync
        def _(sp):
            def load(b):
                sp.dma_start(cin[:], c_rows[bass.ds(b, 1)].rearrange("b p t d -> p (b t) d")).then_inc(ctx_loaded, 16)

            def store(b, p):
                sp.wait_ge(fin_ready, T * (b + 1))
                sp.dma_start(out_rows[bass.ds(b, 1)].rearrange("b p t d -> p (b t) d"), x3[p][:]).then_inc(stored[p], 16)

            load(0)
            sp.wait_ge(ready["ctx"], 1)
            load(1)
            with sp.Fori(1, B // 2) as i:
                for p in range(2):
                    b = 2 * i + p
                    sp.wait_ge(ready["ctx"], b)
                    load(b)
                    store(b - 2, p)
            store(B - 2, 0)
            store(B - 1, 1)
            for p in range(2):
                sp.wait_ge(stored[p], 16 * B // 2)

        @block.gpsimd
        def _(pool):
            oc = Ordered(pool, own_combine, 2)

            def gather(b):
                pool.wait_ge(gathered, 16 * T * K * b)
                pool.wait_ge(summed, b)
                nc.gpsimd.tensor_copy(index_now[:], row_index[:, bass.ds(T * b, T), :]).then_inc(index_copied, 1)
                pool.wait_ge(index_copied, b + 1)
                pool.sem_inc(index_seen, 1)
                for t in range(T):
                    for k in range(K):
                        nc.gpsimd.indirect_dma_start(
                            out=rows[:, t, k, :], out_offset=None, in_=scratch_oe,
                            in_offset=bass.IndirectOffsetOnAxis(ap=index_now[:, t, k:k + 1], axis=0)).then_inc(gathered, 16)

            def combine(b, p):
                oc.start(b)
                nc.gpsimd.tensor_copy(weight_now[:], row_weight[:, bass.ds(T * b, T), :]).then_inc(weight_copied, 1)
                pool.wait_ge(weight_copied, b + 1)
                pool.wait_ge(gathered, 16 * T * K * (b + 1))
                oc.done(nc.gpsimd.tensor_tensor(rows[:], rows[:], weight_now[:].unsqueeze(3).to_broadcast([P, T, K, D]), ALU.mult))
                oc.wait()
                oc.done(nc.gpsimd.tensor_tensor(rows[:, :, 0:2, :], rows[:, :, 0:2, :], rows[:, :, 2:4, :], ALU.add))
                oc.wait()
                pool.wait_ge(xn_ready, max(T * (b - 1), 0) if isinstance(b, int) else T * (b - 1))
                pool.wait_ge(xb_ready, max(b - 1, 0) if isinstance(b, int) else b - 1)
                nc.gpsimd.tensor_tensor(x2[p][:], rows[:, :, 0, :], rows[:, :, 1, :], ALU.add).then_inc(summed, 1)

            def rstds(b, late):
                mine = (own_front_rstd, own_late_rstd)[late]
                pool.wait_ge((f_moments, l_moments)[late], T * (b + 1))
                nc.gpsimd.tensor_tensor(var_eps[:, late, :], moments[:, late, :, 1], eps[:, 0:T], ALU.add).then_inc(mine, 1)
                pool.wait_ge(mine, b + 1)
                nc.gpsimd.tensor_tensor(rstd[:, late, :], var_eps[:, late, :], neg_half[:, 0:T], ALU.pow).then_inc((f_rstd, l_rstd)[late], 1)

            def with_bias(b, p):
                pool.wait_ge(x2_ready, T * (b + 1))
                nc.gpsimd.tensor_tensor(xb[p][:], x2[p][:], bo_g[:].unsqueeze(1).to_broadcast([P, T, D]), ALU.add).then_inc(xb_ready, 1)

            def v_low(b, p):
                pool.wait_ge(v_hi, T * (b + 1))
                for t in range(T):
                    at = v_pad[p][:, t, PAD:].rearrange("p (h m) -> p h m", m=P)
                    nc.gpsimd.tensor_tensor(at[:, :, DK:2 * DK], v_sum[:, t, :].rearrange("p (h d) -> p h d", d=DK), at[:, :, 0:DK].bitcast(F32),
                                            ALU.subtract).then_inc(v_lo, 1)

            def slot(b, p, more, behind, combines, gathers):
                if more:
                    rstds(b + 1, 0)
                if combines:
                    combine(b + 2, p)
                if gathers:
                    gather(b + 3)
                if behind:
                    pool.wait_ge(x3_ready, T * b)
                if more:
                    with_bias(b + 1, 1 - p)
                if behind:
                    rstds(b - 1, 1)
                if more:
                    v_low(b + 1, 1 - p)

            for i in range(2):
                nc.gpsimd.memset(v_pad[i][:].bitcast(F32), 0.0).then_inc(v_zero, 1)
            gather(0)
            combine(0, 0)
            gather(1)
            rstds(0, 0)
            combine(1, 1)
            gather(2)
            with_bias(0, 0)
            v_low(0, 0)
            slot(0, 0, True, False, True, True)
            with pool.Fori(0, B // 2 - 2) as i:
                slot(2 * i + 1, 1, True, True, True, True)
                slot(2 * i + 2, 0, True, True, True, True)
            slot(B - 3, 1, True, True, True, False)
            slot(B - 2, 0, True, True, False, False)
            slot(B - 1, 1, False, True, False, False)
            rstds(B - 1, 1)

        @block.vector
        def _(dve):
            of = Ordered(dve, own_front, T)
            ol = Ordered(dve, own_late, T)

            def front(b, p, step=None):
                if step in (None, 0):
                    dve.wait_ge(summed, b + 1)
                    of.start(b)
                    for t in range(T):
                        nc.vector.scalar_tensor_tensor(out=x2[p][:, t, :], in0=x2[p][:, t, :], scalar=tgates[:, 2:3],
                                                       in1=x_all[:, bass.ds(T * b + t, 1), :].rearrange("p t d -> p (t d)"),
                                                       op0=ALU.mult, op1=ALU.add).then_inc(x2_ready, 1)
                if step in (None, 1):
                    dve.wait_ge(x2_ready, T * (b + 1))
                    for t in range(T):
                        of.done(nc.vector.bn_stats(stats[:, 0, t, :], x2[p][:, t, :]))
                if step in (None, 2):
                    of.wait()
                    dve.sem_inc(stats_seen, 1)
                    for t in range(T):
                        nc.vector.bn_aggr(moments[:, 0, t, :], stats[:, 0, t, :]).then_inc(f_moments, 1)
                if step in (None, 3):
                    dve.wait_ge(f_rstd, b + 1)
                    dve.wait_ge(ready["x"], b)
                    for t in range(T):
                        nc.vector.tensor_scalar(xn[:, t, :], x2[p][:, t, :], moments[:, 0, t, 0:1], rstd[:, 0, t:t + 1],
                                                ALU.subtract, ALU.mult).then_inc(xn_ready, 1)

            def late(b, p, step=None):
                if step in (None, 0):
                    ol.start(b)
                    dve.wait_ge(x3_ready, T * (b + 1))
                    for t in range(T):
                        ol.done(nc.vector.bn_stats(stats[:, 1, t, :], x3[p][:, t, :]))
                if step in (None, 1):
                    ol.wait()
                    dve.sem_inc(stats_seen, 1)
                    for t in range(T):
                        nc.vector.bn_aggr(moments[:, 1, t, :], stats[:, 1, t, :]).then_inc(l_moments, 1)
                if step in (None, 2):
                    dve.wait_ge(l_rstd, b + 1)
                    dve.wait_ge(ready["x3"], b)
                    for t in range(T):
                        nc.vector.tensor_scalar(x3n[:, t, :], x3[p][:, t, :], moments[:, 1, t, 0:1], rstd[:, 1, t:t + 1],
                                                ALU.subtract, ALU.mult).then_inc(x3n_ready, 1)

            def take(name, b, p):
                if name in ("o_join", "ctx", "k", "o", "y", "v", "x3", "x", "ff", "q"):
                    bank = ps_work[:, BANK[name], :]
                    free = bank_free[BANK[name]]
                    if name in ("ctx", "x3", "x", "o"):
                        dve.wait_ge(hi_out[name], b + 1)
                        hi, lo = turned2[name]
                        nc.vector.tensor_tensor(lo[:].rearrange("p c s -> p (c s)"), bank, hi[:].bitcast(F32).rearrange("p c s -> p (c s)"),
                                                ALU.subtract).then_inc(free, 1)
                    elif name in ("q", "k"):
                        dve.wait_ge(hi_out[name], C * (b + 1))
                        hi, lo = qk2[name]
                        bias_col = (b_neg, b_cols[:, 1, :])[name == "k"]
                        for c in range(C):
                            ins = nc.vector.scalar_tensor_tensor(out=lo[:, c, :], in0=bank[:, c * S:(c + 1) * S], scalar=bias_col[:, c:c + 1],
                                                                 in1=hi[:, c, :].bitcast(F32), op0=ALU.add, op1=ALU.subtract)
                        ins.then_inc(free, 1)
                    elif name == "v":
                        dve.wait_ge(ready["v"], b + 1)
                        dve.wait_ge(v_lo, T * b)
                        nc.vector.tensor_tensor(v_sum[:], bank.rearrange("p (t d) -> p t d", t=T),
                                                bv_row[:].unsqueeze(1).to_broadcast([P, T, D]), ALU.add).then_inc(v_summed, 1)
                        dve.wait_ge(v_summed, b + 1)
                        dve.sem_inc(free, 1)
                    elif name == "o_join":
                        dve.wait_ge(ready["o_join"], b + 1)
                        dve.wait_ge(rinv_ready, b + 1)
                        dve.wait_ge(ready["o"], b)
                        nc.vector.tensor_tensor(o_rows[:].rearrange("p t (h d) -> p t h d", d=DK), bank.rearrange("p (t h d) -> p t h d", t=T, d=DK),
                                                rinv[:].rearrange("p h t -> p t h").unsqueeze(3).to_broadcast([P, T, H, DK]),
                                                ALU.mult).then_inc(free, 1)
                    elif name == "y":
                        dve.wait_ge(ready["y"], b + 1)
                        dve.wait_ge(xb_ready, b + 1)
                        dve.wait_ge(stored[p], 8 * (b - p))
                        for t in range(T):
                            ins = nc.vector.scalar_tensor_tensor(out=x3[p][:, t, :], in0=bank[:, t * D:(t + 1) * D], scalar=tgates[:, 1:2],
                                                                 in1=xb[p][:, t, :], op0=ALU.mult, op1=ALU.add)
                            ins.then_inc(x3_ready, 1)
                        dve.wait_ge(x3_ready, T * (b + 1))
                        dve.sem_inc(free, 1)
                    else:
                        dve.wait_ge(ready["ff"], b + 1)
                        for t in range(T):
                            nc.vector.scalar_tensor_tensor(out=x3[p][:, t, :], in0=bank[:, t * D:(t + 1) * D], scalar=tgates[:, 3:4],
                                                           in1=x3[p][:, t, :], op0=ALU.mult, op1=ALU.add).then_inc(fin_ready, 1)
                        dve.wait_ge(fin_ready, T * (b + 1))
                        dve.sem_inc(free, 1)

            def bias(b, h):
                dve.wait_ge(probs_ready, T * heads(b, h - 2))
                dve.wait_ge(scores_ready, heads(b, h))
                dve.sem_inc(scores_seen, 1)
                for t in range(T):
                    nc.vector.tensor_tensor_reduce(s_neg[:, h % 2, t, :], ps_scores[:, h % 2, t, :], rel_bias[:, h, (1 - t) * P:(1 - t) * P + S],
                                                   1.0, 3.0e38, ALU.add, ALU.min, max_neg[:, h % 2, t:t + 1]).then_inc(biased, 1)

            def probs_low(b, h):
                dve.wait_ge(pT_hi, heads(b, h))
                nc.vector.tensor_tensor(pT2[1][:, h % 2], ps_turn[:, h % 2], pT2[0][:, h % 2].bitcast(F32), ALU.subtract).then_inc(pT_lo, 1)

            def row_sums(b, p):
                dve.wait_ge(probs_ready, T * heads(b, H - 1))
                nc.vector.reciprocal(rinv[:], rsum[p][:]).then_inc(rinv_ready, 1)

            def slot(b, p, more, behind):
                for h in range(H):
                    if h < H - 1:
                        bias(b, h + 1)
                    elif more:
                        bias(b + 1, 0)
                    empty_banks(take, b, p, h, more, behind)
                    if h:
                        probs_low(b, h - 1)
                    elif behind:
                        probs_low(b - 1, H - 1)
                        row_sums(b - 1, 1 - p)
                    for n in range(len(FRONT_AT)):
                        if more and h == FRONT_AT[n]:
                            front(b + 1, 1 - p, n)
                    if behind and h in LATE_AT:
                        late(b - 1, 1 - p, LATE_AT.index(h))

            front(0, 0)
            for name, ahead, _ in USES:
                if ahead:
                    take(name, 0, 0)
            bias(0, 0)
            slots(dve, slot)
            probs_low(B - 1, H - 1)
            row_sums(B - 1, 1)
            take("o_join", B - 1, 1)
            take("o", B - 1, 1)
            take("y", B - 1, 1)
            late(B - 1, 1)
            take("x3", B - 1, 1)
            take("ff", B - 1, 1)

        @block.scalar
        def _(act):
            def take(name, b, p):
                bank = ps_work[:, BANK[name], :]
                if name in ("ctx", "x3", "x", "o"):
                    act.wait_ge(ready[name], b + 1)
                    nc.scalar.copy(turned2[name][0][:].rearrange("p c s -> p (c s)"), bank).then_inc(hi_out[name], 1)
                elif name in ("q", "k"):
                    act.wait_ge(ready[name], b + 1)
                    bias_col = (b_neg, b_cols[:, 1, :])[name == "k"]
                    for c in range(C):
                        nc.scalar.activation(qk2[name][0][:, c, :], bank[:, c * S:(c + 1) * S], ACT.Identity, bias=bias_col[:, c:c + 1],
                                             scale=1.0).then_inc(hi_out[name], 1)
                elif name[0] in "qk":
                    act.wait_ge(ready[name], b + 1)
                    m = 2 * int(name[1])
                    nc.scalar.copy(stacked[name[0]][p][:, m:m + 2, :].rearrange("p m s -> p (m s)"), bank).then_inc(bank_free[BANK[name]], 1)
                elif name == "v":
                    act.wait_ge(v_summed, b + 1)
                    for t in range(T):
                        nc.scalar.copy(v_pad[p][:, t, PAD:].rearrange("p (h m) -> p h m", m=P)[:, :, 0:DK],
                                       v_sum[:, t, :].rearrange("p (h d) -> p h d", d=DK)).then_inc(v_hi, 1)

            def slot(b, p, more, behind):
                if behind:
                    act.wait_ge(rinv_ready, b - 1)
                for h in range(H):
                    act.wait_ge(biased, T * heads(b, h))
                    act.wait_ge(turned, heads(b, h - 2))
                    for t in range(T):
                        nc.scalar.activation(probs[:, h % 2, t, :], s_neg[:, h % 2, t, :], ACT.Exp, bias=max_neg[:, h % 2, t:t + 1],
                                             scale=-1.0, accum_out=rsum[p][:, h, t:t + 1]).then_inc(probs_ready, 1)
                    empty_banks(take, b, p, h, more, behind)
                    if h:
                        probs_high(b, h - 1)
                    elif behind:
                        probs_high(b - 1, H - 1)
                    if h == 1 and behind:
                        parts_out(b - 1)

            def probs_high(b, h):
                act.wait_ge(turned, heads(b, h))
                act.wait_ge(pv_ready, heads(b, h - 2))
                nc.scalar.copy(pT2[0][:, h % 2], ps_turn[:, h % 2]).then_inc(pT_hi, 1)

            def parts_out(b):
                act.wait_ge(pv_ready, H * (b + 1))
                act.wait_ge(ready["o_join"], b)
                for g in range(0, H // GR, 2):
                    nc.scalar.copy(o_parts[:, g:g + 2, :], ps_o[:, g:g + 2, :]).then_inc(o_parts_out, 1)

            for name, ahead, _ in USES:
                if ahead:
                    take(name, 0, 0)
            slots(act, slot)
            probs_high(B - 1, H - 1)
            parts_out(B - 1)
            take("o", B - 1, 1)
            take("x3", B - 1, 1)

        @block.tensor
        def _(pe):
            ahead_uses = [sum(1 for n, a, _ in USES if a and BANK[n] == k) for k in range(2)]
            behind_uses = [sum(1 for n, a, _ in USES if not a and BANK[n] == k) for k in range(2)]
            before, used = [0, 0], [0, 0]
            place = {}

            def start_slot(b):
                for k in range(2):
                    before[k] = ahead_uses[k] if isinstance(b, int) and b == 0 else \
                        (ahead_uses[k] + behind_uses[k]) * b + ahead_uses[k] - behind_uses[k]
                    used[k] = 0

            def fill(name):
                k = BANK[name]
                pe.wait_ge(bank_free[k], before[k] + used[k])
                place[name] = used[k]
                used[k] += 1
                return ps_work[:, k, :]

            def emptied(name):
                pe.wait_ge(bank_free[BANK[name]], before[BANK[name]] + place[name] + 1)

            def product(out, a, b, first=True, last=True):
                nc.tensor.matmul(out, a[0], b[0], start=first, stop=False)
                nc.tensor.matmul(out, a[0], b[1], start=False, stop=False)
                return nc.tensor.matmul(out, a[1], b[0], start=False, stop=last)

            def turn(bank, src):
                for c in range(C):
                    for t in range(T):
                        ins = nc.tensor.transpose(bank[:, c * S + t * P:c * S + (t + 1) * P], src[:, t, c * P:(c + 1) * P], ident[:])
                return ins

            def project(bank, srcT, w):
                for t in range(T):
                    for c in range(C):
                        ins = product(bank[:, t * D:(t + 1) * D], [s[:, c, t * P:(t + 1) * P] for s in srcT], [s[:, c, :] for s in w],
                                      c == 0, c == C - 1)
                return ins

            def use(name, b, p):
                bank = fill(name)
                if name == "ctx":
                    pe.wait_ge(ctx_loaded, 16 * (b + 1))
                    ins = turn(bank, cin)
                elif name == "x":
                    pe.wait_ge(xn_ready, T * (b + 1))
                    ins = turn(bank, xn)
                elif name == "x3":
                    pe.wait_ge(x3n_ready, T * (b + 1))
                    ins = turn(bank, x3n)
                elif name == "o":
                    emptied("o_join")
                    ins = turn(bank, o_rows)
                elif name in ("q", "k"):
                    src = {"q": "x", "k": "ctx"}[name]
                    emptied(src)
                    for m in range(2):
                        for c in range(C):
                            ins = product(bank[:, m * S:(m + 1) * S], [w[:, c, m * P:(m + 1) * P] for w in w2["w" + name]],
                                          [s[:, c, :] for s in turned2[src]], c == 0, c == C - 1)
                elif name[0] in "qk":
                    emptied(name[0])
                    for k in range(2):
                        m = 2 * int(name[1]) + k
                        for part in range(2):
                            ins = nc.tensor.matmul(bank[:, k * S:(k + 1) * S], sel[name[0]][part][:, m % 4].rearrange("p h k i -> p (h k i)"),
                                                   qk2[name[0]][part][:, m // 4, :], start=(part == 0), stop=(part == 1))
                elif name == "v":
                    ins = project(bank, turned2["ctx"], w2["wv"])
                elif name == "o_join":
                    pe.wait_ge(o_parts_out, 2 * (b + 1))
                    for t in range(T):
                        for g in range(H // GR):
                            at = (t * (H // GR) + g) * GR * DK
                            ins = nc.tensor.matmul(bank[:, at:at + GR * DK], o_parts[:, g, t * P:(t + 1) * P], join[:].rearrange("p j d -> p (j d)"),
                                                   start=True, stop=True)
                elif name == "y":
                    emptied("o")
                    ins = project(bank, turned2["o"], w2["wo"])
                else:
                    emptied("x3")
                    for t in range(T):
                        for c in range(C):
                            for part in range(2):
                                ins = nc.tensor.matmul(bank[:, t * D:(t + 1) * D], turned2["x3"][part][:, c, t * P:(t + 1) * P], swT[:, c, :],
                                                       start=(c == 0 and part == 0), stop=(c == C - 1 and part == 1))
                ins.then_inc(ready[name], 1)

            def scores(b, p, h):
                m, at = h // 2, slice(64 * (h % 2), 64 * (h % 2) + 64)
                pe.wait_ge(biased, T * heads(b, h - 2))
                for t in range(T):
                    ins = nc.tensor.matmul(ps_scores[:, h % 2, t, :], stacked["q"][p][at, m, t * P:(t + 1) * P], stacked["k"][p][at, m, :],
                                           start=True, stop=True)
                ins.then_inc(scores_ready, 1)

            def turn_probs(b, h):
                pe.wait_ge(probs_ready, T * heads(b, h))
                pe.wait_ge(pT_lo, heads(b, h - 2))
                for tk in range(T):
                    for tq in range(T):
                        ins = nc.tensor.transpose(ps_turn[:, h % 2, tk, tq * P:(tq + 1) * P], probs[:, h % 2, tq, tk * P:(tk + 1) * P], ident[:])
                ins.then_inc(turned, 1)

            def values(b, p, h):
                g, j = divmod(h, GR)
                pe.wait_ge(pT_lo, heads(b, h))
                if h == 0:
                    pe.wait_ge(o_parts_out, 2 * b)
                    pe.wait_ge(v_lo, T * (b + 1))
                at = PAD + P * h - 32 * j
                for tk in range(T):
                    for part in range(2):
                        ins = nc.tensor.matmul(ps_o[:, g, :], v_pad[p][:, tk, at:at + P], pT2[part][:, h % 2, tk, :],
                                               start=(j == 0 and tk == 0 and part == 0), stop=(j == GR - 1 and tk == T - 1 and part == 1))
                ins.then_inc(pv_ready, 1)

            def stacks_ready():
                for k in range(2):
                    pe.wait_ge(bank_free[k], before[k] + used[k])

            def slot(b, p, more, behind):
                start_slot(b)
                for h in range(H):
                    turn_probs(b, h)
                    if h == 2:
                        for k in range(2):
                            pe.wait_ge(bank_free[k], before[k])
                    if h + 2 < H:
                        scores(b, p, h + 2)
                    elif more:
                        if h + 2 == H:
                            emptied("q0")
                            emptied("k0")
                        scores(b + 1, 1 - p, h + 2 - H)
                    if h:
                        values(b, p, h - 1)
                    elif behind:
                        values(b - 1, 1 - p, H - 1)
                    for name, ahead in uses_at(h, more, behind):
                        use(name, b + 1 if ahead else b - 1, 1 - p)

            pe.wait_ge(v_zero, 2)
            for name, ahead, _ in USES:
                if ahead:
                    use(name, 0, 0)
            stacks_ready()
            scores(0, 0, 0)
            scores(0, 0, 1)
            slots(pe, slot)
            values(B - 1, 1, H - 1)
            start_slot(B)
            for k in range(2):
                before[k] -= ahead_uses[k]
            for name, ahead, _ in USES:
                if not ahead:
                    use(name, B - 1, 1)


_INS = ["x", "ctx_1024", "g_xattn", "g_ffn", "L0_xattn_ln_l_w", "L0_xattn_ln_l_b", "L0_xattn_ln_c_w", "L0_xattn_ln_c_b",
        "L0_xattn_Wq", "L0_xattn_Wkv", "L0_xattn_Wo", "L0_xattn_bo", "L0_ffn_wg", "L0_ffn_w1", "L0_ffn_w2", "L0_ffn_w3",
        "L0_ffn_sw1", "L0_ffn_sw2", "L0_ffn_sw3", "L1_xattn_Wq", "L1_xattn_bq", "L1_xattn_Wk", "L1_xattn_bk",
        "L1_xattn_Wv", "L1_xattn_bv", "L1_xattn_Wo", "L1_xattn_bo", "L1_xattn_rel", "L1_ffn_weight"]


def kernel(**inputs):
    import numpy as np
    import concourse.bacc as bacc
    from concourse.bass_utils import run_bass_kernel_spmd

    nc = bacc.Bacc("TRN2", target_bir_lowering=False, num_devices=1)
    arrays, args = {}, []
    for name in _INS:
        a = np.ascontiguousarray(inputs[name])
        arrays[f"in_{name}"] = a
        args.append(nc.dram_tensor(f"in_{name}", a.shape, mybir.dt.from_np(a.dtype), kind="ExternalInput").ap())
    shape = inputs["x"].shape
    args.append(nc.dram_tensor("out", shape, F32, kind="ExternalOutput").ap())
    flamingo_kernel(nc, *args)
    r = run_bass_kernel_spmd(nc, [arrays], core_ids=[0])
    return r.results[0]["out"]
```

```python
from contextlib import ExitStack

import numpy as np

import concourse.bass as bass
from concourse import mybir

P = 128
ALU = mybir.AluOpType
ACT = mybir.ActivationFunctionType
F32 = mybir.dt.float32
F32R = mybir.dt.float32r
U32 = mybir.dt.uint32
AX = mybir.AxisListType

EPS = 1e-5
CLIP = 11.0
FAR = float(1 << 20)
AREA = 8192
ROUTE_STEPS = 39


def flamingo_kernel(
    nc: bass.Bass,
    x, ctx_in, g_xattn, g_ffn,
    ln_l_w, ln_l_b, ln_c_w, ln_c_b, Wq, Wkv, Wo, bo,
    wg, w1, w2, w3, sw1, sw2, sw3,
    Wq1, bq1, Wk1, bk1, Wv1, bv1, Wo1, bo1, rel, sign_w,
    out,
):
    B, S, D = x.shape
    INNER = Wq.shape[1]
    H0, D0 = 16, INNER // 16
    PAIRS = H0 // 2
    E, F = wg.shape[0], w1.shape[2]
    K, G, LG = 4, 8, 4
    N = B * S
    NT = N // P
    T = S // P
    C = D // P
    CAP = int(1.25 * N * K / E)
    H1 = rel.shape[0]
    DK = D // H1
    WIDTH = rel.shape[1] - 1
    SCALE1 = DK ** -0.5
    assert (T, C, NT, CAP) == (2, 2, 16, 320)

    stack = ExitStack()
    scratch_rel = nc.dram_tensor("scratch_rel", [H1, P, 4 * P - 1], F32, kind="Internal").ap()
    scratch_xe = nc.dram_tensor("scratch_xe", [E * CAP, D], F32, kind="Internal").ap()
    scratch_oe = nc.dram_tensor("scratch_oe", [E * CAP, D], F32, kind="Internal").ap()

    with stack as keep:
        def alloc(where):
            def sb(name, shape, dt=F32):
                return where.enter_context(nc.sbuf_tensor(name, shape, dt))
            return sb

        sb = alloc(keep)
        ident = sb("ident", [P, P])
        x_all = sb("x_all", [P, NT, D])
        gates = sb("gates", [P, 4])
        tgates = sb("tgates", [P, 4])
        neg_half = sb("neg_half", [P, NT])
        eps = sb("eps", [P, NT])
        row_index = sb("row_index", [P, NT, K], U32)
        row_weight = sb("row_weight", [P, NT, K])
        area = sb("area", [P, AREA])[:]
        carve = carver(area)
        xfT_all = carve([P, C, N])
        router = Router(nc, keep, locals())

        xattn0(nc, keep, locals())
        l1_parts = {n: [sb(f"l1_{n}_{part}", [P, C, D], F32R) for part in ("hi", "lo")] for n in ("wq", "wk", "wv", "wo")}
        swT = sb("swT", [P, C, D], F32R)
        sel = {n: [sb(f"sel{n}_{part}", [P, 4, 2, 4, DK], F32R) for part in ("hi", "lo")] for n in ("q", "k")}
        join = sb("join", [P, P // 32, DK])
        b_cols = sb("b_cols", [P, 2, C])
        b_neg = sb("b_neg", [P, C])
        bv_row = sb("bv_row", [P, D])
        bo1_g = sb("bo1_g", [P, D])
        rel_bias = sb("rel_bias", [P, H1, 3 * P])
        moe(nc, keep, locals())
        xattn1(nc, keep, locals())


def make_tools(nc, phase, keep, name):
    def sb(n, shape, dt=F32):
        return phase.enter_context(nc.sbuf_tensor(f"{name}_{n}", shape, dt))

    def ps(n, shape, dt=F32):
        return phase.enter_context(nc.psum_tensor(f"{name}_{n}", shape, dt))

    def sem(n):
        return keep.enter_context(nc.semaphore(f"{name}_{n}"))

    return sb, ps, sem


def carver(area):
    used = [0]

    def carve(shape, dt=F32):
        size = int(np.prod(shape[1:]))
        part = area[:, used[0]:used[0] + size]
        used[0] += size + size % 2
        assert used[0] <= AREA, used
        if dt != F32:
            part = part.bitcast(dt)
        if len(shape) == 2:
            return part
        dims = "abc"[:len(shape) - 1]
        return part.rearrange(f"p ({' '.join(dims)}) -> p {' '.join(dims)}", **dict(zip(dims, shape[1:])))

    return carve


class Ordered:

    def __init__(self, engine, sem, per_round):
        self.engine, self.sem, self.per_round = engine, sem, per_round
        self.base, self.count = 0, 0

    def start(self, rnd, done=0):
        self.base, self.count = rnd * self.per_round, done

    def done(self, instruction):
        self.count += 1
        instruction.then_inc(self.sem, 1)

    def wait(self):
        self.engine.wait_ge(self.sem, self.base + self.count)


class Router:

    def __init__(self, nc, keep, env):
        E, K, G, LG, T, C, D, S = (env[k] for k in ("E", "K", "G", "LG", "T", "C", "D", "S"))
        self.nc, self.env = nc, env
        _, _, sem = make_tools(nc, keep, keep, "r")
        carve = env["carve"]

        def sb(name, shape, dt=F32):
            return carve(shape, dt)

        self.wgT = sb("wgT", [P, C, E])
        self.count_e = sb("count_e", [P, E])
        self.ones = sb("ones", [P, P])
        self.before = sb("before", [P, P])
        self.x_new = sb("x_new", [P, T, D])
        self.stats = sb("stats", [P, T, 6])
        self.moments = sb("moments", [P, T, 2])
        self.var_eps = sb("var_eps", [P, T])
        self.rstd = sb("rstd", [P, T])
        self.xf = [sb(f"xf{i}", [P, T, D]) for i in range(2)]
        self.xfT = sb("xfT", [P, C, S])
        self.neg_max = sb("neg_max", [P, T])
        self.logits = sb("logits", [P, T, E])
        self.exps = sb("exps", [P, T, E])
        self.total = sb("total", [P, T])
        self.rtotal = sb("rtotal", [P, T])
        self.score = sb("score", [P, T, E])
        self.gmax = sb("gmax", [P, T, G])
        self.gtop = sb("gtop", [P, T, 8])
        self.gidx = sb("gidx", [P, T, 8], U32)
        self.gidx_f = sb("gidx_f", [P, T, LG])
        self.ghot = sb("ghot", [P, T, LG, G])
        self.gkeep = sb("gkeep", [P, T, G])
        self.gpen = sb("gpen", [P, T, G])
        self.masked = sb("masked", [P, T, E])
        self.etop = sb("etop", [P, T, 8])
        self.eidx = sb("eidx", [P, T, 8], U32)
        self.eidx_f = sb("eidx_f", [P, T, K])
        self.wsum = sb("wsum", [P, T])
        self.rwsum = sb("rwsum", [P, T])
        self.ehot = sb("ehot", [P, T, K, E])
        self.epos = sb("epos", [P, T, K, E])
        self.chosen = sb("chosen", [P, T, E])
        self.earlier = sb("earlier", [P, T + 1, E])
        self.weight = sb("weight", [P, T, K])
        self.pos = sb("pos", [P, T, K])
        self.fits = sb("fits", [P, T, K])
        self.dest = sb("dest", [P, T, K])
        self.kept = sb("kept", [P, T, K])
        self.away = sb("away", [P, T, K])
        self.send_index = [sb(f"send_index{i}", [P, T, K], U32) for i in range(2)]
        self.x_kept = sem("x_kept")
        self.moments_ready = sem("moments_ready")
        self.own_pool = sem("own_pool")
        self.rstd_ready = sem("rstd_ready")
        self.xf_ready = sem("xf_ready")
        self.turned = sem("turned")
        self.xfT_ready = sem("xfT_ready")
        self.xfT_kept = sem("xfT_kept")
        self.logits_ready = sem("logits_ready")
        self.shifted_ready = sem("shifted_ready")
        self.exps_ready = sem("exps_ready")
        self.chosen_ready = sem("chosen_ready")
        self.places_ready = sem("places_ready")
        self.index_ready = sem("index_ready")
        self.places_used = sem("places_used")
        self.scattered = [sem(f"scattered{i}") for i in range(2)]
        self.own_dve = sem("own_dve")
        self.seen = sem("seen")
        self.tables_ready = sem("tables_ready")
        self.wgT_ready = sem("wgT_ready")
        self.E, self.K, self.G, self.LG, self.T, self.C, self.S = E, K, G, LG, T, C, S
        self.EG = E // G
        self.CAP = env["CAP"]

    def on_vector(self, dve):
        self.dve = dve
        self.own = Ordered(dve, self.own_dve, ROUTE_STEPS)

    def step(self, instruction):
        self.own.done(instruction)
        self.own.wait()

    def wait_sent(self, eng, b, p):
        eng.wait_ge(self.scattered[p], 8 * self.T * self.K * (b - p) + 16 * self.T * self.K)


    def moments_of(self, b):
        nc, T = self.nc, self.T
        self.own.start(b)
        for t in range(T):
            self.own.done(nc.vector.bn_stats(self.stats[:, t, :], self.x_new[:, t, :]))
        self.own.wait()
        self.dve.sem_inc(self.seen, 1)
        for t in range(T):
            nc.vector.bn_aggr(self.moments[:, t, :], self.stats[:, t, :]).then_inc(self.moments_ready, 1)

    def normalise(self, b, p):
        nc, T = self.nc, self.T
        self.own.start(b, T)
        self.dve.wait_ge(self.rstd_ready, b + 1)
        for t in range(T):
            nc.vector.tensor_scalar(self.xf[p][:, t, :], self.x_new[:, t, :],
                                    self.moments[:, t, 0:1], self.rstd[:, t:t + 1], ALU.subtract, ALU.mult).then_inc(self.xf_ready, 1)

    def shift(self, b, logits):
        nc, T, E = self.nc, self.T, self.E
        raw = logits.rearrange("p (t e) -> p t e", e=E)
        self.dve.wait_ge(self.logits_ready, b + 1)
        self.step(nc.vector.tensor_reduce(self.neg_max[:], raw, AX.X, ALU.max, negate=True))
        nc.vector.tensor_tensor(self.logits[:], raw, self.neg_max[:].unsqueeze(2).to_broadcast([P, T, E]), ALU.add).then_inc(self.shifted_ready, 1)

    def groups(self, b):
        nc, T, E, G, LG = self.nc, self.T, self.E, self.G, self.LG
        self.dve.wait_ge(self.exps_ready, b + 1)
        self.step(nc.vector.tensor_reduce(self.total[:], self.exps[:], AX.X, ALU.add))
        self.step(nc.vector.reciprocal(self.rtotal[:], self.total[:]))
        self.step(nc.vector.tensor_tensor(self.score[:], self.exps[:], self.rtotal[:].unsqueeze(2).to_broadcast([P, T, E]), ALU.mult))
        self.step(nc.vector.tensor_reduce(self.gmax[:], self.score[:].rearrange("p t (g e) -> p t g e", g=G), AX.X, ALU.max))
        self.dve.sem_inc(self.seen, 1)
        for t in range(T):
            self.own.done(nc.vector.max(self.gtop[:, t, :], self.gmax[:, t, :]))
        self.own.wait()
        self.dve.sem_inc(self.seen, 1)
        for t in range(T):
            self.own.done(nc.vector.max_index(self.gidx[:, t, :], self.gtop[:, t, :], self.gmax[:, t, :]))
        self.own.wait()
        self.step(nc.vector.tensor_copy(self.gidx_f[:], self.gidx[:, :, 0:LG]))
        self.step(nc.vector.tensor_tensor(self.ghot[:], self.count_e[:, 0:G].unsqueeze(1).unsqueeze(1).to_broadcast([P, T, LG, G]),
                                          self.gidx_f[:].unsqueeze(3).to_broadcast([P, T, LG, G]), ALU.is_equal))
        self.step(nc.vector.tensor_reduce(self.gkeep[:], self.ghot[:].rearrange("p t k g -> p t g k"), AX.X, ALU.add))

    def experts(self, b):
        nc, T, E, K, G = self.nc, self.T, self.E, self.K, self.G
        masked = self.masked[:].rearrange("p t (g e) -> p t g e", g=G)
        spread = [P, T, G, self.EG]
        self.own.done(nc.vector.tensor_scalar(self.gpen[:], self.gkeep[:], -1.0, None, ALU.add))
        self.step(nc.vector.tensor_tensor(masked, self.score[:].rearrange("p t (g e) -> p t g e", g=G),
                                          self.gkeep[:].unsqueeze(3).to_broadcast(spread), ALU.mult))
        self.step(nc.vector.tensor_tensor(masked, masked, self.gpen[:].unsqueeze(3).to_broadcast(spread), ALU.add))
        self.dve.sem_inc(self.seen, 1)
        for t in range(T):
            self.own.done(nc.vector.max(self.etop[:, t, :], self.masked[:, t, :]))
        self.own.wait()
        self.dve.sem_inc(self.seen, 1)
        for t in range(T):
            self.own.done(nc.vector.max_index(self.eidx[:, t, :], self.etop[:, t, :], self.masked[:, t, :]))
        self.own.wait()
        self.step(nc.vector.tensor_copy(self.eidx_f[:], self.eidx[:, :, 0:K]))
        self.step(nc.vector.tensor_tensor(self.ehot[:], self.count_e[:].unsqueeze(1).unsqueeze(1).to_broadcast([P, T, K, E]),
                                          self.eidx_f[:].unsqueeze(3).to_broadcast([P, T, K, E]), ALU.is_equal))
        self.step(nc.vector.tensor_reduce(self.chosen[:], self.ehot[:].rearrange("p t k e -> p t e k"), AX.X, ALU.add))
        for t in range(T):
            self.step(nc.vector.tensor_tensor(self.earlier[:, t + 1, :], self.earlier[:, t, :], self.chosen[:, t, :], ALU.add))
        self.dve.sem_inc(self.chosen_ready, 1)

    def index(self, b, p, places):
        nc, T, E, K, CAP = self.nc, self.T, self.E, self.K, self.CAP
        row_index, row_weight = self.env["row_index"], self.env["row_weight"]
        spread = [P, T, K, E]
        self.own.done(nc.vector.tensor_reduce(self.wsum[:], self.etop[:, :, 0:K], AX.X, ALU.add))
        self.dve.wait_ge(self.places_ready, b + 1)
        self.step(nc.vector.tensor_tensor(self.epos[:], self.ehot[:], places.rearrange("p (t e) -> p t e", e=E).unsqueeze(2).to_broadcast(spread), ALU.mult))
        self.dve.sem_inc(self.places_used, 1)
        self.own.done(nc.vector.tensor_scalar(self.wsum[:], self.wsum[:], 1e-9, None, ALU.add))
        self.own.done(nc.vector.tensor_copy(self.earlier[:, 0, :], self.earlier[:, T, :]))
        self.step(nc.vector.tensor_reduce(self.pos[:], self.epos[:], AX.X, ALU.add))
        self.own.done(nc.vector.reciprocal(self.rwsum[:], self.wsum[:]))
        self.own.done(nc.vector.tensor_scalar(self.fits[:], self.pos[:], float(CAP), None, ALU.is_lt))
        self.step(nc.vector.scalar_tensor_tensor(out=self.dest[:], in0=self.eidx_f[:], scalar=float(CAP), in1=self.pos[:], op0=ALU.mult, op1=ALU.add))
        self.own.done(nc.vector.tensor_tensor(self.kept[:], self.dest[:], self.fits[:], ALU.mult))
        self.own.done(nc.vector.tensor_tensor(self.weight[:], self.etop[:, :, 0:K], self.rwsum[:].unsqueeze(2).to_broadcast([P, T, K]), ALU.mult))
        self.step(nc.vector.tensor_scalar(self.away[:], self.fits[:], -FAR, FAR, ALU.mult, ALU.add))
        nc.vector.tensor_tensor(self.send_index[p][:], self.kept[:], self.away[:], ALU.add).then_inc(self.index_ready, 1)
        self.own.done(nc.vector.tensor_tensor(row_weight[:, bass.ds(T * b, T), :], self.weight[:], self.fits[:], ALU.mult))
        self.own.done(nc.vector.tensor_copy(row_index[:, bass.ds(T * b, T), :], self.kept[:]))
        assert self.own.count == ROUTE_STEPS


    def tables(self, pool):
        nc = self.nc
        nc.gpsimd.iota(self.count_e[:], [[1, self.E]], base=0, channel_multiplier=0,
                       allow_small_or_imprecise_dtypes=True).then_inc(self.tables_ready, 1)
        nc.gpsimd.memset(self.ones[:], 1.0).then_inc(self.tables_ready, 1)
        nc.gpsimd.memset(self.earlier[:, 0, :], 0.0).then_inc(self.tables_ready, 1)
        pool.wait_ge(self.tables_ready, 3)
        nc.gpsimd.affine_select(out=self.before[:], in_=self.ones[:], compare_op=ALU.is_gt, fill=0.0, base=0,
                                pattern=[[1, P]], channel_multiplier=-1).then_inc(self.tables_ready, 1)

    def rstds(self, pool, b, p):
        nc, T, eps, neg_half = self.nc, self.T, self.env["eps"], self.env["neg_half"]
        pool.wait_ge(self.moments_ready, T * (b + 1))
        nc.gpsimd.tensor_tensor(self.var_eps[:], self.moments[:, :, 1], eps[:, 0:T], ALU.add).then_inc(self.own_pool, 1)
        pool.wait_ge(self.own_pool, b + 1)
        self.wait_sent(pool, b - 2, p)
        nc.gpsimd.tensor_tensor(self.rstd[:], self.var_eps[:], neg_half[:, 0:T], ALU.pow).then_inc(self.rstd_ready, 1)

    def keep_rows(self, pool, b):
        pool.wait_ge(self.moments_ready, self.T * (b + 1))
        x_all = self.env["x_all"]
        self.nc.gpsimd.tensor_copy(x_all[:, bass.ds(self.T * b, self.T), :], self.x_new).then_inc(self.x_kept, 1)

    def keep_turned(self, pool, b):
        pool.wait_ge(self.xfT_ready, b + 1)
        self.nc.gpsimd.tensor_copy(self.env["xfT_all"][:, :, bass.ds(self.S * b, self.S)], self.xfT[:]).then_inc(self.xfT_kept, 1)

    def send(self, pool, b, p):
        scratch_xe = self.env["scratch_xe"]
        pool.wait_ge(self.index_ready, b + 1)
        pool.sem_inc(self.seen, 1)
        for t in range(self.T):
            for k in range(self.K):
                self.nc.gpsimd.indirect_dma_start(
                    out=scratch_xe, out_offset=bass.IndirectOffsetOnAxis(ap=self.send_index[p][:, t, k:k + 1], axis=0),
                    in_=self.xf[p][:, t, :], in_offset=None, bounds_check=self.E * self.CAP - 1, oob_is_err=False).then_inc(self.scattered[p], 16)


    def take_turned(self, act, b, bank):
        act.wait_ge(self.turned, b + 1)
        act.wait_ge(self.xfT_kept, b)
        self.nc.scalar.copy(self.xfT[:].rearrange("p c s -> p (c s)"), bank).then_inc(self.xfT_ready, 1)

    def exp(self, act, b):
        act.wait_ge(self.shifted_ready, b + 1)
        self.nc.scalar.activation(self.exps[:], self.logits[:], ACT.Exp).then_inc(self.exps_ready, 1)


    def turn(self, pe, b, p, bank):
        pe.wait_ge(self.xf_ready, self.T * (b + 1))
        for c in range(self.C):
            for t in range(self.T):
                ins = self.nc.tensor.transpose(bank[:, c * self.S + t * P:c * self.S + (t + 1) * P],
                                               self.xf[p][:, t, c * P:(c + 1) * P], self.env["ident"][:])
        ins.then_inc(self.turned, 1)

    def score_experts(self, pe, b, logits):
        pe.wait_ge(self.xfT_ready, b + 1)
        for t in range(self.T):
            for c in range(self.C):
                ins = self.nc.tensor.matmul(logits[:, t * self.E:(t + 1) * self.E], self.xfT[:, c, t * P:(t + 1) * P], self.wgT[:, c, :],
                                            start=(c == 0), stop=(c == self.C - 1))
        ins.then_inc(self.logits_ready, 1)

    def count_places(self, pe, b, places):
        pe.wait_ge(self.chosen_ready, b + 1)
        T = self.T
        self.nc.tensor.matmul(places, self.before[:], self.chosen[:].rearrange("p t e -> p (t e)"), start=True, stop=False)
        self.nc.tensor.matmul(places, self.ones[:], self.earlier[:, 0:T, :].rearrange("p t e -> p (t e)"), start=False, stop=True).then_inc(self.places_ready, 1)


def xattn0(nc, keep, env):
    x, ctx_in, g_xattn, g_ffn = env["x"], env["ctx_in"], env["g_xattn"], env["g_ffn"]
    ln_l_w, ln_l_b, ln_c_w, ln_c_b = env["ln_l_w"], env["ln_l_b"], env["ln_c_w"], env["ln_c_b"]
    Wq, Wkv, Wo, bo, rel = env["Wq"], env["Wkv"], env["Wo"], env["bo"], env["rel"]
    ident, gates, tgates, neg_half = env["ident"], env["gates"], env["tgates"], env["neg_half"]
    eps = env["eps"]
    scratch_rel, scratch_xe = env["scratch_rel"], env["scratch_xe"]
    B, D, INNER, T, C, PAIRS, D0, H0 = (env[k] for k in ("B", "D", "INNER", "T", "C", "PAIRS", "D0", "H0"))
    H1, WIDTH, E, CAP, router, wg = (env[k] for k in ("H1", "WIDTH", "E", "CAP", "router", "wg"))
    S = T * P
    SC = D0 ** -0.5

    with ExitStack() as phase:
        sb, ps, sem = make_tools(nc, phase, keep, "a")
        ps_scores = ps("scores", [P, 2, 2, T, S])
        ps_pv = ps("pv", [P, 2, 512])
        ps_work = ps("work", [P, 2, 512])

        w2 = [[sb(f"w{n}_{part}", [P, C, INNER], F32R) for part in ("hi", "lo")] for n in ("q", "k", "v")]
        wo = sb("wo", [P, PAIRS, D])
        affine = sb("affine", [P, 4, C])
        bo_g = sb("bo_g", [P, D])
        xin = [sb(f"xin{i}", [P, T, D]) for i in range(2)]
        cin = [sb(f"cin{i}", [P, T, D]) for i in range(2)]
        stats = sb("stats", [P, 3 * T, 6])
        moments = sb("moments", [P, 3 * T, 2])
        var_eps = sb("var_eps", [P, 3 * T])
        rstd = sb("rstd", [P, 3 * T])
        xn = sb("xn", [P, T, D])
        cn = sb("cn", [P, T, D])
        turned = sb("turned", [P, C, S])
        turned2 = [[sb(f"{n}T_{part}", [P, C, S], F32R) for part in ("hi", "lo")] for n in ("ctx", "lat")]
        qkT = [sb(f"{n}T", [P, PAIRS, S]) for n in ("q", "k")]
        v_aug = sb("v", [P, T, H0, D0 + 1])
        clipped = sb("clipped", [P, 2, 2, T, S])
        probs = sb("probs", [P, 2, 2, T, S])
        rsum = sb("rsum", [P, 2, 2, 2])
        o_rows = sb("o_rows", [P, T, INNER])
        oT = sb("oT", [P, PAIRS, S])
        relpad = oT[0:H1, 0:2, :].rearrange("p m s -> p (m s)")[:, 0:4 * P - 1]
        bo_row = oT[:, 2, :]
        wg_rows = oT[0:E, 3, :]
        w_rows = [a.rearrange(pat).rearrange("p (c n) -> p c n", c=C) for a, pat in (
            (clipped[:], "p a b t s -> p (a b t s)"), (probs[:], "p a b t s -> p (a b t s)"), (o_rows[:], "p t n -> p (t n)"))]
        rel_in = sb("rel_in", [H1, WIDTH + 1])
        xb = [sb(f"xb{i}", [P, T, D]) for i in range(2)]
        ZR = 2
        ZERO_DMAS = E * CAP // (P * ZR)
        zeros = sb("zeros", [P, ZR * D])

        wg_loaded = sem("wg_loaded")
        wg_turned = sem("wg_turned")
        w_loaded = [sem(f"w{n}_loaded") for n in "qkv"]
        w_hi = sem("w_hi")
        w_lo = sem("w_lo")
        wo_loaded = sem("wo_loaded")
        params_loaded = sem("params_loaded")
        inputs_loaded = [sem(f"inputs_loaded{i}") for i in range(2)]
        rel_loaded = sem("rel_loaded")
        rel_stored = sem("rel_stored")
        zeroed = sem("zeroed")
        consts_ready = sem("consts_ready")
        relpad_zero = sem("relpad_zero")
        relpad_ready = sem("relpad_ready")
        xb_ready = sem("xb_ready")
        gates_ready = sem("gates_ready")
        bo_ready = sem("bo_ready")
        dve_steps = sem("dve_steps")
        moments_ready = sem("moments_ready")
        pool_steps = sem("pool_steps")
        rstd_ready = sem("rstd_ready")
        lat_ready = sem("lat_ready")
        front_ready = sem("front_ready")
        front_hi = sem("front_hi")
        front_lo = sem("front_lo")
        front_out = sem("front_out")
        turned_out = sem("turned_out")
        scores_ready = sem("scores_ready")
        clip_ready = sem("clip_ready")
        probs_ready = sem("probs_ready")
        pv_ready = sem("pv_ready")
        rsum_ready = sem("rsum_ready")
        o_ready = sem("o_ready")
        oT_ready = sem("oT_ready")
        oT_out = sem("oT_out")
        y_ready = sem("y_ready")
        x_updated = sem("x_updated")

        turned_rows = ps_scores[:, 0, 0].rearrange("p t s -> p (t s)")
        logits, places = (bank.rearrange("p t s -> p (t s)")[:, 0:T * E] for bank in (ps_scores[:, 0, 1], ps_scores[:, 1, 0]))
        BANKS = [ps_work[:, 0, :], ps_work[:, 1, :], ps_pv[:, 0, :], ps_pv[:, 1, :]]
        TURNS = 2
        FRONT = 14
        x_rows = x.rearrange("b (t p) d -> b p t d", p=P)
        c_rows = ctx_in.rearrange("b (t p) d -> b p t d", p=P)

        def batches(eng, front, attend):
            if front:
                front(0, 0)
            attend(0, 0, True, False)
            attend(1, 1, True, True)
            attend(2, 0, True, True)
            with eng.Fori(1, B // 2 - 1) as i:
                attend(2 * i + 1, 1, True, True)
                attend(2 * i + 2, 0, True, True)
            attend(B - 1, 1, False, True)

        block = phase.enter_context(nc.Block())

        @block.sync
        def _(sp):
            def load(b, p):
                sp.dma_start(xin[p][:], x_rows[bass.ds(b, 1)].rearrange("b p t d -> p (b t) d")).then_inc(inputs_loaded[p], 16)
                sp.dma_start(cin[p][:], c_rows[bass.ds(b, 1)].rearrange("b p t d -> p (b t) d")).then_inc(inputs_loaded[p], 16)

            load(0, 0)
            for i, v in enumerate((ln_l_w, ln_l_b, ln_c_w, ln_c_b)):
                sp.dma_start(affine[:, i, :], v.rearrange("(c p) -> p c", p=P), allow_slow_non_contiguous=True).then_inc(params_loaded, 16)
            sp.dma_start(bo_row, bo.partition_broadcast(P)).then_inc(params_loaded, 16)
            for i, v in enumerate((g_xattn, g_ffn)):
                sp.dma_start(gates[:, 2 * i:2 * i + 2], v.partition_broadcast(P)).then_inc(params_loaded, 16)
            sp.dma_start(wg_rows, wg).then_inc(wg_loaded, 16)
            for n, w in enumerate((Wq, Wkv[:, 0:INNER], Wkv[:, INNER:2 * INNER])):
                sp.dma_start(w_rows[n], w.rearrange("(c p) n -> p c n", p=P)).then_inc(w_loaded[n], 16)
            load(1, 1)
            sp.dma_start(wo[:], Wo.rearrange("(j p) n -> p j n", p=P)).then_inc(wo_loaded, 16)
            sp.dma_start(rel_in[:], rel).then_inc(rel_loaded, 16)
            sp.wait_ge(relpad_ready, 1)
            sp.dma_start(scratch_rel, relpad.unsqueeze(1).to_broadcast([H1, P, 4 * P - 1])).then_inc(rel_stored, 16)
            sp.wait_ge(rel_stored, 16)
            sp.wait_ge(consts_ready, 3)
            for j in range(ZERO_DMAS):
                rows = scratch_xe[j * P * ZR:(j + 1) * P * ZR, :]
                sp.dma_start(rows.rearrange("(p r) d -> p (r d)", p=P), zeros[:]).then_inc(zeroed, 16)
            with sp.Fori(1, B // 2) as i:
                for p in range(2):
                    sp.wait_ge(x_updated, (2 * i - 1 + p) * T)
                    load(2 * i + p, p)
            sp.wait_ge(zeroed, 16 * ZERO_DMAS)

        @block.gpsimd
        def _(pool):
            nc.gpsimd.memset(ident[:], 0.0).then_inc(consts_ready, 1)
            nc.gpsimd.memset(neg_half[:], -0.5).then_inc(consts_ready, 1)
            nc.gpsimd.memset(zeros[:], 0.0).then_inc(consts_ready, 1)
            nc.gpsimd.memset(eps[:], EPS).then_inc(consts_ready, 1)
            pool.wait_ge(consts_ready, 4)
            nc.gpsimd.affine_select(out=ident[:], in_=ident[:], compare_op=ALU.not_equal, fill=1.0, base=0,
                                    pattern=[[-1, P]], channel_multiplier=1).then_inc(consts_ready, 1)
            nc.gpsimd.memset(v_aug[:, :, :, D0:D0 + 1], 1.0).then_inc(consts_ready, 1)
            router.tables(pool)
            own = Ordered(pool, pool_steps, 2)

            def rstds(b):
                own.start(b)
                for lo, hi in ((0, 2 * T), (2 * T, 3 * T)):
                    pool.wait_ge(moments_ready, 3 * T * b + hi)
                    own.done(nc.gpsimd.tensor_tensor(var_eps[:, lo:hi], moments[:, lo:hi, 1], eps[:, lo:hi], ALU.add))
                    own.wait()
                    nc.gpsimd.tensor_tensor(rstd[:, lo:hi], var_eps[:, lo:hi], neg_half[:, lo:hi], ALU.pow).then_inc(rstd_ready, 1)

            def route(b, p):
                rstds(b + 2)
                router.keep_turned(pool, b)
                router.send(pool, b, p)
                router.rstds(pool, b + 1, 1 - p)
                router.keep_rows(pool, b + 1)

            rstds(0)
            rstds(1)
            router.rstds(pool, 0, 0)
            router.keep_rows(pool, 0)
            pool.wait_ge(zeroed, 16 * ZERO_DMAS)
            for b in range(2):
                route(b, b)
            with pool.Fori(1, B // 2 - 1) as i:
                for p in range(2):
                    route(2 * i + p, p)

        @block.vector
        def _(dve):
            own = Ordered(dve, dve_steps, 4 * T)

            def front(b, p, step=None):
                if step in (None, 0):
                    own.start(b)
                    dve.wait_ge(inputs_loaded[p], 16 * (b - p) + 32)
                    for n in range(2 * T):
                        own.done(nc.vector.bn_stats(stats[:, n, :], (xin[p], cin[p])[n // T][:, n % T, :]))
                    own.wait()
                    nc.vector.tensor_tensor(xb[p][:], xin[p][:], bo_g[:].unsqueeze(1).to_broadcast([P, T, D]), ALU.add).then_inc(xb_ready, 1)
                    for n in range(2 * T):
                        nc.vector.bn_aggr(moments[:, n, :], stats[:, n, :]).then_inc(moments_ready, 1)
                if step in (None, 1):
                    dve.wait_ge(rstd_ready, 2 * b + 1)
                    if step is not None:
                        dve.wait_ge(front_ready, FRONT * (b - 1) + 2)
                    for t in range(T):
                        own.done(nc.vector.tensor_scalar(xn[:, t, :], xin[p][:, t, :], moments[:, t, 0:1], rstd[:, t:t + 1],
                                                         ALU.subtract, ALU.mult))
                if step in (None, 2):
                    own.wait()
                    for t in range(T):
                        own.done(nc.vector.bn_stats(stats[:, 2 * T + t, :], xn[:, t, :]))
                    own.wait()
                    for t in range(T):
                        nc.vector.tensor_scalar(cn[:, t, :], cin[p][:, t, :], moments[:, T + t, 0:1], rstd[:, T + t:T + t + 1],
                                                ALU.subtract, ALU.mult).then_inc(lat_ready, 1)
                    for t in range(T):
                        nc.vector.bn_aggr(moments[:, 2 * T + t, :], stats[:, 2 * T + t, :]).then_inc(moments_ready, 1)
                if step in (None, 3):
                    dve.wait_ge(rstd_ready, 2 * b + 2)
                    for t in range(T):
                        m = 2 * T + t
                        nc.vector.tensor_scalar(xn[:, t, :], xn[:, t, :], moments[:, m, 0:1], rstd[:, m:m + 1],
                                                ALU.subtract, ALU.mult).then_inc(lat_ready, 1)

            def clip(b, j):
                dve.wait_ge(scores_ready, PAIRS * b + j + 1)
                dve.wait_ge(probs_ready, PAIRS * b + max(j - 1, 0))
                nc.vector.tensor_scalar(clipped[:, j % 2], ps_scores[:, j % 2], CLIP / SC, -CLIP / SC,
                                        ALU.min, ALU.max).then_inc(clip_ready, 1)

            def normalise(b, j):
                dve.wait_ge(pv_ready, PAIRS * b + j + 1)
                if j == 0:
                    dve.wait_ge(oT_ready, 4 * b)
                pv = ps_pv[:, j % 2, 0:T * 2 * (D0 + 1)].rearrange("p (t h d) -> p t h d", t=T, h=2)
                nc.vector.reciprocal(rsum[:, j % 2], pv[:, :, :, D0]).then_inc(rsum_ready, 1)
                dve.wait_ge(rsum_ready, PAIRS * b + j + 1)
                nc.vector.tensor_tensor(o_rows[:, :, 2 * D0 * j:2 * D0 * (j + 1)].rearrange("p t (h d) -> p t h d", h=2),
                                        pv[:, :, :, 0:D0], rsum[:, j % 2].unsqueeze(3).to_broadcast([P, T, 2, D0]),
                                        ALU.mult).then_inc(o_ready, 1)

            def low(b, n):
                dve.wait_ge(front_hi, TURNS * b + n + 1)
                hi, lo = turned2[n]
                nc.vector.tensor_tensor(lo[:], turned[:], hi[:].bitcast(F32), ALU.subtract).then_inc(front_lo, 1)

            def attend(b, p, more, routes):
                for j in range(PAIRS):
                    clip(b, j)
                    if j >= 2:
                        normalise(b, j - 2)
                    if routes and j == 0:
                        router.normalise(b - 1, 1 - p)
                    if more and 1 <= j <= 4:
                        front(b + 1, 1 - p, j - 1)
                if more:
                    low(b + 1, 0)
                    low(b + 1, 1)
                for j in range(PAIRS - 2, PAIRS):
                    normalise(b, j)
                if routes and more:
                    router.shift(b - 1, logits)
                    router.groups(b - 1)
                    router.experts(b - 1)
                    router.index(b - 1, 1 - p, places)
                dve.wait_ge(router.x_kept, b)
                for t in range(T):
                    dve.wait_ge(y_ready, T * b + t + 1)
                    dve.wait_ge(xb_ready, b + 1)
                    nc.vector.scalar_tensor_tensor(router.x_new[:, t, :], ps_work[:, t, 0:D], tgates[:, 0:1], xb[p][:, t, :],
                                                   ALU.mult, ALU.add).then_inc(x_updated, 1)
                if more:
                    dve.wait_ge(x_updated, T * (b + 1))
                    router.moments_of(b)

            router.on_vector(dve)
            dve.wait_ge(gates_ready, 1)
            nc.vector.tensor_scalar(bo_g[:], bo_row, tgates[:, 0:1], None, ALU.mult).then_inc(bo_ready, 1)
            dve.wait_ge(bo_ready, 1)
            front(0, 0)
            low(0, 0)
            low(0, 1)
            dve.wait_ge(rel_loaded, 16)
            nc.vector.memset(relpad, 0.0).then_inc(relpad_zero, 1)
            dve.wait_ge(relpad_zero, 1)
            lead = P + P // 2 - 1
            nc.vector.tensor_scalar(relpad[:, lead:lead + WIDTH + 1], rel_in[:], -1.0, None, ALU.mult).then_inc(relpad_ready, 1)
            for n in range(3):
                dve.wait_ge(w_hi, n + 1)
                nc.vector.tensor_tensor(w2[n][1][:], w_rows[n], w2[n][0][:].bitcast(F32), ALU.subtract).then_inc(w_lo, 1)
            batches(dve, None, attend)

        @block.scalar
        def _(act):
            def front(b, p, first=0, last=FRONT, routes=False):
                for n in range(first, last):
                    act.wait_ge(front_ready, FRONT * b + n + 1)
                    bank = BANKS[n % 4]
                    if n < TURNS:
                        act.wait_ge(front_lo, TURNS * b + n)
                        for c in range(C):
                            nc.scalar.activation(turned[:, c, :], bank[:, c * S:(c + 1) * S], ACT.Identity,
                                                 bias=affine[:, 3 - 2 * n, c:c + 1], scale=affine[:, 2 - 2 * n, c:c + 1]).then_inc(turned_out, 1)
                        act.wait_ge(turned_out, C * (TURNS * b + n + 1))
                        nc.scalar.copy(turned2[n][0][:], turned[:]).then_inc(front_hi, 1)
                    elif n < 10:
                        m = 2 * ((n - 2) % 4)
                        nc.scalar.copy(qkT[(n - 2) // 4][:, m:m + 2, :].rearrange("p m s -> p (m s)"), bank).then_inc(front_out, 1)
                    else:
                        t, half = divmod(n - 10, 2)
                        hs = H0 // 2
                        nc.scalar.copy(v_aug[:, t, half * hs:(half + 1) * hs, 0:D0], bank.rearrange("p (h d) -> p h d", d=D0)).then_inc(front_out, 1)
                    if routes and n == 3:
                        router.take_turned(act, b - 2, turned_rows)
                    if routes and n == 7:
                        router.exp(act, b - 2)

            def attend(b, p, more, routes):
                for j in range(PAIRS):
                    act.wait_ge(clip_ready, PAIRS * b + j + 1)
                    act.wait_ge(pv_ready, PAIRS * b + max(j - 1, 0))
                    nc.scalar.activation(probs[:, j % 2], clipped[:, j % 2], ACT.Exp, scale=SC).then_inc(probs_ready, 1)
                    if more and j in (5, 7):
                        front(b + 1, 1 - p, j // 7, j // 7 + 1)
                if more:
                    front(b + 1, 1 - p, TURNS, FRONT, routes)
                if isinstance(b, int) and b == 0:
                    act.wait_ge(rel_stored, 16)
                for n in range(4):
                    act.wait_ge(oT_ready, 4 * b + n + 1)
                    nc.scalar.copy(oT[:, 2 * n:2 * n + 2, :].rearrange("p m s -> p (m s)"), BANKS[n]).then_inc(oT_out, 1)

            act.wait_ge(params_loaded, 16 * 7)
            nc.scalar.activation(tgates[:], gates[:], ACT.Tanh).then_inc(gates_ready, 1)
            act.wait_ge(wg_turned, 1)
            nc.scalar.copy(router.wgT, ps_work[:, 1, 0:C * E].rearrange("p (c e) -> p c e", c=C)).then_inc(router.wgT_ready, 1)
            front(0, 0, 0, TURNS)
            for n in range(3):
                act.wait_ge(w_loaded[n], 16)
                nc.scalar.copy(w2[n][0][:], w_rows[n]).then_inc(w_hi, 1)
            front(0, 0, TURNS)
            batches(act, None, attend)

        @block.tensor
        def _(pe):
            def product(out, a, b, first=True, last=True):
                nc.tensor.matmul(out, a[0], b[0], start=first, stop=False)
                nc.tensor.matmul(out, a[0], b[1], start=False, stop=False)
                return nc.tensor.matmul(out, a[1], b[0], start=False, stop=last)

            def front(b, p, first=0, last=FRONT, routes=False):
                for n in range(first, last):
                    if routes and n == 2:
                        router.turn(pe, b - 2, p, turned_rows)
                    if routes and n == 5:
                        router.score_experts(pe, b - 2, logits)
                    bank = BANKS[n % 4]
                    if n >= 6:
                        pe.wait_ge(front_out, (FRONT - TURNS) * b + n - 5)
                    elif 2 <= n < 4:
                        pe.wait_ge(o_ready, PAIRS * b)
                    if n < 2:
                        if isinstance(b, int) and b == 0:
                            pe.wait_ge(router.wgT_ready, 1)
                        else:
                            pe.wait_ge(x_updated, T * (b - 1))
                        pe.wait_ge(lat_ready, 2 * T * b + (T, 2 * T)[n])
                        rows = (cn, xn)[n]
                        for c in range(C):
                            for t in range(T):
                                ins = nc.tensor.transpose(bank[:, c * S + t * P:c * S + (t + 1) * P],
                                                          rows[:, t, c * P:(c + 1) * P], ident[:])
                    elif n < 10:
                        src = (turned2[1], turned2[0])[(n - 2) // 4]
                        pe.wait_ge(front_lo, TURNS * (b + 1))
                        if isinstance(b, int) and b == 0 and n in (2, 6):
                            pe.wait_ge(w_lo, n // 6 + 1)
                        for k in range(2):
                            m = 2 * ((n - 2) % 4) + k
                            for c in range(C):
                                ins = product(bank[:, k * S:(k + 1) * S], [w[:, c, m * P:(m + 1) * P] for w in w2[(n - 2) // 4]],
                                              [a[:, c, :] for a in src], c == 0, c == C - 1)
                    else:
                        if isinstance(b, int) and b == 0:
                            pe.wait_ge(w_lo, 3)
                        t, half = divmod(n - 10, 2)
                        for c in range(C):
                            ins = product(bank, [a[:, c, t * P:(t + 1) * P] for a in turned2[0]],
                                          [w[:, c, half * 512:(half + 1) * 512] for w in w2[2]], c == 0, c == C - 1)
                    ins.then_inc(front_ready, 1)

            def scores(b, p, j):
                pe.wait_ge(clip_ready, PAIRS * b + max(j - 1, 0))
                for h in range(2):
                    rows = slice(h * D0, (h + 1) * D0)
                    for t in range(T):
                        ins = nc.tensor.matmul(ps_scores[:, j % 2, h, t, :], qkT[1][rows, j, t * P:(t + 1) * P], qkT[0][rows, j, :],
                                               start=True, stop=True)
                ins.then_inc(scores_ready, 1)

            def values(b, p, j):
                pe.wait_ge(probs_ready, PAIRS * b + j + 1)
                pe.wait_ge(o_ready, PAIRS * b + max(j - 1, 0))
                for tq in range(T):
                    for h in range(2):
                        at = (2 * tq + h) * (D0 + 1)
                        for t in range(T):
                            ins = nc.tensor.matmul(ps_pv[:, j % 2, at:at + D0 + 1], probs[:, j % 2, h, t, tq * P:(tq + 1) * P],
                                                   v_aug[:, t, 2 * j + h, :], start=(t == 0), stop=(t == T - 1))
                ins.then_inc(pv_ready, 1)

            def attend(b, p, more, routes):
                pe.wait_ge(front_out, (FRONT - TURNS) * (b + 1))
                if routes:
                    pe.wait_ge(router.places_used, b - 1)
                scores(b, p, 0)
                scores(b, p, 1)
                for j in range(PAIRS):
                    if j + 2 < PAIRS:
                        scores(b, p, j + 2)
                    values(b, p, j)
                    if more and j in (4, 5):
                        front(b + 1, 1 - p, j - 4, j - 3)
                if more:
                    front(b + 1, 1 - p, TURNS, FRONT, routes)
                    pe.wait_ge(front_out, (FRONT - TURNS) * (b + 2))
                else:
                    pe.wait_ge(x_updated, T * b)
                pe.wait_ge(o_ready, PAIRS * b + PAIRS)
                for n in range(4):
                    for k in range(2):
                        m = 2 * n + k
                        for t in range(T):
                            ins = nc.tensor.transpose(BANKS[n][:, k * S + t * P:k * S + (t + 1) * P],
                                                      o_rows[:, t, m * P:(m + 1) * P], ident[:])
                    ins.then_inc(oT_ready, 1)
                if more and routes:
                    router.count_places(pe, b - 1, places)
                pe.wait_ge(oT_out, 4 * b + 4)
                if isinstance(b, int) and b == 0:
                    pe.wait_ge(wo_loaded, 16)
                for t in range(T):
                    for m in range(PAIRS):
                        ins = nc.tensor.matmul(ps_work[:, t, 0:D], oT[:, m, t * P:(t + 1) * P], wo[:, m, :],
                                               start=(m == 0), stop=(m == PAIRS - 1))
                    ins.then_inc(y_ready, 1)

            pe.wait_ge(consts_ready, 5)
            pe.wait_ge(wg_loaded, 16)
            for c in range(C):
                ins = nc.tensor.transpose(ps_work[:, 1, c * E:(c + 1) * E], wg_rows[:, c * P:(c + 1) * P], ident[0:E, 0:E])
            ins.then_inc(wg_turned, 1)
            pe.wait_ge(consts_ready, 6)
            pe.wait_ge(router.tables_ready, 4)
            batches(pe, front, attend)


def moe(nc, keep, env):
    w1, w2, w3, sw1, sw2, sw3, router, xfT = (env[k] for k in ("w1", "w2", "w3", "sw1", "sw2", "sw3", "router", "xfT_all"))
    x_all, ident, tgates = (env[k] for k in ("x_all", "ident", "tgates"))
    scratch_xe, scratch_oe = env["scratch_xe"], env["scratch_oe"]
    E, CAP, NT, D, F, C = (env[k] for k in ("E", "CAP", "NT", "D", "F", "C"))
    Wq1, bq1, Wk1, bk1, Wv1, bv1, Wo1, bo1, sign_w = (env[k] for k in ("Wq1", "bq1", "Wk1", "bk1", "Wv1", "bv1", "Wo1", "bo1", "sign_w"))
    l1_parts, swT, sel, join, b_cols, b_neg, bv_row, bo1_g = (env[k] for k in ("l1_parts", "swT", "sel", "join", "b_cols", "b_neg", "bv_row", "bo1_g"))
    DK, SCALE1, H1, rel_bias, scratch_rel = (env[k] for k in ("DK", "SCALE1", "H1", "rel_bias", "scratch_rel"))
    TG = 4
    NG = NT // TG
    GS = TG * P
    FC = F // P
    LAST = env["B"] - 1
    assert (LAST % 2, NG) == (1, 4)
    tails = ((0, 2, P), (2, 3, CAP - 2 * P))

    with ExitStack() as phase:
        sb, ps, sem = make_tools(nc, phase, keep, "m")
        ps_turn = ps("turn", [P, C, 512])
        ps_h = ps("h", [P, 2, FC, 512])
        ps_out = ps("out", [P, 2, 512])

        T = NT // env["B"]
        turned_rows = ps_turn[:, 0, :]
        logits = places = ps_turn[:, 1, 0:T * E]
        s1 = sb("s1", [P, C, F])
        s3 = sb("s3", [P, C, F])
        s2 = sb("s2", [P, FC, D])
        act_t = sb("act_t", [P, FC, GS])
        act_a = sb("act_a", [P, FC, GS])
        gated = sb("gated", [P, FC, GS])
        w1s = [sb(f"w1_{i}", [P, C, F]) for i in range(2)]
        w3s = [sb(f"w3_{i}", [P, C, F]) for i in range(2)]
        w2s = [sb(f"w2_{i}", [P, FC, D]) for i in range(2)]
        xe = [sb(f"xe{i}", [P, 3, D]) for i in range(2)]
        w13_2 = [[[sb(f"{n}_{part}{i}", [P, C, F], F32R) for part in ("hi", "lo")] for n in ("w1", "w3")] for i in range(2)]
        w2_2 = [[sb(f"w2_{part}{i}", [P, FC, D], F32R) for part in ("hi", "lo")] for i in range(2)]
        xeT2 = [[sb(f"xeT_{part}{i}", [P, C, CAP], F32R) for part in ("hi", "lo")] for i in range(2)]
        e_tanh = sb("e_tanh", [P, FC, CAP])
        e_a = sb("e_a", [P, FC, CAP])
        e_gated = sb("e_gated", [P, FC, CAP])
        gated2 = [[sb(f"e_gated_{part}{i}", [P, FC, CAP], F32R) for part in ("hi", "lo")] for i in range(2)]
        oe = [sb(f"oe{i}", [P, 3, D]) for i in range(2)]

        l1_rows = {n: sb(f"{n}_rows", [P, C, D]) for n in ("wq", "wk", "wv", "wo")}
        l1_rows["sw"] = e_a[:].rearrange("p c n -> p (c n)")[:, 0:C * D].rearrange("p (c d) -> p c d", d=D)
        sw_pos, sw_neg = (sb(n, [P, C, D])[:] for n in ("sw_pos", "sw_neg"))
        sw_sign = sw_pos

        bo1_row = e_tanh[:].rearrange("p c n -> p (c n)")[:, 0:D]

        shared_loaded = sem("shared_loaded")
        l1_loaded = sem("l1_loaded")
        own_dve = sem("own_dve")
        bias_loaded = sem("bias_loaded")
        sel_ready = sem("sel_ready")
        hi_ready = sem("hi_ready")
        lo_ready = sem("lo_ready")
        sign_ready = sem("sign_ready")
        sign_turned = sem("sign_turned")
        swT_ready = sem("swT_ready")
        w13_loaded = [sem(f"w13_loaded{i}") for i in range(2)]
        w2_loaded = [sem(f"w2_loaded{i}") for i in range(2)]
        xe_loaded = [sem(f"xe_loaded{i}") for i in range(2)]
        stored = [sem(f"stored{i}") for i in range(2)]
        sh_ready = sem("sh_ready")
        sh_tanh = sem("sh_tanh")
        sh_a = sem("sh_a")
        sh_gated = sem("sh_gated")
        z_ready = sem("z_ready")
        z_out = sem("z_out")
        e_turned = sem("e_turned")
        xeT_hi = sem("xeT_hi")
        xeT_lo = sem("xeT_lo")
        w13_hi = sem("w13_hi")
        w1_lo = sem("w1_lo")
        w3_lo = sem("w3_lo")
        w2_hi = sem("w2_hi")
        w2_lo = sem("w2_lo")
        gated_hi = sem("gated_hi")
        gated_lo = sem("gated_lo")
        h_ready = sem("h_ready")
        tanh_ready = sem("tanh_ready")
        a_ready = sem("a_ready")
        gated_ready = sem("gated_ready")
        o_ready = sem("o_ready")
        oe_ready = sem("oe_ready")

        def experts(eng, expert):
            for e in range(3):
                expert(e, e % 2)
            with eng.Fori(1, E // 2 - 2) as i:
                for p in (1, 0):
                    expert(2 * i + 2 - p, p)
            expert(E - 3, 1)
            expert(E - 2, 0, True, False)
            expert(E - 1, 1, False, False)

        block = phase.enter_context(nc.Block())

        @block.sync
        def _(sp):
            def load_w13(e, p):
                for w, s in ((w1, w1s), (w3, w3s)):
                    sp.dma_start(s[p][:], w[bass.ds(e, 1)].rearrange("e (c p) n -> p (e c) n", p=P)).then_inc(w13_loaded[p], 16)

            def load_w2(e, p):
                sp.dma_start(w2s[p][:], w2[bass.ds(e, 1)].rearrange("e (c p) n -> p (e c) n", p=P)).then_inc(w2_loaded[p], 16)

            def load_xe(e, p):
                for lo, hi, rows in tails:
                    src = scratch_xe[bass.ds(e * CAP + lo * P, (hi - lo) * rows)].rearrange("(c p) d -> p c d", p=rows)
                    sp.dma_start(xe[p][0:rows, lo:hi, :], src).then_inc(xe_loaded[p], 16)

            for w, s in ((sw1, s1), (sw3, s3), (sw2, s2)):
                sp.dma_start(s[:], w.rearrange("(c p) n -> p c n", p=P)).then_inc(shared_loaded, 16)
            load_w13(0, 0)
            load_w13(1, 1)
            load_w2(0, 0)
            for w, n in ((Wq1, "wq"), (Wk1, "wk"), (Wv1, "wv"), (Wo1, "wo"), (sign_w, "sw")):
                sp.dma_start(l1_rows[n][:], w.rearrange("(c p) n -> p c n", p=P)).then_inc(l1_loaded, 16)
            for r, d in ((bv1, bv_row[:]), (bo1, bo1_row)):
                sp.dma_start(d, r.partition_broadcast(P)).then_inc(l1_loaded, 16)
            for n, r in enumerate((bq1, bk1)):
                sp.dma_start(b_cols[:, n, :], r.rearrange("(c p) -> p c", p=P), allow_slow_non_contiguous=True).then_inc(l1_loaded, 16)
            sp.dma_start(rel_bias[:], bass.AP(scratch_rel.tensor, P - 1, [[4 * P - 2, P], [P * (4 * P - 1), H1], [1, 3 * P]])).then_inc(bias_loaded, 16)
            sp.wait_ge(bias_loaded, 16)
            for p in range(2):
                router.wait_sent(sp, LAST - 1 + p, p)
            load_xe(0, 0)
            load_xe(1, 1)

            def load_expert(e, p):
                sp.wait_ge(e_turned, e - 1)
                load_xe(e, p)
                sp.wait_ge(w1_lo, e - 1)
                sp.wait_ge(w3_lo, e - 1)
                load_w13(e, p)
                sp.wait_ge(w2_lo, e - 2)
                load_w2(e - 1, 1 - p)

            for e in (2, 3):
                load_expert(e, e % 2)
            with sp.Fori(2, E // 2) as i:
                for p in range(2):
                    load_expert(2 * i + p, p)
            sp.wait_ge(w2_lo, E - 2)
            load_w2(E - 1, 1)

        @block.gpsimd
        def _(pool):
            router.keep_turned(pool, LAST - 1)
            router.rstds(pool, LAST, 1)
            router.keep_rows(pool, LAST)
            router.keep_turned(pool, LAST)
            router.send(pool, LAST - 1, 0)
            router.send(pool, LAST, 1)
            for p in range(2):
                router.wait_sent(pool, LAST - 1 + p, p)

            def low_w3(e, p):
                pool.wait_ge(w13_hi, 2 * (e + 1))
                nc.gpsimd.tensor_tensor(w13_2[p][1][1][:], w3s[p][:], w13_2[p][1][0][:].bitcast(F32), ALU.subtract).then_inc(w3_lo, 1)

            def split_w2(e, p):
                pool.wait_ge(w2_loaded[p], 8 * (e - p) + 16)
                pool.wait_ge(o_ready, 2 * max(e - 1, 0) if isinstance(e, int) else 2 * (e - 1))
                pool.sem_inc(router.seen, 1)
                nc.gpsimd.tensor_copy(w2_2[p][0][:], w2s[p][:]).then_inc(w2_hi, 1)
                pool.wait_ge(w2_hi, e + 1)
                nc.gpsimd.tensor_tensor(w2_2[p][1][:], w2s[p][:], w2_2[p][0][:].bitcast(F32), ALU.subtract).then_inc(w2_lo, 1)

            low_w3(0, 0)
            low_w3(1, 1)
            split_w2(0, 0)
            low_w3(2, 0)
            for e in (1, 2):
                split_w2(e, e % 2)
                low_w3(e + 2, e % 2)
            with pool.Fori(1, E // 2 - 2) as i:
                for p in (1, 0):
                    e = 2 * i + 2 - p
                    split_w2(e, p)
                    low_w3(e + 2, p)
            split_w2(E - 3, 1)
            low_w3(E - 1, 1)
            split_w2(E - 2, 0)
            split_w2(E - 1, 1)

        @block.vector
        def _(dve):
            router.on_vector(dve)

            def layer1_selectors():
                blocks = {("q", 0): (0, 1), ("q", 1): (2, 3), ("k", 0): (0, 2), ("k", 1): (1, 3)}
                for n in ("q", "k"):
                    for part in range(2):
                        nc.vector.memset(sel[n][part][:].bitcast(F32), 0.0).then_inc(own_dve, 1)
                dve.wait_ge(own_dve, 4)
                for (n, part), at in blocks.items():
                    for k in at:
                        nc.vector.tensor_copy(sel[n][part][:, :, :, k, :], ident[:].rearrange("p (m h i) -> p m h i", m=4, h=2)).then_inc(sel_ready, 1)
                parts = ident[:].rearrange("p (j a d) -> p j a d", a=2, d=DK)
                nc.vector.tensor_tensor(join[:], parts[:, :, 0, :], parts[:, :, 1, :], ALU.add).then_inc(sel_ready, 1)

            def layer1_weights():
                dve.wait_ge(l1_loaded, 16 * 9)
                nc.vector.tensor_scalar(l1_rows["wq"][:], l1_rows["wq"][:], -SCALE1, None, ALU.mult).then_inc(own_dve, 1)
                nc.vector.tensor_scalar(b_neg[:], b_cols[:, 0, :], -SCALE1, None, ALU.mult).then_inc(lo_ready, 1)
                nc.vector.tensor_scalar(bo1_g[:], bo1_row, tgates[:, 1:2], None, ALU.mult).then_inc(lo_ready, 1)
                nc.vector.tensor_scalar(sw_pos, l1_rows["sw"][:], 0.0, None, ALU.is_gt).then_inc(own_dve, 1)
                nc.vector.tensor_scalar(sw_neg, l1_rows["sw"][:], 0.0, None, ALU.is_lt).then_inc(own_dve, 1)
                dve.wait_ge(own_dve, 7)
                nc.vector.tensor_tensor(sw_sign, sw_pos, sw_neg, ALU.subtract).then_inc(sign_ready, 1)
                for n in l1_parts:
                    nc.vector.tensor_copy(l1_parts[n][0][:], l1_rows[n][:]).then_inc(hi_ready, 1)
                for i, n in enumerate(l1_parts):
                    dve.wait_ge(hi_ready, i + 1)
                    nc.vector.tensor_tensor(l1_parts[n][1][:], l1_rows[n][:], l1_parts[n][0][:].bitcast(F32), ALU.subtract).then_inc(lo_ready, 1)

            def low_w1(e, p):
                dve.wait_ge(w13_hi, 2 * e + 1)
                nc.vector.tensor_tensor(w13_2[p][0][1][:], w1s[p][:], w13_2[p][0][0][:].bitcast(F32), ALU.subtract).then_inc(w1_lo, 1)

            def add_shared(g):
                for half in range(2):
                    dve.wait_ge(z_ready, 2 * g + half + 1)
                    t = g * TG + 2 * half
                    at = x_all[:, t:t + 2, :].rearrange("p t d -> p (t d)")
                    nc.vector.scalar_tensor_tensor(out=at, in0=ps_out[:, half, :], scalar=tgates[:, 2:3], in1=at,
                                                   op0=ALU.mult, op1=ALU.add).then_inc(z_out, 1)

            def shared(g):
                dve.wait_ge(sh_tanh, g + 1)
                if g:
                    dve.wait_ge(sh_gated, FC * g)
                for m in range(FC):
                    nc.vector.scalar_tensor_tensor(out=act_a[:, m, :], in0=act_t[:, m, :], scalar=1.0, in1=ps_h[:, 0, m, :],
                                                   op0=ALU.add, op1=ALU.mult).then_inc(sh_a, 1)
                if g:
                    add_shared(g - 1)
                dve.wait_ge(sh_a, FC * (g + 1))
                dve.wait_ge(sh_ready, 2 * g + 2)
                for m in range(FC):
                    nc.vector.scalar_tensor_tensor(out=gated[:, m, :], in0=act_a[:, m, :], scalar=0.5, in1=ps_h[:, 1, m, :],
                                                   op0=ALU.mult, op1=ALU.mult).then_inc(sh_gated, 1)

            layer1_selectors()
            router.own.start(LAST - 1, T)
            router.shift(LAST - 1, logits)
            router.groups(LAST - 1)
            shared(0)
            router.experts(LAST - 1)
            router.index(LAST - 1, 0, places)
            router.moments_of(LAST)
            router.normalise(LAST, 1)
            shared(1)
            layer1_weights()
            router.shift(LAST, logits)
            router.groups(LAST)
            router.experts(LAST)
            shared(2)
            router.index(LAST, 1, places)
            low_w1(0, 0)
            low_w1(1, 1)
            shared(3)
            dve.wait_ge(router.x_kept, LAST + 1)
            add_shared(3)

            def gate(e):
                dve.wait_ge(tanh_ready, e + 1)
                dve.wait_ge(gated_lo, e)
                for m in range(FC):
                    nc.vector.scalar_tensor_tensor(out=e_a[:, m, :], in0=e_tanh[:, m, :], scalar=1.0, in1=ps_h[:, 0, m, 0:CAP],
                                                   op0=ALU.add, op1=ALU.mult).then_inc(a_ready, 1)
                dve.wait_ge(a_ready, FC * (e + 1))
                dve.wait_ge(h_ready, 2 * e + 2)
                for m in range(FC):
                    nc.vector.scalar_tensor_tensor(out=e_gated[:, m, :], in0=e_a[:, m, :], scalar=0.5, in1=ps_h[:, 1, m, 0:CAP],
                                                   op0=ALU.mult, op1=ALU.mult).then_inc(gated_ready, 1)

            def low_inputs(e, p):
                dve.wait_ge(xeT_hi, e + 1)
                nc.vector.tensor_tensor(xeT2[p][1][:], ps_turn[:, :, 0:CAP], xeT2[p][0][:].bitcast(F32), ALU.subtract).then_inc(xeT_lo, 1)

            def low_gated(e, p):
                dve.wait_ge(gated_hi, e + 1)
                nc.vector.tensor_tensor(gated2[p][1][:], e_gated[:], gated2[p][0][:].bitcast(F32), ALU.subtract).then_inc(gated_lo, 1)

            def expert(e, p, inputs=True, weights=True):
                gate(e)
                if inputs:
                    low_inputs(e + 1, 1 - p)
                low_gated(e, p)
                if weights:
                    low_w1(e + 2, p)

            low_inputs(0, 0)
            experts(dve, expert)

        @block.scalar
        def _(act):
            def shared(g):
                act.wait_ge(sh_ready, 2 * g + 1)
                act.wait_ge(sh_a, FC * g)
                nc.scalar.activation(act_t[:], ps_h[:, 0], ACT.Tanh, scale=0.5).then_inc(sh_tanh, 1)

            def high_weights(e, p):
                act.wait_ge(w13_loaded[p], 16 * (e - p) + 32)
                for n, w in enumerate((w1s, w3s)):
                    nc.scalar.copy(w13_2[p][n][0][:], w[p][:]).then_inc(w13_hi, 1)

            router.take_turned(act, LAST - 1, turned_rows)
            shared(0)
            router.exp(act, LAST - 1)
            shared(1)
            router.take_turned(act, LAST, turned_rows)
            router.exp(act, LAST)
            shared(2)
            high_weights(0, 0)
            high_weights(1, 1)
            act.wait_ge(sign_turned, 1)
            nc.scalar.copy(swT[:].rearrange("p c s -> p (c s)"), turned_rows).then_inc(swT_ready, 1)
            shared(3)

            def take_inputs(e, p):
                act.wait_ge(e_turned, e + 1)
                nc.scalar.copy(xeT2[p][0][:], ps_turn[:, :, 0:CAP]).then_inc(xeT_hi, 1)

            def high_gated(e, p):
                act.wait_ge(gated_ready, FC * (e + 1))
                nc.scalar.copy(gated2[p][0][:], e_gated[:]).then_inc(gated_hi, 1)

            def tanh(e):
                act.wait_ge(h_ready, 2 * e + 1)
                nc.scalar.activation(e_tanh[:], ps_h[:, 0, :, 0:CAP], ACT.Tanh, scale=0.5).then_inc(tanh_ready, 1)

            def put_outputs(e, p):
                for n, (lo, hi, rows) in enumerate(tails):
                    act.wait_ge(o_ready, 2 * e + n + 1)
                    if n == 0:
                        act.wait_ge(stored[p], 16 * (e - p))
                    nc.scalar.copy(oe[p][0:rows, lo:hi, :], ps_out[0:rows, n, 0:(hi - lo) * D].rearrange("p (c d) -> p c d", d=D)).then_inc(oe_ready, 1)
                for n, (lo, hi, rows) in enumerate(tails):
                    act.wait_ge(oe_ready, 2 * e + n + 1)
                    dst = scratch_oe[bass.ds(e * CAP + lo * P, (hi - lo) * rows)].rearrange("(c p) d -> p c d", p=rows)
                    act.dma_start(dst, oe[p][0:rows, lo:hi, :]).then_inc(stored[p], 16)

            def expert(e, p, inputs=True, weights=True):
                tanh(e)
                if inputs:
                    take_inputs(e + 1, 1 - p)
                high_gated(e, p)
                if not (isinstance(e, int) and e == 0):
                    put_outputs(e - 1, 1 - p)
                if weights:
                    high_weights(e + 2, p)

            take_inputs(0, 0)
            experts(act, expert)
            put_outputs(E - 1, 1)
            for p in range(2):
                act.wait_ge(stored[p], 16 * E)

        @block.tensor
        def _(pe):
            def shared_h(g, w):
                pe.wait_ge((sh_a, sh_gated)[w], FC * g)
                for m in range(FC):
                    for c in range(C):
                        ins = nc.tensor.matmul(ps_h[:, w, m, :], (s1, s3)[w][:, c, m * P:(m + 1) * P], xfT[:, c, g * GS:(g + 1) * GS],
                                               start=(c == 0), stop=(c == C - 1))
                ins.then_inc(sh_ready, 1)

            def shared_out(g):
                pe.wait_ge(sh_gated, FC * (g + 1))
                for half in range(2):
                    if g:
                        pe.wait_ge(z_out, 2 * (g - 1) + half + 1)
                    for k in range(2):
                        t = 2 * half + k
                        for m in range(FC):
                            ins = nc.tensor.matmul(ps_out[:, half, k * D:(k + 1) * D], gated[:, m, t * P:(t + 1) * P], s2[:, m, :],
                                                   start=(m == 0), stop=(m == FC - 1))
                    ins.then_inc(z_ready, 1)

            router.turn(pe, LAST - 1, 0, turned_rows)
            pe.wait_ge(shared_loaded, 48)
            shared_h(0, 0)
            router.score_experts(pe, LAST - 1, logits)
            shared_h(0, 1)
            shared_h(1, 0)
            shared_out(0)
            router.count_places(pe, LAST - 1, places)
            shared_h(1, 1)
            router.turn(pe, LAST, 1, turned_rows)
            shared_h(2, 0)
            pe.wait_ge(router.places_used, LAST)
            router.score_experts(pe, LAST, logits)
            shared_out(1)
            shared_h(2, 1)
            pe.wait_ge(router.xfT_kept, LAST + 1)
            shared_h(3, 0)
            router.count_places(pe, LAST, places)
            shared_out(2)
            pe.wait_ge(sign_ready, 1)
            for c in range(C):
                for t in range(C):
                    ins = nc.tensor.transpose(turned_rows[:, c * D + t * P:c * D + (t + 1) * P], sw_sign[:, t, c * P:(c + 1) * P], ident[:])
            ins.then_inc(sign_turned, 1)
            shared_h(3, 1)
            shared_out(3)

            def turn(e, p):
                pe.wait_ge(xe_loaded[p], 16 * (e - p) + 32)
                pe.wait_ge(xeT_lo, e)
                for c in range(C):
                    for chunk in range(3):
                        rows = min(P, CAP - chunk * P)
                        ins = nc.tensor.transpose(ps_turn[:, c, chunk * P:chunk * P + rows],
                                                  xe[p][0:rows, chunk, c * P:(c + 1) * P], ident[0:rows, 0:rows])
                ins.then_inc(e_turned, 1)

            def product(out, a, b, first=True, last=True):
                nc.tensor.matmul(out, a[0], b[0], start=first, stop=False)
                nc.tensor.matmul(out, a[0], b[1], start=False, stop=False)
                return nc.tensor.matmul(out, a[1], b[0], start=False, stop=last)

            def hidden(e, p):
                pe.wait_ge(w1_lo, e + 1)
                pe.wait_ge(w3_lo, e + 1)
                pe.wait_ge(xeT_lo, e + 1)
                for w in range(2):
                    pe.wait_ge((a_ready, gated_ready)[w], FC * e)
                    for m in range(FC):
                        for c in range(C):
                            ins = product(ps_h[:, w, m, 0:CAP], [a[:, c, m * P:(m + 1) * P] for a in w13_2[p][w]], [a[:, c, :] for a in xeT2[p]],
                                          c == 0, c == C - 1)
                    ins.then_inc(h_ready, 1)

            def output(e, p):
                pe.wait_ge(w2_lo, e + 1)
                pe.wait_ge(gated_lo, e + 1)
                for n, (lo, hi, rows) in enumerate(tails):
                    pe.wait_ge(oe_ready, 2 * e)
                    for chunk in range(lo, hi):
                        for m in range(FC):
                            ins = product(ps_out[0:rows, n, (chunk - lo) * D:(chunk - lo + 1) * D],
                                          [a[:, m, chunk * P:chunk * P + rows] for a in gated2[p]], [a[:, m, :] for a in w2_2[p]],
                                          m == 0, m == FC - 1)
                    ins.then_inc(o_ready, 1)

            pe.wait_ge(z_out, 2 * NG)
            pe.wait_ge(router.index_ready, LAST + 1)
            pe.wait_ge(swT_ready, 1)
            turn(0, 0)
            hidden(0, 0)
            turn(1, 1)

            def expert(e, p):
                hidden(e, p)
                turn(e + 1, 1 - p)
                output(e - 1, 1 - p)

            expert(1, 1)
            expert(2, 0)
            with pe.Fori(1, E // 2 - 1) as i:
                for p in (1, 0):
                    expert(2 * i + 2 - p, p)
            hidden(E - 1, 1)
            output(E - 2, 0)
            output(E - 1, 1)


def xattn1(nc, keep, env):
    ctx_in, out = env["ctx_in"], env["out"]
    w2, swT, sel, join, b_cols, b_neg, bv_row, bo_g = (env[k] for k in ("l1_parts", "swT", "sel", "join", "b_cols", "b_neg", "bv_row", "bo1_g"))
    x_all, ident, neg_half, eps, tgates, rel_bias = (env[k] for k in ("x_all", "ident", "neg_half", "eps", "tgates", "rel_bias"))
    row_index, row_weight, scratch_oe = env["row_index"], env["row_weight"], env["scratch_oe"]
    B, T, C, D, K, DK = (env[k] for k in ("B", "T", "C", "D", "K", "DK"))
    H = env["H1"]
    S = T * P
    GR = P // 32
    M = H // 2
    PAD = P - 32
    WORK = 3

    with ExitStack() as phase:
        sb, ps, sem = make_tools(nc, phase, keep, "c")
        carve = carver(env["area"])
        ps_scores = ps("scores", [P, 2, T, S])
        ps_turn = ps("turn", [P, 2, T, S])
        ps_o = ps("o", [P, 2, S])
        ps_work = ps("work", [P, WORK, 512])

        cin = carve([P, T, D])
        index_now = sb("index_now", [P, T, K], U32)
        rows = carve([P, T, K, D])
        weight_now = sb("weight_now", [P, T, K])
        x2 = [carve([P, T, D]) for i in range(2)]
        xb = [carve([P, T, D]) for i in range(2)]
        stats = sb("stats", [P, 2, T, 6])
        moments = sb("moments", [P, 2, T, 2])
        var_eps = sb("var_eps", [P, 2, T])
        rstd = sb("rstd", [P, 2, T])
        xn = carve([P, T, D])
        x3 = [carve([P, T, D]) for i in range(2)]
        x3n = sb("x3n", [P, T, D])
        o_rows = x3n
        turned2 = {n: [sb(f"{n}T_{part}", [P, C, S], F32R) for part in ("hi", "lo")] for n in ("ctx", "x", "x3", "o")}
        qk2 = {n: [sb(f"{n}_{part}", [P, C, S], F32R) for part in ("hi", "lo")] for n in ("q", "k")}
        stacked = {n: [sb(f"{n}S{i}", [P, M, S], F32R) for i in range(2)] for n in ("q", "k")}
        v_sum = sb("v_sum", [P, T, D])
        v_pad = [sb(f"v_pad{i}", [P, T, PAD + H * P], F32R) for i in range(2)]
        s_neg = carve([P, 2, T, S])
        max_neg = sb("max_neg", [P, 2, T])
        probs = carve([P, 2, T, S])
        rsum = [sb(f"rsum{i}", [P, H, T]) for i in range(2)]
        rinv = sb("rinv", [P, H, T])
        pT2 = [sb(f"pT_{part}", [P, 2, T, S], F32R) for part in ("hi", "lo")]
        o_parts = sb("o_parts", [P, H // GR, S])

        USES = (("ctx", True, 0), ("o_join", False, 2), ("k", True, 2), ("o", False, 4), ("x", True, 4), ("y", False, 6),
                ("k0", True, 6), ("q", True, 7), ("k1", True, 8), ("q0", True, 9), ("q1", True, 10), ("v", True, 11),
                ("x3", False, 11), ("k2", True, 12), ("ff", False, 13), ("k3", True, 14), ("q2", True, 15), ("q3", True, 15))
        BANK = {u[0]: n % WORK for n, u in enumerate(USES)}

        names = ("v_zero", "own_front", "own_late", "own_combine", "f_moments", "f_rstd", "l_moments", "l_rstd", "index_copied",
                 "weight_copied", "summed", "x2_ready", "xb_ready", "xn_ready", "scores_ready", "biased", "probs_ready", "turned",
                 "pT_hi", "pT_lo", "pv_ready", "o_parts_out", "rinv_ready", "v_summed", "v_hi", "v_lo", "own_front_rstd",
                 "own_late_rstd", "x3_ready", "x3n_ready", "fin_ready")
        (v_zero, own_front, own_late, own_combine, f_moments, f_rstd, l_moments, l_rstd, index_copied, weight_copied, summed,
         x2_ready, xb_ready, xn_ready, scores_ready, biased, probs_ready, turned, pT_hi, pT_lo, pv_ready, o_parts_out, rinv_ready,
         v_summed, v_hi, v_lo, own_front_rstd, own_late_rstd, x3_ready, x3n_ready, fin_ready) = [sem(n) for n in names]
        ready = {u[0]: sem(f"{u[0]}_in_bank") for u in USES if len(u[0]) != 2 or u[0][0] not in "qk"}
        stack_in_bank = sem("stack_in_bank")
        STACKS = [u[0] for u in USES if u[0] not in ready]
        hi_out = {n: sem(f"{n}_hi_out") for n in ("ctx", "k", "o", "x3", "x", "q")}
        bank_free = [sem(f"bank_free{i}") for i in range(WORK)]
        ctx_loaded = sem("ctx_loaded")
        gathered = sem("gathered")
        stored = [sem(f"stored{i}") for i in range(2)]

        c_rows = ctx_in.rearrange("b (t p) d -> b p t d", p=P)
        out_rows = out.rearrange("b (t p) d -> b p t d", p=P)

        def slots(eng, slot):
            slot(0, 0, True, False)
            with eng.Fori(0, B // 2 - 1) as i:
                slot(2 * i + 1, 1, True, True)
                slot(2 * i + 2, 0, True, True)
            slot(B - 1, 1, False, True)

        def uses_at(h, more, behind):
            return [(n, ahead) for n, ahead, at in USES if at == h and (more if ahead else behind)]

        FIRST = [n for n, ahead, _ in USES if ahead and n[0] not in "xq"] + [n for n, ahead, _ in USES if ahead and n[0] in "xq"]
        FIRST_STACKS = [n for n in FIRST if n in STACKS]

        def empty_banks(take, b, p, h, more, behind):
            if h >= 2:
                for name, ahead in uses_at(h - 2, more, behind):
                    take(name, b + 1 if ahead else b - 1, 1 - p)
            elif behind:
                for name, _ in uses_at(H + h - 2, True, False):
                    take(name, b, p)

        FRONT_AT = (0, 1, 1, 3)
        LATE_AT = (8, 9, 10)
        V_HIGH_AT = 14

        def heads(b, h):
            n = H * b + h + 1
            return max(n, 0) if isinstance(n, int) else n

        block = phase.enter_context(nc.Block())

        @block.sync
        def _(sp):
            def load(b):
                sp.dma_start(cin[:], c_rows[bass.ds(b, 1)].rearrange("b p t d -> p (b t) d")).then_inc(ctx_loaded, 16)

            def store(b, p):
                sp.wait_ge(fin_ready, T * (b + 1))
                sp.dma_start(out_rows[bass.ds(b, 1)].rearrange("b p t d -> p (b t) d"), x3[p][:]).then_inc(stored[p], 16)

            load(0)
            sp.wait_ge(ready["ctx"], 1)
            load(1)
            with sp.Fori(1, B // 2) as i:
                for p in range(2):
                    b = 2 * i + p
                    sp.wait_ge(ready["ctx"], b)
                    load(b)
                    store(b - 2, p)
            store(B - 2, 0)
            store(B - 1, 1)
            for p in range(2):
                sp.wait_ge(stored[p], 16 * B // 2)

        @block.gpsimd
        def _(pool):
            oc = Ordered(pool, own_combine, 2)

            def gather(b):
                pool.wait_ge(gathered, 16 * T * K * b)
                pool.wait_ge(summed, b)
                nc.gpsimd.tensor_copy(index_now[:], row_index[:, bass.ds(T * b, T), :]).then_inc(index_copied, 1)
                pool.wait_ge(index_copied, b + 1)
                pool.sem_inc(env["router"].seen, 1)
                for t in range(T):
                    for k in range(K):
                        nc.gpsimd.indirect_dma_start(
                            out=rows[:, t, k, :], out_offset=None, in_=scratch_oe,
                            in_offset=bass.IndirectOffsetOnAxis(ap=index_now[:, t, k:k + 1], axis=0)).then_inc(gathered, 16)

            def combine(b, p):
                oc.start(b)
                nc.gpsimd.tensor_copy(weight_now[:], row_weight[:, bass.ds(T * b, T), :]).then_inc(weight_copied, 1)
                pool.wait_ge(weight_copied, b + 1)
                pool.wait_ge(gathered, 16 * T * K * (b + 1))
                oc.done(nc.gpsimd.tensor_tensor(rows[:], rows[:], weight_now[:].unsqueeze(3).to_broadcast([P, T, K, D]), ALU.mult))
                oc.wait()
                oc.done(nc.gpsimd.tensor_tensor(rows[:, :, 0:2, :], rows[:, :, 0:2, :], rows[:, :, 2:4, :], ALU.add))
                oc.wait()
                pool.wait_ge(xn_ready, max(T * (b - 1), 0) if isinstance(b, int) else T * (b - 1))
                pool.wait_ge(xb_ready, max(b - 1, 0) if isinstance(b, int) else b - 1)
                nc.gpsimd.tensor_tensor(x2[p][:], rows[:, :, 0, :], rows[:, :, 1, :], ALU.add).then_inc(summed, 1)

            def rstds(b, late):
                mine = (own_front_rstd, own_late_rstd)[late]
                pool.wait_ge((f_moments, l_moments)[late], T * (b + 1))
                nc.gpsimd.tensor_tensor(var_eps[:, late, :], moments[:, late, :, 1], eps[:, 0:T], ALU.add).then_inc(mine, 1)
                pool.wait_ge(mine, b + 1)
                nc.gpsimd.tensor_tensor(rstd[:, late, :], var_eps[:, late, :], neg_half[:, 0:T], ALU.pow).then_inc((f_rstd, l_rstd)[late], 1)

            def with_bias(b, p):
                pool.wait_ge(x2_ready, T * (b + 1))
                nc.gpsimd.tensor_tensor(xb[p][:], x2[p][:], bo_g[:].unsqueeze(1).to_broadcast([P, T, D]), ALU.add).then_inc(xb_ready, 1)

            def v_low(b, p):
                pool.wait_ge(v_hi, T * (b + 1))
                for t in range(T):
                    at = v_pad[p][:, t, PAD:].rearrange("p (h m) -> p h m", m=P)
                    nc.gpsimd.tensor_tensor(at[:, :, DK:2 * DK], v_sum[:, t, :].rearrange("p (h d) -> p h d", d=DK), at[:, :, 0:DK].bitcast(F32),
                                            ALU.subtract).then_inc(v_lo, 1)

            def slot(b, p, more, behind, combines, gathers):
                if more:
                    rstds(b + 1, 0)
                if combines:
                    combine(b + 2, p)
                if gathers:
                    gather(b + 3)
                if behind:
                    pool.wait_ge(x3_ready, T * b)
                if more:
                    with_bias(b + 1, 1 - p)
                if behind:
                    rstds(b - 1, 1)
                if more:
                    v_low(b + 1, 1 - p)

            gather(0)
            combine(0, 0)
            rstds(0, 0)
            gather(1)
            with_bias(0, 0)
            v_low(0, 0)
            combine(1, 1)
            gather(2)
            slot(0, 0, True, False, True, True)
            with pool.Fori(0, B // 2 - 2) as i:
                slot(2 * i + 1, 1, True, True, True, True)
                slot(2 * i + 2, 0, True, True, True, True)
            slot(B - 3, 1, True, True, True, False)
            slot(B - 2, 0, True, True, False, False)
            slot(B - 1, 1, False, True, False, False)
            rstds(B - 1, 1)

        @block.vector
        def _(dve):
            of = Ordered(dve, own_front, T)
            ol = Ordered(dve, own_late, T)

            def front(b, p, step=None):
                if step in (None, 0):
                    dve.wait_ge(summed, b + 1)
                    of.start(b)
                    for t in range(T):
                        nc.vector.scalar_tensor_tensor(out=x2[p][:, t, :], in0=x2[p][:, t, :], scalar=tgates[:, 2:3],
                                                       in1=x_all[:, bass.ds(T * b + t, 1), :].rearrange("p t d -> p (t d)"),
                                                       op0=ALU.mult, op1=ALU.add).then_inc(x2_ready, 1)
                if step in (None, 1):
                    dve.wait_ge(x2_ready, T * (b + 1))
                    for t in range(T):
                        of.done(nc.vector.bn_stats(stats[:, 0, t, :], x2[p][:, t, :]))
                if step in (None, 2):
                    of.wait()
                    dve.sem_inc(env["router"].seen, 1)
                    for t in range(T):
                        nc.vector.bn_aggr(moments[:, 0, t, :], stats[:, 0, t, :]).then_inc(f_moments, 1)
                if step in (None, 3):
                    dve.wait_ge(f_rstd, b + 1)
                    dve.wait_ge(ready["x"], b)
                    for t in range(T):
                        nc.vector.tensor_scalar(xn[:, t, :], x2[p][:, t, :], moments[:, 0, t, 0:1], rstd[:, 0, t:t + 1],
                                                ALU.subtract, ALU.mult).then_inc(xn_ready, 1)

            def late(b, p, step=None):
                if step in (None, 0):
                    ol.start(b)
                    dve.wait_ge(x3_ready, T * (b + 1))
                    for t in range(T):
                        ol.done(nc.vector.bn_stats(stats[:, 1, t, :], x3[p][:, t, :]))
                if step in (None, 1):
                    ol.wait()
                    dve.sem_inc(env["router"].seen, 1)
                    for t in range(T):
                        nc.vector.bn_aggr(moments[:, 1, t, :], stats[:, 1, t, :]).then_inc(l_moments, 1)
                if step in (None, 2):
                    dve.wait_ge(l_rstd, b + 1)
                    dve.wait_ge(ready["x3"], b)
                    for t in range(T):
                        nc.vector.tensor_scalar(x3n[:, t, :], x3[p][:, t, :], moments[:, 1, t, 0:1], rstd[:, 1, t:t + 1],
                                                ALU.subtract, ALU.mult).then_inc(x3n_ready, 1)

            def take(name, b, p):
                if name not in STACKS:
                    bank = ps_work[:, BANK[name], :]
                    free = bank_free[BANK[name]]
                    if name in ("ctx", "x3", "x", "o"):
                        dve.wait_ge(hi_out[name], b + 1)
                        hi, lo = turned2[name]
                        nc.vector.tensor_tensor(lo[:].rearrange("p c s -> p (c s)"), bank, hi[:].bitcast(F32).rearrange("p c s -> p (c s)"),
                                                ALU.subtract).then_inc(free, 1)
                    elif name in ("q", "k"):
                        dve.wait_ge(hi_out[name], C * (b + 1))
                        hi, lo = qk2[name]
                        bias_col = (b_neg, b_cols[:, 1, :])[name == "k"]
                        for c in range(C):
                            ins = nc.vector.scalar_tensor_tensor(out=lo[:, c, :], in0=bank[:, c * S:(c + 1) * S], scalar=bias_col[:, c:c + 1],
                                                                 in1=hi[:, c, :].bitcast(F32), op0=ALU.add, op1=ALU.subtract)
                        ins.then_inc(free, 1)
                    elif name == "v":
                        dve.wait_ge(ready["v"], b + 1)
                        dve.wait_ge(v_lo, T * b)
                        nc.vector.tensor_tensor(v_sum[:], bank.rearrange("p (t d) -> p t d", t=T),
                                                bv_row[:].unsqueeze(1).to_broadcast([P, T, D]), ALU.add).then_inc(v_summed, 1)
                        dve.wait_ge(v_summed, b + 1)
                        dve.sem_inc(free, 1)
                    elif name == "o_join":
                        dve.wait_ge(ready["o_join"], b + 1)
                        dve.wait_ge(rinv_ready, b + 1)
                        dve.wait_ge(ready["o"], b)
                        nc.vector.tensor_tensor(o_rows[:].rearrange("p t (h d) -> p t h d", d=DK), bank.rearrange("p (t h d) -> p t h d", t=T, d=DK),
                                                rinv[:].rearrange("p h t -> p t h").unsqueeze(3).to_broadcast([P, T, H, DK]),
                                                ALU.mult).then_inc(free, 1)
                    elif name == "y":
                        dve.wait_ge(ready["y"], b + 1)
                        dve.wait_ge(xb_ready, b + 1)
                        dve.wait_ge(stored[p], 8 * (b - p))
                        for t in range(T):
                            ins = nc.vector.scalar_tensor_tensor(out=x3[p][:, t, :], in0=bank[:, t * D:(t + 1) * D], scalar=tgates[:, 1:2],
                                                                 in1=xb[p][:, t, :], op0=ALU.mult, op1=ALU.add)
                            ins.then_inc(x3_ready, 1)
                        dve.wait_ge(x3_ready, T * (b + 1))
                        dve.sem_inc(free, 1)
                    else:
                        dve.wait_ge(ready["ff"], b + 1)
                        for t in range(T):
                            nc.vector.scalar_tensor_tensor(out=x3[p][:, t, :], in0=bank[:, t * D:(t + 1) * D], scalar=tgates[:, 3:4],
                                                           in1=x3[p][:, t, :], op0=ALU.mult, op1=ALU.add).then_inc(fin_ready, 1)
                        dve.wait_ge(fin_ready, T * (b + 1))
                        dve.sem_inc(free, 1)

            def bias(b, h):
                dve.wait_ge(probs_ready, T * heads(b, h - 2))
                dve.wait_ge(scores_ready, heads(b, h))
                dve.sem_inc(env["router"].seen, 1)
                for t in range(T):
                    nc.vector.tensor_tensor_reduce(s_neg[:, h % 2, t, :], ps_scores[:, h % 2, t, :], rel_bias[:, h, (1 - t) * P:(1 - t) * P + S],
                                                   1.0, 3.0e38, ALU.add, ALU.min, max_neg[:, h % 2, t:t + 1]).then_inc(biased, 1)

            def probs_low(b, h):
                dve.wait_ge(pT_hi, heads(b, h))
                nc.vector.tensor_tensor(pT2[1][:, h % 2], ps_turn[:, h % 2], pT2[0][:, h % 2].bitcast(F32), ALU.subtract).then_inc(pT_lo, 1)

            def row_sums(b, p):
                dve.wait_ge(probs_ready, T * heads(b, H - 1))
                nc.vector.reciprocal(rinv[:], rsum[p][:]).then_inc(rinv_ready, 1)

            def slot(b, p, more, behind):
                for h in range(H):
                    if h >= 2:
                        probs_low(b, h - 2)
                    elif behind:
                        probs_low(b - 1, H + h - 2)
                    if h < H - 1:
                        bias(b, h + 1)
                    elif more:
                        bias(b + 1, 0)
                    if h == 1 and behind:
                        row_sums(b - 1, 1 - p)
                    empty_banks(take, b, p, h, more, behind)
                    for n in range(len(FRONT_AT)):
                        if more and h == FRONT_AT[n]:
                            front(b + 1, 1 - p, n)
                    if behind and h in LATE_AT:
                        late(b - 1, 1 - p, LATE_AT.index(h))

            for i in range(2):
                nc.vector.memset(v_pad[i][:].bitcast(F32), 0.0).then_inc(v_zero, 1)
            for name in FIRST:
                if name == "x":
                    front(0, 0)
                take(name, 0, 0)
            bias(0, 0)
            slots(dve, slot)
            probs_low(B - 1, H - 2)
            probs_low(B - 1, H - 1)
            row_sums(B - 1, 1)
            take("o_join", B - 1, 1)
            take("o", B - 1, 1)
            take("y", B - 1, 1)
            late(B - 1, 1)
            take("x3", B - 1, 1)
            take("ff", B - 1, 1)

        @block.scalar
        def _(act):
            def take(name, b, p):
                bank = ps_work[:, BANK[name], :]
                if name in ("ctx", "x3", "x", "o"):
                    act.wait_ge(ready[name], b + 1)
                    nc.scalar.copy(turned2[name][0][:].rearrange("p c s -> p (c s)"), bank).then_inc(hi_out[name], 1)
                elif name in ("q", "k"):
                    act.wait_ge(ready[name], b + 1)
                    bias_col = (b_neg, b_cols[:, 1, :])[name == "k"]
                    for c in range(C):
                        nc.scalar.activation(qk2[name][0][:, c, :], bank[:, c * S:(c + 1) * S], ACT.Identity, bias=bias_col[:, c:c + 1],
                                             scale=1.0).then_inc(hi_out[name], 1)
                elif name in STACKS:
                    order = FIRST_STACKS if isinstance(b, int) and b == 0 else STACKS
                    act.wait_ge(stack_in_bank, len(STACKS) * b + order.index(name) + 1)
                    m = 2 * int(name[1])
                    nc.scalar.copy(stacked[name[0]][p][:, m:m + 2, :].rearrange("p m s -> p (m s)"), bank).then_inc(bank_free[BANK[name]], 1)

            def v_high(b, p):
                if isinstance(b, int) and b == 0:
                    act.wait_ge(v_zero, 2)
                act.wait_ge(v_summed, b + 1)
                for t in range(T):
                    nc.scalar.copy(v_pad[p][:, t, PAD:].rearrange("p (h m) -> p h m", m=P)[:, :, 0:DK],
                                   v_sum[:, t, :].rearrange("p (h d) -> p h d", d=DK)).then_inc(v_hi, 1)

            def slot(b, p, more, behind):
                if behind:
                    act.wait_ge(rinv_ready, b - 1)
                for h in range(H):
                    if h == 2 and behind:
                        parts_out(b - 1, 1)
                    if h == H // 2 + 2:
                        parts_out(b, 0)
                    act.wait_ge(biased, T * heads(b, h))
                    act.wait_ge(turned, heads(b, h - 2))
                    for t in range(T):
                        nc.scalar.activation(probs[:, h % 2, t, :], s_neg[:, h % 2, t, :], ACT.Exp, bias=max_neg[:, h % 2, t:t + 1],
                                             scale=-1.0, accum_out=rsum[p][:, h, t:t + 1]).then_inc(probs_ready, 1)
                    empty_banks(take, b, p, h, more, behind)
                    if h:
                        probs_high(b, h - 1)
                    elif behind:
                        probs_high(b - 1, H - 1)
                    if h == V_HIGH_AT and more:
                        v_high(b + 1, 1 - p)

            def probs_high(b, h):
                act.wait_ge(turned, heads(b, h))
                act.wait_ge(pv_ready, heads(b, h - 2))
                nc.scalar.copy(pT2[0][:, h % 2], ps_turn[:, h % 2]).then_inc(pT_hi, 1)

            def parts_out(b, half):
                act.wait_ge(pv_ready, heads(b, H // 2 * (half + 1) - 1))
                act.wait_ge(ready["o_join"], b)
                nc.scalar.copy(o_parts[:, 2 * half:2 * half + 2, :], ps_o[:]).then_inc(o_parts_out, 1)

            for name in FIRST:
                if name == "x":
                    v_high(0, 0)
                take(name, 0, 0)
            slots(act, slot)
            probs_high(B - 1, H - 1)
            parts_out(B - 1, 1)
            take("o", B - 1, 1)
            take("x3", B - 1, 1)

        @block.tensor
        def _(pe):
            ahead_uses = [sum(1 for n, a, _ in USES if a and BANK[n] == k) for k in range(WORK)]
            behind_uses = [sum(1 for n, a, _ in USES if not a and BANK[n] == k) for k in range(WORK)]
            before, used = [0] * WORK, [0] * WORK
            place = {}

            def start_slot(b):
                for k in range(WORK):
                    before[k] = ahead_uses[k] if isinstance(b, int) and b == 0 else \
                        (ahead_uses[k] + behind_uses[k]) * b + ahead_uses[k] - behind_uses[k]
                    used[k] = 0

            def fill(name):
                k = BANK[name]
                pe.wait_ge(bank_free[k], before[k] + used[k])
                place[name] = used[k]
                used[k] += 1
                return ps_work[:, k, :]

            def emptied(name):
                pe.wait_ge(bank_free[BANK[name]], before[BANK[name]] + place[name] + 1)

            def product(out, a, b, first=True, last=True):
                nc.tensor.matmul(out, a[0], b[0], start=first, stop=False)
                nc.tensor.matmul(out, a[0], b[1], start=False, stop=False)
                return nc.tensor.matmul(out, a[1], b[0], start=False, stop=last)

            def turn(bank, src):
                for c in range(C):
                    for t in range(T):
                        ins = nc.tensor.transpose(bank[:, c * S + t * P:c * S + (t + 1) * P], src[:, t, c * P:(c + 1) * P], ident[:])
                return ins

            def project(bank, srcT, w):
                for t in range(T):
                    for c in range(C):
                        ins = product(bank[:, t * D:(t + 1) * D], [s[:, c, t * P:(t + 1) * P] for s in srcT], [s[:, c, :] for s in w],
                                      c == 0, c == C - 1)
                return ins

            def use(name, b, p):
                bank = fill(name)
                if name == "ctx":
                    pe.wait_ge(ctx_loaded, 16 * (b + 1))
                    ins = turn(bank, cin)
                elif name == "x":
                    pe.wait_ge(xn_ready, T * (b + 1))
                    ins = turn(bank, xn)
                elif name == "x3":
                    pe.wait_ge(x3n_ready, T * (b + 1))
                    ins = turn(bank, x3n)
                elif name == "o":
                    emptied("o_join")
                    ins = turn(bank, o_rows)
                elif name in ("q", "k"):
                    src = {"q": "x", "k": "ctx"}[name]
                    emptied(src)
                    for m in range(2):
                        for c in range(C):
                            ins = product(bank[:, m * S:(m + 1) * S], [w[:, c, m * P:(m + 1) * P] for w in w2["w" + name]],
                                          [s[:, c, :] for s in turned2[src]], c == 0, c == C - 1)
                elif name[0] in "qk":
                    emptied(name[0])
                    for k in range(2):
                        m = 2 * int(name[1]) + k
                        for part in range(2):
                            ins = nc.tensor.matmul(bank[:, k * S:(k + 1) * S], sel[name[0]][part][:, m % 4].rearrange("p h k i -> p (h k i)"),
                                                   qk2[name[0]][part][:, m // 4, :], start=(part == 0), stop=(part == 1))
                elif name == "v":
                    ins = project(bank, turned2["ctx"], w2["wv"])
                elif name == "o_join":
                    pe.wait_ge(o_parts_out, 2 * (b + 1))
                    for t in range(T):
                        for g in range(H // GR):
                            at = (t * (H // GR) + g) * GR * DK
                            ins = nc.tensor.matmul(bank[:, at:at + GR * DK], o_parts[:, g, t * P:(t + 1) * P], join[:].rearrange("p j d -> p (j d)"),
                                                   start=True, stop=True)
                elif name == "y":
                    emptied("o")
                    ins = project(bank, turned2["o"], w2["wo"])
                else:
                    emptied("x3")
                    for t in range(T):
                        for c in range(C):
                            for part in range(2):
                                ins = nc.tensor.matmul(bank[:, t * D:(t + 1) * D], turned2["x3"][part][:, c, t * P:(t + 1) * P], swT[:, c, :],
                                                       start=(c == 0 and part == 0), stop=(c == C - 1 and part == 1))
                ins.then_inc(stack_in_bank if name in STACKS else ready[name], 1)

            def scores(b, p, h):
                m, at = h // 2, slice(64 * (h % 2), 64 * (h % 2) + 64)
                pe.wait_ge(biased, T * heads(b, h - 2))
                for t in range(T):
                    ins = nc.tensor.matmul(ps_scores[:, h % 2, t, :], stacked["q"][p][at, m, t * P:(t + 1) * P], stacked["k"][p][at, m, :],
                                           start=True, stop=True)
                ins.then_inc(scores_ready, 1)

            def turn_probs(b, h):
                pe.wait_ge(probs_ready, T * heads(b, h))
                pe.wait_ge(pT_lo, heads(b, h - 2))
                for tk in range(T):
                    for tq in range(T):
                        ins = nc.tensor.transpose(ps_turn[:, h % 2, tk, tq * P:(tq + 1) * P], probs[:, h % 2, tq, tk * P:(tk + 1) * P], ident[:])
                ins.then_inc(turned, 1)

            def values(b, p, h):
                g, j = divmod(h, GR)
                pe.wait_ge(pT_lo, heads(b, h))
                if h % (H // 2) == 0:
                    pe.wait_ge(o_parts_out, 2 * b + h // (H // 2))
                if h == 0:
                    pe.wait_ge(v_lo, T * (b + 1))
                at = PAD + P * h - 32 * j
                for tk in range(T):
                    for part in range(2):
                        ins = nc.tensor.matmul(ps_o[:, g % 2, :], v_pad[p][:, tk, at:at + P], pT2[part][:, h % 2, tk, :],
                                               start=(j == 0 and tk == 0 and part == 0), stop=(j == GR - 1 and tk == T - 1 and part == 1))
                ins.then_inc(pv_ready, 1)

            def stacks_ready():
                for k in range(WORK):
                    pe.wait_ge(bank_free[k], before[k] + used[k])

            def slot(b, p, more, behind):
                start_slot(b)
                for h in range(H):
                    if h == 2:
                        for k in range(WORK):
                            pe.wait_ge(bank_free[k], before[k])
                    if h + 2 < H:
                        scores(b, p, h + 2)
                    elif more:
                        if h + 2 == H:
                            emptied("q0")
                            emptied("k0")
                        scores(b + 1, 1 - p, h + 2 - H)
                    if h >= 2:
                        values(b, p, h - 2)
                    elif behind:
                        values(b - 1, 1 - p, H + h - 2)
                    turn_probs(b, h)
                    for name, ahead in uses_at(h, more, behind):
                        use(name, b + 1 if ahead else b - 1, 1 - p)

            for name in FIRST:
                use(name, 0, 0)
            stacks_ready()
            scores(0, 0, 0)
            scores(0, 0, 1)
            slots(pe, slot)
            values(B - 1, 1, H - 2)
            values(B - 1, 1, H - 1)
            start_slot(B)
            for k in range(WORK):
                before[k] -= ahead_uses[k]
            for name, ahead, _ in USES:
                if not ahead:
                    use(name, B - 1, 1)


_INS = ["x", "ctx_1024", "g_xattn", "g_ffn", "L0_xattn_ln_l_w", "L0_xattn_ln_l_b", "L0_xattn_ln_c_w", "L0_xattn_ln_c_b",
        "L0_xattn_Wq", "L0_xattn_Wkv", "L0_xattn_Wo", "L0_xattn_bo", "L0_ffn_wg", "L0_ffn_w1", "L0_ffn_w2", "L0_ffn_w3",
        "L0_ffn_sw1", "L0_ffn_sw2", "L0_ffn_sw3", "L1_xattn_Wq", "L1_xattn_bq", "L1_xattn_Wk", "L1_xattn_bk",
        "L1_xattn_Wv", "L1_xattn_bv", "L1_xattn_Wo", "L1_xattn_bo", "L1_xattn_rel", "L1_ffn_weight"]


def kernel(**inputs):
    import concourse.bacc as bacc
    from concourse.bass_utils import run_bass_kernel_spmd

    nc = bacc.Bacc("TRN2", target_bir_lowering=False, num_devices=1)
    arrays, args = {}, []
    for name in _INS:
        a = np.ascontiguousarray(inputs[name])
        arrays[f"in_{name}"] = a
        args.append(nc.dram_tensor(f"in_{name}", a.shape, mybir.dt.from_np(a.dtype), kind="ExternalInput").ap())
    shape = inputs["x"].shape
    args.append(nc.dram_tensor("out", shape, F32, kind="ExternalOutput").ap())
    flamingo_kernel(nc, *args)
    r = run_bass_kernel_spmd(nc, [arrays], core_ids=[0])
    return r.results[0]["out"]
```
